# Optimizing a Trainium2 kernel written in Bass

```python
import numpy as np
import jax
import jax.numpy as jnp

def _softmax(x, axis=-1):
    return jax.nn.softmax(x, axis=axis)

def _gelu(x):
    return jax.nn.gelu(x, approximate=True)

def _silu(x):
    return jax.nn.silu(x)

def _sigmoid(x):
    return jax.nn.sigmoid(x)

def _layernorm(x, axis=-1, eps=1e-05):
    m = jnp.mean(x, axis=axis, keepdims=True)
    v = jnp.var(x, axis=axis, keepdims=True)
    return (x - m) / jnp.sqrt(v + eps)

def _scatter_add(tgt, idx, src, axis=0):
    return tgt.at[idx].add(src)

def _segment_sum(src, seg, n):
    return jax.ops.segment_sum(src, seg, n)
kernel_name = 'mk_gnn_preln_d4_gnn_r32_41b06c'

def setup_inputs(seed: int=0):
    np.random.seed(seed)
    _w = jnp.asarray

    def _rec_inputs():
        import jax
        import jax.numpy as jnp
        _gk = jax.random.key(seed)
        x = -0.0001006 + 1 * jax.random.normal(jax.random.fold_in(_gk, 1), (3125, 96), jnp.float32)
        _s = jax.random.randint(jax.random.fold_in(_gk, 2), (50000,), 0, 3125, jnp.int32)
        _d = jax.random.randint(jax.random.fold_in(_gk, 3), (50000,), 0, 3125, jnp.int32)
        _loop = jnp.arange(3125, dtype=jnp.int32)
        src = jnp.concatenate([_s, _d, _loop])
        dst = jnp.concatenate([_d, _s, _loop])
        _o = jnp.argsort(dst, stable=True)
        src = src[_o]
        dst = dst[_o]
        edge_attr_64 = 0.000189758 + 1.00013 * jax.random.normal(jax.random.fold_in(_gk, 11), (103125, 64), jnp.float32)
        edge_weight = jax.random.uniform(jax.random.fold_in(_gk, 13), (103125,), jnp.float32, 0.0, 0.999998)
        return (x, src, dst, edge_attr_64, edge_weight)
    x, src, dst, edge_attr_64, edge_weight = _rec_inputs()

    def _L0_gnn_setup():
        import jax, jax.numpy as jnp
        import numpy as np
        K = 10
        ALPHA = 0.1
        BETA = 0.9
        N_NODES = 50000
        N_EDGES = 25000
        D_FEAT = 96
        key = jax.random.key(seed)
        k1, k2, k3 = jax.random.split(key, 3)
        x = jax.random.normal(k1, (N_NODES, D_FEAT), dtype=jnp.float32)
        row = jax.random.randint(k2, (N_EDGES,), 0, N_NODES, dtype=jnp.int64)
        col = jax.random.randint(k3, (N_EDGES,), 0, N_NODES, dtype=jnp.int64)
        edge_index = jnp.stack([row, col], axis=0)
        return {'x': x, 'edge_index': edge_index}
    _L0_gnn_all = _L0_gnn_setup()
    _L0_gnn_in = {k: v for k, v in _L0_gnn_all.items() if k in ()}
    del _L0_gnn_all

    def _L1_gnn_setup():
        import jax, jax.numpy as jnp
        import numpy as np
        N, E = (50000, 25000)
        NODE_DIM, EDGE_DIM = (96, 64)
        IN_DIM = 2 * NODE_DIM + EDGE_DIM
        key = jax.random.key(seed)
        k = jax.random.split(key, 7)
        h = jax.random.normal(k[0], (N, NODE_DIM), dtype=jnp.float32)
        edge_index = jax.random.randint(k[1], (2, E), 0, N, dtype=jnp.int64)
        edge_attr = jax.random.normal(k[2], (E, EDGE_DIM), dtype=jnp.float32)
        s = 1.0 / np.sqrt(IN_DIM)
        W_e = jax.random.uniform(k[3], (IN_DIM, NODE_DIM), jnp.float32, -s, s)
        b_e = jax.random.uniform(k[4], (NODE_DIM,), jnp.float32, -s, s)
        W_n = jax.random.uniform(k[5], (IN_DIM, NODE_DIM), jnp.float32, -s, s)
        b_n = jax.random.uniform(k[6], (NODE_DIM,), jnp.float32, -s, s)
        return {'h': h, 'edge_index': edge_index, 'edge_attr': edge_attr, 'W_e': W_e, 'b_e': b_e, 'W_n': W_n, 'b_n': b_n}
    _L1_gnn_all = _L1_gnn_setup()
    _L1_gnn_in = {k: v for k, v in _L1_gnn_all.items() if k in ('W_e', 'b_e', 'W_n', 'b_n')}
    del _L1_gnn_all

    def _L2_gnn_setup():
        import jax, jax.numpy as jnp
        import numpy as np
        EPS = 1e-05

        def _gcn_conv(x, edge_index, W, b):
            h = x @ W
            src, dst = (edge_index[0], edge_index[1])
            msgs = h[src]
            agg = jax.ops.segment_sum(msgs, dst, num_segments=x.shape[0])
            return agg + b

        def _graph_norm(x, weight, bias, mean_scale):
            mean = jnp.mean(x, axis=0, keepdims=True)
            xc = x - mean_scale * mean
            var = jnp.mean(xc * xc, axis=0, keepdims=True)
            return xc * jax.lax.rsqrt(var + EPS) * weight + bias
        key = jax.random.key(seed)
        ks = jax.random.split(key, 8)
        N, E, D = (50000, 25000, 96)
        x = jax.random.normal(ks[0], (N, D), dtype=jnp.float32)
        edge_index = jax.random.randint(ks[1], (2, E), 0, N, dtype=jnp.int32)
        s = 1.0 / np.sqrt(D)
        W1 = jax.random.normal(ks[2], (D, D), dtype=jnp.float32) * s
        b1 = jnp.zeros((D,), dtype=jnp.float32)
        W2 = jax.random.normal(ks[3], (D, D), dtype=jnp.float32) * s
        b2 = jnp.zeros((D,), dtype=jnp.float32)
        gn1_w = jnp.ones((D,), dtype=jnp.float32)
        gn1_b = jnp.zeros((D,), dtype=jnp.float32)
        gn1_a = jnp.ones((D,), dtype=jnp.float32)
        gn2_w = jnp.ones((D,), dtype=jnp.float32)
        gn2_b = jnp.zeros((D,), dtype=jnp.float32)
        gn2_a = jnp.ones((D,), dtype=jnp.float32)
        return {'x': x, 'edge_index': edge_index, 'W1': W1, 'b1': b1, 'W2': W2, 'b2': b2, 'gn1_w': gn1_w, 'gn1_b': gn1_b, 'gn1_a': gn1_a, 'gn2_w': gn2_w, 'gn2_b': gn2_b, 'gn2_a': gn2_a}
    _L2_gnn_all = _L2_gnn_setup()
    _L2_gnn_in = {k: v for k, v in _L2_gnn_all.items() if k in ('W1', 'b1', 'W2', 'b2', 'gn1_w', 'gn1_b', 'gn1_a', 'gn2_w', 'gn2_b', 'gn2_a')}
    del _L2_gnn_all

    def _L3_gnn_setup():
        import jax, jax.numpy as jnp
        import numpy as np
        N_NODES = 50000
        N_EDGES = 25000
        FEAT = 96

        def gcn_conv(x, edge_index, edge_weight, W, b, n_nodes):
            row, col = (edge_index[0], edge_index[1])
            loop = jnp.arange(n_nodes, dtype=edge_index.dtype)
            row = jnp.concatenate([row, loop])
            col = jnp.concatenate([col, loop])
            ew = jnp.concatenate([edge_weight, jnp.ones((n_nodes,), x.dtype)])
            deg = jax.ops.segment_sum(ew, col, num_segments=n_nodes)
            dinv = jnp.where(deg > 0, jax.lax.rsqrt(deg), jnp.zeros_like(deg))
            norm = dinv[row] * ew * dinv[col]
            h = x @ W
            msg = h[row] * norm[:, None]
            out = jax.ops.segment_sum(msg, col, num_segments=n_nodes)
            return out + b
        key = jax.random.key(seed)
        k = jax.random.split(key, 6)
        x = jax.random.normal(k[0], (N_NODES, FEAT), dtype=jnp.float32)
        edge_index = jax.random.randint(k[1], (2, N_EDGES), 0, N_NODES, dtype=jnp.int64)
        edge_weight = jax.random.uniform(k[2], (N_EDGES,), dtype=jnp.float32)
        s = 1.0 / np.sqrt(FEAT)
        W1 = jax.random.normal(k[3], (FEAT, FEAT), dtype=jnp.float32) * s
        W2 = jax.random.normal(k[4], (FEAT, FEAT), dtype=jnp.float32) * s
        b1 = jnp.zeros((FEAT,), dtype=jnp.float32)
        b2 = jnp.zeros((FEAT,), dtype=jnp.float32)
        return {'x': x, 'edge_index': edge_index, 'edge_weight': edge_weight, 'W1': W1, 'b1': b1, 'W2': W2, 'b2': b2}
    _L3_gnn_all = _L3_gnn_setup()
    _L3_gnn_in = {k: v for k, v in _L3_gnn_all.items() if k in ('W1', 'b1', 'W2', 'b2')}
    del _L3_gnn_all
    return {'x': x, 'src': src, 'dst': dst, 'edge_attr_64': edge_attr_64, 'edge_weight': edge_weight, 'L1_gnn_W_e': _L1_gnn_in['W_e'], 'L1_gnn_b_e': _L1_gnn_in['b_e'], 'L1_gnn_W_n': _L1_gnn_in['W_n'], 'L1_gnn_b_n': _L1_gnn_in['b_n'], 'L2_gnn_W1': _L2_gnn_in['W1'], 'L2_gnn_b1': _L2_gnn_in['b1'], 'L2_gnn_W2': _L2_gnn_in['W2'], 'L2_gnn_b2': _L2_gnn_in['b2'], 'L2_gnn_gn1_w': _L2_gnn_in['gn1_w'], 'L2_gnn_gn1_b': _L2_gnn_in['gn1_b'], 'L2_gnn_gn1_a': _L2_gnn_in['gn1_a'], 'L2_gnn_gn2_w': _L2_gnn_in['gn2_w'], 'L2_gnn_gn2_b': _L2_gnn_in['gn2_b'], 'L2_gnn_gn2_a': _L2_gnn_in['gn2_a'], 'L3_gnn_W1': _L3_gnn_in['W1'], 'L3_gnn_b1': _L3_gnn_in['b1'], 'L3_gnn_W2': _L3_gnn_in['W2'], 'L3_gnn_b2': _L3_gnn_in['b2']}

def reference(x, src, dst, edge_attr_64, edge_weight, L1_gnn_W_e, L1_gnn_b_e, L1_gnn_W_n, L1_gnn_b_n, L2_gnn_W1, L2_gnn_b1, L2_gnn_W2, L2_gnn_b2, L2_gnn_gn1_w, L2_gnn_gn1_b, L2_gnn_gn1_a, L2_gnn_gn2_w, L2_gnn_gn2_b, L2_gnn_gn2_a, L3_gnn_W1, L3_gnn_b1, L3_gnn_W2, L3_gnn_b2):
    import jax
    import jax.numpy as jnp

    def _L0_gnn_ref(x, edge_index):
        import jax, jax.numpy as jnp
        import numpy as np
        K = 10
        ALPHA = 0.1
        BETA = 0.9
        N_NODES = 50000
        N_EDGES = 25000
        D_FEAT = 96
        n = x.shape[0]
        row, col = (edge_index[0], edge_index[1])
        ones = jnp.ones((edge_index.shape[1],), dtype=x.dtype)
        deg_row = jnp.maximum(jax.ops.segment_sum(ones, row, num_segments=n), 1.0)
        deg_col = jnp.maximum(jax.ops.segment_sum(ones, col, num_segments=n), 1.0)
        w = jax.lax.rsqrt(deg_row[row] * deg_col[col])

        def spmm(feat):
            msg = feat[col] * w[:, None]
            return jax.ops.segment_sum(msg, row, num_segments=n)
        h = x
        out = h
        for _ in range(K):
            out = spmm(out) * BETA + h * ALPHA
        theta = BETA ** K + ALPHA * sum((BETA ** i for i in range(K)))
        return out / jnp.asarray(theta, dtype=x.dtype)

    def _L1_gnn_ref(h, edge_index, edge_attr, W_e, b_e, W_n, b_n):
        import jax, jax.numpy as jnp
        import numpy as np
        N, E = (50000, 25000)
        NODE_DIM, EDGE_DIM = (96, 64)
        IN_DIM = 2 * NODE_DIM + EDGE_DIM
        src, dst = (edge_index[0], edge_index[1])
        concat = jnp.concatenate([h[src], h[dst], edge_attr], axis=-1)
        gates = jax.nn.sigmoid(concat @ W_e + b_e)
        messages = jax.nn.softplus(concat @ W_n + b_n)
        gated = gates * messages
        n = h.shape[0]
        h_new = jax.ops.segment_sum(gated, dst, num_segments=n)
        edge_count = jax.ops.segment_sum(jnp.ones((dst.shape[0],), h.dtype), dst, num_segments=n)
        edge_count = jnp.clip(edge_count, 1.0, None)[:, None]
        return h + h_new / edge_count

    def _L2_gnn_ref(x, edge_index, W1, b1, W2, b2, gn1_w, gn1_b, gn1_a, gn2_w, gn2_b, gn2_a):
        import jax, jax.numpy as jnp
        import numpy as np
        EPS = 1e-05

        def _gcn_conv(x, edge_index, W, b):
            h = x @ W
            src, dst = (edge_index[0], edge_index[1])
            msgs = h[src]
            agg = jax.ops.segment_sum(msgs, dst, num_segments=x.shape[0])
            return agg + b

        def _graph_norm(x, weight, bias, mean_scale):
            mean = jnp.mean(x, axis=0, keepdims=True)
            xc = x - mean_scale * mean
            var = jnp.mean(xc * xc, axis=0, keepdims=True)
            return xc * jax.lax.rsqrt(var + EPS) * weight + bias
        identity = x
        h = _gcn_conv(x, edge_index, W1, b1)
        h = _graph_norm(h, gn1_w, gn1_b, gn1_a)
        h = jax.nn.relu(h)
        h = h + identity
        identity = h
        h2 = _gcn_conv(h, edge_index, W2, b2)
        h2 = _graph_norm(h2, gn2_w, gn2_b, gn2_a)
        h2 = jax.nn.relu(h2)
        h2 = h2 + identity
        return h2

    def _L3_gnn_ref(x, edge_index, edge_weight, W1, b1, W2, b2):
        import jax, jax.numpy as jnp
        import numpy as np
        N_NODES = 50000
        N_EDGES = 25000
        FEAT = 96

        def gcn_conv(x, edge_index, edge_weight, W, b, n_nodes):
            row, col = (edge_index[0], edge_index[1])
            loop = jnp.arange(n_nodes, dtype=edge_index.dtype)
            row = jnp.concatenate([row, loop])
            col = jnp.concatenate([col, loop])
            ew = jnp.concatenate([edge_weight, jnp.ones((n_nodes,), x.dtype)])
            deg = jax.ops.segment_sum(ew, col, num_segments=n_nodes)
            dinv = jnp.where(deg > 0, jax.lax.rsqrt(deg), jnp.zeros_like(deg))
            norm = dinv[row] * ew * dinv[col]
            h = x @ W
            msg = h[row] * norm[:, None]
            out = jax.ops.segment_sum(msg, col, num_segments=n_nodes)
            return out + b
        n = x.shape[0]
        h = gcn_conv(x, edge_index, edge_weight, W1, b1, n)
        h = jax.nn.relu(h)
        h = gcn_conv(h, edge_index, edge_weight, W2, b2, n)
        return jax.nn.log_softmax(h, axis=1)
    edge_index = jnp.stack([src, dst])
    h = jnp.maximum(_layernorm(x, axis=-1), 0.0)
    x = x + _L0_gnn_ref(h, edge_index)
    h = jnp.maximum(_layernorm(x, axis=-1), 0.0)
    x = x + _L1_gnn_ref(h, edge_index, edge_attr_64, L1_gnn_W_e, L1_gnn_b_e, L1_gnn_W_n, L1_gnn_b_n)
    h = jnp.maximum(_layernorm(x, axis=-1), 0.0)
    x = x + _L2_gnn_ref(h, edge_index, L2_gnn_W1, L2_gnn_b1, L2_gnn_W2, L2_gnn_b2, L2_gnn_gn1_w, L2_gnn_gn1_b, L2_gnn_gn1_a, L2_gnn_gn2_w, L2_gnn_gn2_b, L2_gnn_gn2_a)
    h = jnp.maximum(_layernorm(x, axis=-1), 0.0)
    x = x + _L3_gnn_ref(h, edge_index, edge_weight, L3_gnn_W1, L3_gnn_b1, L3_gnn_W2, L3_gnn_b2)
    return x

_drawn_inputs = setup_inputs


def setup_inputs(seed=0):
    import zlib

    import numpy as np

    out = dict(_drawn_inputs(seed))
    spreads = {'L2_gnn_b1': (0.0, 0.8),
     'L2_gnn_b2': (0.0, 0.8),
     'L2_gnn_gn1_w': (1.0, 0.2),
     'L2_gnn_gn1_b': (0.0, 0.33),
     'L2_gnn_gn1_a': (1.0, 0.2),
     'L2_gnn_gn2_w': (1.0, 0.2),
     'L2_gnn_gn2_b': (0.0, 0.339),
     'L2_gnn_gn2_a': (1.0, 0.2),
     'L3_gnn_b1': (0.0, 0.43),
     'L3_gnn_b2': (0.0, 0.271)}
    factors = {'edge_attr_64': 8.0, 'edge_weight': 8.0, 'L1_gnn_b_e': 8.0, 'L1_gnn_b_n': 8.0}
    for name, (base, spread) in spreads.items():
        noise = np.random.default_rng([zlib.crc32(name.encode()), seed]).standard_normal(out[name].shape)
        drawn = base * np.exp(spread * noise) if base else spread * noise
        out[name] = jnp.asarray(drawn.astype(out[name].dtype))
    for name, factor in factors.items():
        out[name] = (out[name] * factor).astype(out[name].dtype)
    return out
```

```python
from contextlib import ExitStack

import concourse.bass as bass
from concourse import mybir

F32, F16, BF16, I32 = mybir.dt.float32, mybir.dt.float16, mybir.dt.bfloat16, mybir.dt.int32
ALU = mybir.AluOpType
ACT = mybir.ActivationFunctionType
AX = mybir.AxisListType

P = 128
N, D, E, DE = 3125, 96, 103125, 64
NT = -(-N // P)
NP = NT * P
LAST = N - (NT - 1) * P
ET = 896
EG = ET // P
WIN = 8
NW = NP // WIN
WPT = P // WIN
WC = WIN * NT
CH = 4
ECH = 6
NO_NODE = 4000
QG = 5
TCLAMP = -(-E // P)
ETC = TCLAMP + 16
K_STEPS, ALPHA, BETA = 10, 0.1, 0.9
THETA = BETA ** K_STEPS + ALPHA * sum(BETA ** i for i in range(K_STEPS))
LN_EPS = 1e-5
USCALE = 64.0
RING = 5
EVAC0 = 7
LOSCALE = 2048.0


class Scope:

    def __init__(self, nc, ctx, stage):
        self.nc, self.ctx, self.stage = nc, ctx, stage

    def sb(self, name, shape, dt):
        return self.ctx.enter_context(self.nc.sbuf_tensor(f"{self.stage}_{name}", shape, dt))

    def ps(self, name, shape, dt=F32):
        return self.ctx.enter_context(self.nc.psum_tensor(f"{self.stage}_{name}", shape, dt))

    def sem(self, name):
        return self.ctx.enter_context(self.nc.semaphore(f"{self.stage}_{name}"))


class Chain:

    def __init__(self, eng, sem):
        self.eng, self.sem, self.n = eng, sem, 0

    def __call__(self, ins):
        self.n += 1
        ins.then_inc(self.sem, 1)
        self.eng.wait_ge(self.sem, self.n)


def edge_ranges(nc, src_cols, dst_cols, dst_rows, w_cols, tab_d, key, smod, wpart):
    with ExitStack() as ctx:
        m = Scope(nc, ctx, "ranges")
        srcI = m.sb("srcI", [P, ETC], I32)
        dstI = m.sb("dstI", [P, ETC], I32)
        rowsI = m.sb("rowsI", [P, EG, P], I32)
        weight = m.sb("weight", [P, ETC], F32)
        least = m.sb("least", [P, EG], F32)
        most = m.sb("most", [P, EG], F32)
        rowno = m.sb("rowno", [P, P], F32)
        colno = m.sb("colno", [P, P], F32)
        ident = m.sb("ident", [P, P], F32)
        ones = m.sb("ones", [P, P], F32)
        spread = m.sb("spread", [P, 2, EG, P], F32)
        up = m.sb("up", [P, ET], F32)
        down = m.sb("down", [P, ET], F32)
        low = m.sb("low", [P, QG], F32)
        high = m.sb("high", [P, QG], F32)
        below = m.sb("below", [P, ET], F32)
        touch = m.sb("touch", [P, ET], F32)
        tileI = rowsI[:, :, :].rearrange("p c e -> p (c e)")[:, 0:ETC]
        left = spread[:, 0, :, :].rearrange("p c e -> p (c e)")[:, 0:ETC]
        r1 = m.sb("r1", [P, QG], F32)
        r2 = m.sb("r2", [P, QG], F32)
        bounds = m.sb("bounds", [P, QG, 2], F32)
        boundsI = m.sb("boundsI", [P, QG, 2], I32)
        bc = m.ps("bc", [P, 4, 512])
        s_in = [m.sem(f"edges_loaded{i}") for i in range(4)]
        s_iota = m.sem("iotas_made")
        s_diag = m.sem("diagonals_made")
        s_bc = m.sem("bounds_broadcast")
        s_bounds = m.sem("bounds_made")
        s_tab = m.sem("bounds_stored")
        s_v = m.sem("ranges_dve_chain")
        block = ctx.enter_context(nc.Block())

        @block.sync
        def _(sp):
            sp.dma_start(rowsI[:, :, :], dst_rows.rearrange("(c p) e -> p c e", p=P)).then_inc(s_in[0], 16)
            sp.dma_start(srcI[:, :], src_cols).then_inc(s_in[1], 16)
            sp.dma_start(dstI[:, :], dst_cols).then_inc(s_in[2], 16)
            sp.dma_start(weight[:, :], w_cols).then_inc(s_in[3], 16)
            sp.wait_ge(s_bounds, 1)
            sp.dma_start(tab_d.rearrange("(q p) b -> p q b", p=P), boundsI[:, :, :]).then_inc(s_tab, 16)
            sp.wait_ge(s_tab, 16)

        @block.gpsimd
        def _(pool):
            nc.gpsimd.iota(colno[:, :], pattern=[[1, P]], base=0, channel_multiplier=0,
                           allow_small_or_imprecise_dtypes=True).then_inc(s_iota, 1)
            nc.gpsimd.iota(rowno[:, :], pattern=[[0, P]], base=0, channel_multiplier=1,
                           allow_small_or_imprecise_dtypes=True).then_inc(s_iota, 1)
            nc.gpsimd.iota(up[:, :], pattern=[[1, ET]], base=1, channel_multiplier=0,
                           allow_small_or_imprecise_dtypes=True).then_inc(s_iota, 1)
            nc.gpsimd.iota(down[:, :], pattern=[[-1, ET]], base=ET, channel_multiplier=0,
                           allow_small_or_imprecise_dtypes=True).then_inc(s_iota, 1)
            nc.gpsimd.iota(low[:, 0:QG - 1], pattern=[[WIN * P, QG - 1]], base=0, channel_multiplier=WIN,
                           allow_small_or_imprecise_dtypes=True).then_inc(s_iota, 1)
            nc.gpsimd.iota(high[:, 0:QG - 1], pattern=[[WIN * P, QG - 1]], base=WIN, channel_multiplier=WIN,
                           allow_small_or_imprecise_dtypes=True).then_inc(s_iota, 1)
            nc.gpsimd.iota(low[:, QG - 1:QG], pattern=[[0, 1]], base=0, channel_multiplier=P,
                           allow_small_or_imprecise_dtypes=True).then_inc(s_iota, 1)
            nc.gpsimd.iota(high[:, QG - 1:QG], pattern=[[0, 1]], base=P, channel_multiplier=P,
                           allow_small_or_imprecise_dtypes=True).then_inc(s_iota, 1)

        @block.tensor
        def _(pe):
            for b in range(2):
                pe.wait_ge(s_diag, b + 1)
                flat = spread[:, b, :, :].rearrange("p c e -> p (c e)")
                for h in range(2):
                    pe.matmul(bc[:, 2 * b + h, 0:ET // 2], ones[:, :], flat[:, h * ET // 2:(h + 1) * ET // 2],
                              start=True, stop=True).then_inc(s_bc, 1)

        @block.vector
        def _(dve):
            do = Chain(dve, s_v)
            dve.wait_ge(s_iota, 8)
            do(nc.vector.tensor_tensor(ident[:, :], rowno[:, :], colno[:, :], ALU.is_equal))
            do(nc.vector.memset(ones[:, :], 1.0))
            dve.wait_ge(s_in[0], 16)
            do(nc.vector.tensor_reduce(least[:, :], rowsI[:, :, :], AX.X, ALU.min))
            nc.vector.tensor_tensor(spread[:, 0, :, :], ident[:, :].unsqueeze(1).to_broadcast([P, EG, P]),
                                    least[:, :].unsqueeze(2).to_broadcast([P, EG, P]), ALU.mult).then_inc(s_diag, 1)
            do(nc.vector.tensor_reduce(most[:, :], rowsI[:, :, :], AX.X, ALU.max))
            nc.vector.tensor_tensor(spread[:, 1, :, :], ident[:, :].unsqueeze(1).to_broadcast([P, EG, P]),
                                    most[:, :].unsqueeze(2).to_broadcast([P, EG, P]), ALU.mult).then_inc(s_diag, 1)
            dve.wait_ge(s_bc, 4)
            for q in range(QG):
                for h in range(2):
                    cols = slice(h * ET // 2, (h + 1) * ET // 2)
                    do(nc.vector.tensor_scalar(below[:, cols], bc[:, h, 0:ET // 2], high[:, q:q + 1], None,
                                               ALU.is_lt))
                    do(nc.vector.scalar_tensor_tensor(touch[:, cols], bc[:, 2 + h, 0:ET // 2], low[:, q:q + 1],
                                                      below[:, cols], ALU.is_ge, ALU.mult))
                do(nc.vector.tensor_tensor(below[:, :], touch[:, :], down[:, :], ALU.mult))
                do(nc.vector.tensor_reduce(r1[:, q:q + 1], below[:, :], AX.X, ALU.max))
                do(nc.vector.tensor_tensor(touch[:, :], touch[:, :], up[:, :], ALU.mult))
                do(nc.vector.tensor_reduce(r2[:, q:q + 1], touch[:, :], AX.X, ALU.max))
            do(nc.vector.tensor_scalar(bounds[:, :, 0], r1[:, :], -1.0, float(ET), ALU.mult, ALU.add))
            do(nc.vector.tensor_scalar(bounds[:, :, 0], bounds[:, :, 0], float(TCLAMP), None, ALU.min))
            do(nc.vector.scalar_tensor_tensor(bounds[:, :, 1], bounds[:, :, 0], 1.0, r2[:, :], ALU.add, ALU.max))
            do(nc.vector.scalar_tensor_tensor(bounds[:, QG - 1:QG, 1], bounds[:, QG - 1:QG, 0], float(ECH + 1),
                                              r2[:, QG - 1:QG], ALU.add, ALU.max))
            nc.vector.tensor_copy(boundsI[:, :, :], bounds[:, :, :]).then_inc(s_bounds, 1)
            dve.wait_ge(s_in[1], 16)
            dve.wait_ge(s_in[2], 16)
            do(nc.vector.tensor_scalar(tileI, srcI[:, :], 7, None, ALU.logical_shift_right))
            do(nc.vector.tensor_scalar(srcI[:, :], srcI[:, :], P - 1, None, ALU.bitwise_and))
            do(nc.vector.scalar_tensor_tensor(key[:, :], dstI[:, :], float(NT), tileI, ALU.mult, ALU.add))
            do(nc.vector.tensor_copy(smod[:, :], srcI[:, :]))
            dve.wait_ge(s_in[3], 16)
            do(nc.vector.tensor_copy(wpart[:, 0, :], weight[:, :]))
            do(nc.vector.tensor_tensor(left, weight[:, :], wpart[:, 0, :], ALU.subtract))
            do(nc.vector.tensor_copy(wpart[:, 1, :], left))
            do(nc.vector.tensor_tensor(left, left, wpart[:, 1, :], ALU.subtract))
            do(nc.vector.tensor_copy(wpart[:, 2, :], left))


def build_matrices(nc, tab_d, key, smod, wpart, CT, indeg, C_d, W_d):
    with ExitStack() as ctx:
        m = Scope(nc, ctx, "build")
        tab = m.sb("tab", [4, NW // 4, 2], I32)
        colsM = m.sb("colsM", [P, WC, CH], F16)
        colsS = m.sb("colsS", [P, P, CH], F16)
        wbase = m.sb("wbase", [P, NW], F32)
        ident = m.sb("ident16", [P, P], F16)
        rowh = m.sb("rowh", [P, P], F16)
        kw = m.sb("kw", [P, 3, CH], F16)
        M = m.sb("M", [P, 3, WC, CH], BF16)
        S = m.sb("S", [P, 3, 4, P, CH], BF16)
        Cblk = m.sb("Cblk", [P, NT, P], F16)
        Wblk = m.sb("Wblk", [P, NT, P], F32)
        win = m.ps("win", [P, 4, 512])
        tp = m.ps("tp", [P, 2, 8, P], F16)
        s_const = m.sem("constants_made")
        s_tab = m.sem("table_loaded")
        s_key = m.sem("window_keys")
        s_hot = m.sem("source_onehots")
        s_made = m.sem("operands_made")
        s_built = m.sem("window_built")
        s_evac = m.sem("window_out")
        s_xkey = m.sem("more_keys")
        s_xhot = m.sem("more_source_onehots")
        s_xmade = m.sem("more_operands_made")
        s_xused = m.sem("more_operands_used")
        s_tp = m.sem("tile_transposed")
        s_ct = m.sem("transposed_out")
        s_cst = m.sem("C_stored")
        s_wst = m.sem("W_stored")
        block = ctx.enter_context(nc.Block())

        @block.gpsimd
        def _(pool):
            small = dict(allow_small_or_imprecise_dtypes=True)
            for k in range(NT):
                nc.gpsimd.iota(colsM[:, k * WIN:(k + 1) * WIN, :], pattern=[[NT, WIN], [0, CH]], base=k,
                               channel_multiplier=0, **small).then_inc(s_const, 1)
            nc.gpsimd.iota(colsS[:, :, :], pattern=[[1, P], [0, CH]], base=0, channel_multiplier=0,
                           **small).then_inc(s_const, 1)
            nc.gpsimd.iota(wbase[:, :], pattern=[[WC, NW]], base=0, channel_multiplier=0,
                           **small).then_inc(s_const, 1)
            nc.gpsimd.iota(rowh[:, :], pattern=[[0, P]], base=0, channel_multiplier=1,
                           **small).then_inc(s_const, 1)

        @block.sync
        def _(sp):
            sp.dma_start(tab[:, :, :], tab_d[0:NW, :].rearrange("(i b) c -> b i c", b=4)).then_inc(s_tab, 16)
            with sp.Fori(0, NT) as j:
                sp.wait_ge(s_evac, j * (2 * WPT) + 2 * WPT + EVAC0)
                sp.dma_start(C_d[bass.ds(j, 1), :, :].rearrange("o p c -> p (o c)"),
                             Cblk[:, :, :].rearrange("p k d -> p (k d)")).then_inc(s_cst, 16)
                sp.dma_start(W_d[bass.ds(j, 1), :, :].rearrange("o p c -> p (o c)"),
                             Wblk[:, :, :].rearrange("p k d -> p (k d)")).then_inc(s_wst, 16)
            sp.wait_ge(s_cst, 16 * NT + 1)
            sp.wait_ge(s_wst, 16 * NT + 1)

        @block.vector
        def _(dve):
            dve.wait_ge(s_const, NT + 3)
            nc.vector.tensor_tensor(ident[:, :], rowh[:, :], colsS[:, :, 0], ALU.is_equal).then_inc(s_const, 1)
            dve.wait_ge(s_tab, 16)

            def operands(slot, w, t, keys, hots, made, n):
                nc.vector.tensor_scalar(kw[:, slot, :], key[:, bass.ds(t, CH)], wbase[:, bass.ds(w, 1)], 1000.0,
                                        ALU.subtract, ALU.min).then_inc(keys, 1)
                nc.vector.tensor_tensor(S[:, slot, 0, :, :], colsS[:, :, :],
                                        smod[:, bass.ds(t, CH)].unsqueeze(1).to_broadcast([P, P, CH]),
                                        ALU.is_equal).then_inc(hots, 1)
                dve.wait_ge(keys, n)
                nc.vector.tensor_tensor(M[:, slot, :, :], colsM[:, :, :],
                                        kw[:, slot, :].unsqueeze(1).to_broadcast([P, WC, CH]), ALU.is_equal)
                dve.wait_ge(hots, n)
                for part in range(3):
                    last = nc.vector.tensor_tensor(
                        S[:, slot, 1 + part, :, :], S[:, slot, 0, :, :],
                        wpart[:, part, bass.ds(t, CH)].unsqueeze(1).to_broadcast([P, P, CH]), ALU.mult)
                last.then_inc(made, 1)

            more = dve.alloc_register("dve_more")
            dve.reg_mov(more, 0)
            with dve.Fori(0, NW // 4) as i:
                w0 = i * 4
                for b in range(4):
                    t = dve.value_load(tab[b:b + 1, bass.ds(i, 1), 0:1], min_val=0, max_val=TCLAMP)
                    end = dve.value_load(tab[b:b + 1, bass.ds(i, 1), 1:2], min_val=1, max_val=TCLAMP + 1)
                    dve.wait_ge(s_built, w0 + b + 1)
                    operands(b % 2, w0 + b, t, s_key, s_hot, s_made, w0 + b + 1)
                    with dve.If(end > t + CH):
                        with dve.Fori(t + CH, end, CH) as tx:
                            dve.wait_ge(s_xused, dve.snap(more) + 1)
                            dve.reg_add(more, more, 1)
                            operands(2, w0 + b, tx, s_xkey, s_xhot, s_xmade, dve.snap(more))

        @block.tensor
        def _(pe):
            pe.sem_inc(s_built, 2)
            pe.sem_inc(s_xused, 1)
            pe.sem_inc(s_evac, EVAC0)
            pe.sem_inc(s_ct, 2)
            pe.sem_inc(s_cst, 1)
            pe.sem_inc(s_wst, 1)
            pe.wait_ge(s_tab, 16)
            pe.wait_ge(s_const, NT + 4)

            def products(slot, bank, tiles, first):
                for u in tiles:
                    for part in range(4):
                        out = win[:, bank, 0:WC] if part == 0 else win[:, bank, WC:2 * WC]
                        mm = pe.matmul(out, S[:, slot, part, :, u], M[:, slot, :, u],
                                       start=(first and u == 0 and part == 0),
                                       stop=(u == CH - 1 and part in (0, 3)), skip_group_check=True)
                return mm

            more = pe.alloc_register("pe_more")
            pe.reg_mov(more, 0)
            with pe.Fori(0, NT) as j:
                with pe.Fori(0, WPT // 4) as q:
                    i = j * (WPT // 4) + q
                    w0 = j * WPT + q * 4
                    for b in range(4):
                        t = pe.value_load(tab[b:b + 1, bass.ds(i, 1), 0:1], min_val=0, max_val=TCLAMP)
                        end = pe.value_load(tab[b:b + 1, bass.ds(i, 1), 1:2], min_val=1, max_val=TCLAMP + 1)
                        pe.wait_ge(s_evac, 2 * w0 + 2 * b + 1)
                        pe.wait_ge(s_made, w0 + b + 1)
                        products(b % 2, b, range(CH - 1), True)
                        with pe.If(end > t + CH):
                            with pe.Fori(t + CH, end, CH):
                                pe.reg_add(more, more, 1)
                                pe.wait_ge(s_xmade, pe.snap(more))
                                products(2, b, range(CH), False).then_inc(s_xused, 1)
                        products(b % 2, b, range(CH - 1, CH), False).then_inc(s_built, 1)
                pe.wait_ge(s_evac, j * (2 * WPT) + 2 * WPT + EVAC0)
                for g in range(5):
                    pe.wait_ge(s_ct, j * 5 + g + 1)
                    for k in range(5):
                        mm = pe.transpose(tp[:, g % 2, k, :], Cblk[:, 5 * g + k, :], ident[:, :])
                    mm.then_inc(s_tp, 1)

        @block.scalar
        def _(act):
            with act.Fori(0, NT) as j:
                act.wait_ge(s_cst, j * 16 + 1)
                act.wait_ge(s_wst, j * 16 + 1)
                with act.Fori(0, WPT // 4) as q:
                    i = j * (WPT // 4) + q
                    w0 = j * WPT + q * 4
                    for b in range(4):
                        at = q * (4 * WIN) + b * WIN
                        act.wait_ge(s_built, w0 + b + 3)
                        nc.scalar.activation(Cblk[:, :, bass.ds(at, WIN)],
                                             win[:, b, 0:WC].rearrange("p (k d) -> p k d", d=WIN),
                                             ACT.Copy, scale=0.5).then_inc(s_evac, 1)
                        nc.scalar.activation(Wblk[:, :, bass.ds(at, WIN)],
                                             win[:, b, WC:2 * WC].rearrange("p (k d) -> p k d", d=WIN),
                                             ACT.Copy).then_inc(s_evac, 1)
                for g in range(5):
                    act.wait_ge(s_tp, j * 5 + g + 1)
                    nc.scalar.activation(CT[:, bass.ds(j, 1), g * 5 * P:(g + 1) * 5 * P],
                                         tp[:, g % 2, 0:5, :].rearrange("p k d -> p (k d)").unsqueeze(1), ACT.Copy,
                                         accum_out=indeg[:, bass.ds(j * 5 + g, 1)]).then_inc(s_ct, 1)


def layernorm_relu(nc, do, act_do, x, out, stat, scratch, eps=LN_EPS):
    mean, var, rstd = stat[:, 0, :], stat[:, 1, :], stat[:, 2, :]
    do(nc.vector.tensor_reduce(mean, x, AX.X, ALU.add))
    do(nc.vector.tensor_scalar(mean, mean, 1.0 / D, None, ALU.mult))
    do(nc.vector.tensor_tensor(out, x, mean.unsqueeze(2).to_broadcast([P, NT, D]), ALU.subtract))
    do(nc.vector.tensor_tensor(scratch, out, out, ALU.mult))
    do(nc.vector.tensor_reduce(var, scratch, AX.X, ALU.add))
    do(nc.vector.tensor_scalar(var, var, 1.0 / D, eps, ALU.mult, ALU.add))
    act_do()
    do(nc.vector.reciprocal(rstd, rstd))
    do(nc.vector.tensor_tensor(out, out, rstd.unsqueeze(2).to_broadcast([P, NT, D]), ALU.mult))
    do(nc.vector.tensor_scalar(out, out, 0.0, None, ALU.max))


def propagate(nc, x_in, CT, indeg, x_out_d):
    with ExitStack() as ctx:
        m = Scope(nc, ctx, "layer0")
        x = m.sb("x", [P, NT, D], F32)
        h = m.sb("h", [P, NT, D], F32)
        g = m.sb("g", [P, NT, D], F32)
        U = m.sb("U", [P, 2, NT, 2, D], F16)
        one = m.sb("one", [P, 1], F16)
        stat = m.sb("stat", [P, 3, NT], F32)
        dc = m.sb("dc", [P, NT], F32)
        dr = m.sb("dr", [P, NT], F32)
        gd = m.sb("gd", [P, NT], F32)
        a = m.sb("a", [P, NT], F32)
        c = m.sb("c", [P, NT], F32)
        lo, s, v, d = (h[:, i * RING:(i + 1) * RING, :] for i in range(4))
        acc = m.ps("acc", [P, RING, 512])
        deg = m.ps("deg", [P, 512])
        s_x = m.sem("x_loaded")
        s_one = m.sem("one_made")
        s_deg = m.sem("out_degrees")
        s_v = m.sem("dve_chain")
        s_var = m.sem("root_wanted")
        s_root = m.sem("root_made")
        s_u = m.sem("part_pairs_made")
        s_acc = m.sem("products_done")
        s_lo = m.sem("low_sums_out")
        s_s = m.sem("sums_made")
        s_new = m.sem("values_made")
        s_hi = m.sem("high_parts_made")
        s_d = m.sem("rests_made")
        s_fin = m.sem("x_updated")
        s_st = m.sem("x_stored")
        block = ctx.enter_context(nc.Block())

        @block.sync
        def _(sp):
            sp.dma_start(x[:, :, :], x_in.rearrange("(k p) f -> p k f", p=P)).then_inc(s_x, 16)
            sp.wait_ge(s_fin, NT)
            sp.dma_start(x_out_d.rearrange("(k p) f -> p k f", p=P), x[:, :, :]).then_inc(s_st, 16)
            sp.wait_ge(s_st, 16)

        @block.vector
        def _(dve):
            do = Chain(dve, s_v)

            def root(n):
                def wait():
                    dve.sem_inc(s_var, 1)
                    dve.wait_ge(s_root, n)
                return wait

            nc.vector.memset(one[:, :], 1.0).then_inc(s_one, 1)
            dve.wait_ge(s_x, 16)
            layernorm_relu(nc, do, root(1), x[:, :, :], h[:, :, :], stat, g[:, :, :])
            do(nc.vector.tensor_reduce(dc[:, :], indeg[:, :].rearrange("p (j g) -> p j g", g=5), AX.X, ALU.add))
            dve.wait_ge(s_deg, 1)
            do(nc.vector.tensor_scalar(dr[:, :], deg[:, 0:NT], 2.0, 1.0, ALU.mult, ALU.max))
            do(nc.vector.tensor_scalar(dc[:, :], dc[:, :], 2.0, 1.0, ALU.mult, ALU.max))
            root(3)()
            do(nc.vector.reciprocal(dc[:, :], dc[:, :]))
            do(nc.vector.reciprocal(dr[:, :], dr[:, :]))
            do(nc.vector.tensor_scalar(gd[:, :], dc[:, :], ALPHA * USCALE, None, ALU.mult))
            do(nc.vector.scalar_tensor_tensor(a[:, :], dr[:, :], 2.0 * BETA, dc[:, :], ALU.mult, ALU.mult))
            do(nc.vector.tensor_scalar(c[:, :], dr[:, :], 2.0 * BETA / USCALE / THETA, None, ALU.mult))
            do(nc.vector.tensor_tensor(g[:, :, :], h[:, :, :], gd[:, :].unsqueeze(2).to_broadcast([P, NT, D]), ALU.mult))
            do(nc.vector.scalar_tensor_tensor(x[:, :, :], h[:, :, :], ALPHA / THETA, x[:, :, :], ALU.mult, ALU.add))
            do(nc.vector.tensor_scalar(h[:, :, :], g[:, :, :], 1.0 / ALPHA, None, ALU.mult))
            do(nc.vector.tensor_copy(U[:, 0, :, 0, :], h[:, :, :]))
            do(nc.vector.tensor_tensor(h[:, :, :], h[:, :, :], U[:, 0, :, 0, :], ALU.subtract))
            do(nc.vector.tensor_scalar(U[:, 0, :, 1, :], h[:, :, :], LOSCALE, None, ALU.mult))
            dve.sem_inc(s_u, NT)

            def step(nxt, at, n):
                for k in range(NT):
                    dve.wait_ge(s_lo, n + k + 1 + RING)
                    nc.vector.tensor_tensor(s[:, k % RING, :], lo[:, k % RING, :], acc[:, k % RING, 0:D], ALU.add).then_inc(s_s, 1)
                    dve.wait_ge(s_s, n + k + 1 + RING)
                    if nxt is None:
                        nc.vector.scalar_tensor_tensor(x[:, k, :], s[:, k % RING, :], c[:, k:k + 1], x[:, k, :],
                                                       ALU.mult, ALU.add).then_inc(s_fin, 1)
                        continue
                    nc.vector.scalar_tensor_tensor(v[:, k % RING, :], s[:, k % RING, :], a[:, k:k + 1], g[:, k, :],
                                                   ALU.mult, ALU.add).then_inc(s_new, 1)
                    dve.wait_ge(s_hi, n + k + 1)
                    nc.vector.tensor_tensor(d[:, k % RING, :], v[:, k % RING, :], U[:, nxt, k, 0, :], ALU.subtract).then_inc(s_d, 1)

            with dve.Fori(0, K_STEPS - 2, 2) as i:
                for b in range(2):
                    step(1 - b, b, i * NT + b * NT)
            step(1, 0, (K_STEPS - 2) * NT)
            step(None, 1, (K_STEPS - 1) * NT)

        @block.scalar
        def _(act):
            act.wait_ge(s_var, 1)
            nc.scalar.sqrt(stat[:, 2, :], stat[:, 1, :]).then_inc(s_root, 1)
            act.wait_ge(s_var, 2)
            nc.scalar.sqrt(dc[:, :], dc[:, :]).then_inc(s_root, 1)
            nc.scalar.sqrt(dr[:, :], dr[:, :]).then_inc(s_root, 1)

            def step(nxt, n):
                for k in range(NT + 1):
                    if k < NT:
                        act.wait_ge(s_acc, n + k + 1)
                        nc.scalar.activation(lo[:, k % RING, :], acc[:, k % RING, D:2 * D], ACT.Copy,
                                             scale=1.0 / LOSCALE).then_inc(s_lo, 1)
                        if nxt is not None:
                            act.wait_ge(s_new, n + k + 1)
                            nc.scalar.activation(U[:, nxt, k, 0, :], v[:, k % RING, :], ACT.Copy).then_inc(s_hi, 1)
                    if k >= 1 and nxt is not None:
                        act.wait_ge(s_d, n + k)
                        nc.scalar.activation(U[:, nxt, k - 1, 1, :], d[:, (k - 1) % RING, :], ACT.Copy,
                                             scale=LOSCALE).then_inc(s_u, 1)

            with act.Fori(0, K_STEPS - 2, 2) as i:
                for b in range(2):
                    step(1 - b, i * NT + b * NT)
            step(1, (K_STEPS - 2) * NT)
            step(None, (K_STEPS - 1) * NT)

        @block.tensor
        def _(pe):
            pe.sem_inc(s_lo, RING)
            pe.sem_inc(s_s, RING)
            pe.wait_ge(s_one, 1)
            for k in range(NT):
                for t in range(NT):
                    mm = pe.matmul(deg[:, k:k + 1], CT[:, t, k * P:(k + 1) * P], one[:, :],
                                   start=(t == 0), stop=(t == NT - 1))
            mm.then_inc(s_deg, 1)

            def step(cur, n):
                for k in range(NT):
                    pe.wait_ge(s_lo, n + k + 1)
                    pe.wait_ge(s_s, n + k + 1)
                    for t in range(NT):
                        if k == 0:
                            pe.wait_ge(s_u, n + t + 1)
                        mm = pe.matmul(acc[:, k % RING, 0:2 * D], CT[:, t, k * P:(k + 1) * P],
                                       U[:, cur, t, :, :].rearrange("p a f -> p (a f)"),
                                       start=(t == 0), stop=(t == NT - 1))
                    mm.then_inc(s_acc, 1)

            with pe.Fori(0, K_STEPS - 2, 2) as i:
                for b in range(2):
                    step(b, i * NT + b * NT)
            step(0, (K_STEPS - 2) * NT)
            step(1, (K_STEPS - 1) * NT)


def node_terms(nc, x_in, We, be, Wn, bn, P_d, x, Q3, ident, colno):
    D2 = 2 * D
    with ExitStack() as ctx:
        m = Scope(nc, ctx, "terms1")
        h = m.sb("h", [P, NT, D], F32)
        stat = m.sb("stat", [P, 3, NT], F32)
        rowno = m.sb("rowno", [P, P], F32)
        W = m.sb("W", [D, 2, D2], F32)
        bias = m.sb("bias", [P, D2], F32)
        hT = m.sb("hT", [D, 2, P], F32)
        Pn = m.sb("Pn", [P, NT, D2], F32)
        Qf = m.sb("Qf", [P, NT, D2], F32)
        tp = m.ps("tp", [P, 2, 512])
        prod = m.ps("prod", [P, 2, 512])
        s_x = m.sem("x_loaded")
        s_w = m.sem("weights_loaded")
        s_c = m.sem("iotas_made")
        s_id = m.sem("identity_made")
        s_v = m.sem("dve_chain")
        s_var = m.sem("root_wanted")
        s_root = m.sem("root_made")
        s_h = m.sem("h_made")
        s_tp = m.sem("h_turned")
        s_hT = m.sem("turned_h_out")
        s_pr = m.sem("products_done")
        s_P = m.sem("source_terms_out")
        s_Q = m.sem("target_terms_out")
        s_st = m.sem("source_terms_stored")
        block = ctx.enter_context(nc.Block())

        @block.sync
        def _(sp):
            sp.dma_start(x[:, :, :], x_in.rearrange("(k p) f -> p k f", p=P)).then_inc(s_x, 16)
            for i, (w, b) in enumerate(((We, be), (Wn, bn))):
                sp.dma_start(W[:, 0, i * D:(i + 1) * D], w[0:D, :]).then_inc(s_w, 16)
                sp.dma_start(W[:, 1, i * D:(i + 1) * D], w[D:2 * D, :]).then_inc(s_w, 16)
                sp.dma_start(bias[:, i * D:(i + 1) * D],
                             b.rearrange("(o f) -> o f", o=1).to_broadcast([P, D])).then_inc(s_w, 16)
            sp.wait_ge(s_P, NT)
            sp.dma_start(P_d.rearrange("(k p) f -> p k f", p=P), Pn[:, :, :]).then_inc(s_st, 16)
            sp.wait_ge(s_st, 16)

        @block.gpsimd
        def _(pool):
            nc.gpsimd.iota(colno[:, :], pattern=[[1, P]], base=0, channel_multiplier=0,
                           allow_small_or_imprecise_dtypes=True).then_inc(s_c, 1)
            nc.gpsimd.iota(rowno[:, :], pattern=[[0, P]], base=0, channel_multiplier=1,
                           allow_small_or_imprecise_dtypes=True).then_inc(s_c, 1)

        @block.vector
        def _(dve):
            do = Chain(dve, s_v)

            def root():
                dve.sem_inc(s_var, 1)
                dve.wait_ge(s_root, 1)

            dve.wait_ge(s_c, 2)
            nc.vector.tensor_tensor(ident[:, :], rowno[:, :], colno[:, :], ALU.is_equal).then_inc(s_id, 1)
            dve.wait_ge(s_x, 16)
            layernorm_relu(nc, do, root, x[:, :, :], h[:, :, :], stat, Qf[:, :, 0:D])
            dve.sem_inc(s_h, 1)
            do(nc.vector.tensor_tensor(x[:, :, :], x[:, :, :], h[:, :, :], ALU.add))
            dve.wait_ge(s_w, 96)
            for k in range(NT):
                dve.wait_ge(s_P, k + 1)
                nc.vector.tensor_tensor(Qf[:, k, :], prod[:, k % 2, D2:2 * D2], bias[:, :], ALU.add).then_inc(s_Q, 1)
            dve.wait_ge(s_Q, NT)
            do(nc.vector.tensor_copy(Q3[:, :, 0, :], Qf[:, :, :]))
            do(nc.vector.tensor_tensor(Qf[:, :, :], Qf[:, :, :], Q3[:, :, 0, :], ALU.subtract))
            do(nc.vector.tensor_copy(Q3[:, :, 1, :], Qf[:, :, :]))
            do(nc.vector.tensor_tensor(Qf[:, :, :], Qf[:, :, :], Q3[:, :, 1, :], ALU.subtract))
            do(nc.vector.tensor_copy(Q3[:, :, 2, :], Qf[:, :, :]))

        @block.scalar
        def _(act):
            act.wait_ge(s_var, 1)
            nc.scalar.sqrt(stat[:, 2, :], stat[:, 1, :]).then_inc(s_root, 1)
            for k in range(NT):
                act.wait_ge(s_tp, k + 1)
                nc.scalar.activation(hT[:, k % 2, :], tp[0:D, k % 2, 0:P], ACT.Copy).then_inc(s_hT, 1)
                act.wait_ge(s_pr, k + 1)
                nc.scalar.activation(Pn[:, k, :], prod[:, k % 2, 0:D2], ACT.Copy).then_inc(s_P, 1)

        @block.tensor
        def _(pe):
            pe.wait_ge(s_id, 1)
            pe.wait_ge(s_w, 96)
            pe.wait_ge(s_h, 1)
            for k in range(NT + 1):
                if k < NT:
                    if k >= 2:
                        pe.wait_ge(s_hT, k - 1)
                    pe.transpose(tp[0:D, k % 2, 0:P], h[:, k, :], ident[:, :]).then_inc(s_tp, 1)
                if k >= 1:
                    pe.wait_ge(s_hT, k)
                    if k >= 3:
                        pe.wait_ge(s_Q, k - 2)
                    pe.matmul(prod[:, (k - 1) % 2, 0:2 * D2], hT[:, (k - 1) % 2, :],
                              W[:, :, :].rearrange("p s f -> p (s f)"), start=True, stop=True).then_inc(s_pr, 1)


def gated_edges(nc, x_in, src_cols, dst_cols, w_cols, attr, We, be, Wn, bn, tab_d, P_d, x_out_d, wdeg):
    D2 = 2 * D
    with ExitStack() as ctx:
        m = Scope(nc, ctx, "layer1")
        x = m.sb("x", [P, NT, D], F32)
        Q3 = m.sb("Q3", [P, NT, 3, D2], BF16)
        ident = m.sb("ident", [P, P], F32)
        colno = m.sb("colno", [P, P], F32)
        agg = m.sb("agg", [P, NT, D + 2], F32)
        node_terms(nc, x_in, We, be, Wn, bn, P_d, x, Q3, ident, colno)
        srcs = m.sb("srcs", [P, 3, 2], I32)
        dstF = m.sb("dstF", [P, ETC], F32)
        dstI = m.sb("dstI", [P, ETC], I32)
        ew = m.sb("ew", [P, ETC], F32)
        tab = m.sb("tab", [1, NT, 2], I32)
        jbase = m.sb("jbase", [P, NT], F32)
        Wa = m.sb("Wa", [DE, D2], F32)
        zero = m.sb("zero", [P, P], BF16)
        rel = m.sb("rel", [P, ECH], F32)
        count = m.sb("count", [P, NT], F32)
        at = m.sb("at", [DE, 3, 2 * P], F32)
        R = m.sb("R", [P, 3, 2, D2], F32)
        hot = m.sb("hot", [P, 3, 2, P], F32)
        hotT = m.sb("hotT", [P, 3, 2, P], BF16)
        z = m.sb("z", [P, 3, 2, D2], F32)
        y = m.sb("y", [P, 3, 2, D2], F32)
        G = m.sb("G", [P, 3, 2, D + 2], F32)
        zp = m.ps("zp", [P, 3, 512])
        tp = m.ps("tp", [P, 512])
        acc = m.ps("acc", [P, 512])
        s_c = m.sem("constants_made")
        s_tab = m.sem("ranges_loaded")
        s_dst = m.sem("targets_loaded")
        s_w = m.sem("weights_loaded")
        s_ew = m.sem("edge_weights_loaded")
        s_at = [m.sem(f"attributes_loaded{k}") for k in range(3)]
        s_ix = [m.sem(f"sources_loaded{k}") for k in range(3)]
        s_R = [m.sem(f"source_terms_gathered{k}") for k in range(3)]
        s_gs = m.sem("gathers_begun")
        s_begun = m.sem("loads_begun")
        s_rel = m.sem("relative_targets_made")
        s_hot = m.sem("onehots_made")
        s_tp = m.sem("onehots_turned")
        s_hT = m.sem("turned_onehots_out")
        s_att = m.sem("attribute_products_done")
        s_z = m.sem("z_summed")
        s_add = m.sem("z_out")
        s_abs = m.sem("magnitudes_made")
        s_e = m.sem("exponentials_made")
        s_l = m.sem("logarithms_made")
        s_ms = m.sem("gate_log_and_message_made")
        s_g = m.sem("gates_made")
        s_G = m.sem("gated_messages_made")
        s_seg = m.sem("pair_aggregated")
        s_agg = m.sem("node_tile_out")
        s_v = m.sem("dve_chain")
        s_st = m.sem("x_stored")
        s_fin = m.sem("x_updated")
        block = ctx.enter_context(nc.Block())

        def ranges(eng, j):
            t0 = eng.value_load(tab[0:1, bass.ds(j, 1), 0:1], min_val=0, max_val=TCLAMP)
            end = eng.value_load(tab[0:1, bass.ds(j, 1), 1:2], min_val=ECH + 1, max_val=TCLAMP + ECH + 1)
            return t0, end

        @block.sync
        def _(sp):
            sp.dma_start(tab[:, :, :], tab_d[(QG - 1) * P:(QG - 1) * P + NT, :].rearrange("(o q) b -> o q b", o=1)).then_inc(s_tab, 16)
            sp.dma_start(dstI[:, :], dst_cols).then_inc(s_dst, 16)
            sp.dma_start(ew[:, :], w_cols).then_inc(s_ew, 16)
            sp.dma_start(Wa[:, 0:D], We[2 * D:, :]).then_inc(s_w, 16)
            sp.dma_start(Wa[:, D:], Wn[2 * D:, :]).then_inc(s_w, 16)
            sp.wait_ge(s_tab, 16)
            n = sp.alloc_register("sp_pairs")
            sp.reg_mov(n, 0)

            def chunk(t):
                c = sp.snap(n)
                for k in range(3):
                    sp.wait_ge(s_add, c + k + 1)
                    sp.sem_inc(s_begun, 1)
                    sp.dma_start(srcs[:, k, :], src_cols[:, bass.ds(t + 2 * k, 2)]).then_inc(s_ix[k], 16)
                    sp.wait_ge(s_att, c + k + 1)
                    sp.dma_start(at[:, k, :], attr[:, bass.ds(t * P + 2 * k * P, 2 * P)]).then_inc(s_at[k], 16)
                sp.reg_add(n, n, 3)

            with sp.Fori(0, NT) as j:
                t0, end = ranges(sp, j)
                with sp.Fori(t0, end, ECH) as t:
                    chunk(t)
            sp.wait_ge(s_fin, 1)
            sp.dma_start(x_out_d.rearrange("(k p) f -> p k f", p=P), x[:, :, :]).then_inc(s_st, 16)
            sp.wait_ge(s_st, 16)

        @block.gpsimd
        def _(pool):
            nc.gpsimd.iota(jbase[:, :], pattern=[[P, NT]], base=0, channel_multiplier=0,
                           allow_small_or_imprecise_dtypes=True).then_inc(s_c, 1)
            nc.gpsimd.memset(zero[:, :], 0.0).then_inc(s_c, 1)
            nc.gpsimd.memset(G[:, :, :, D + 1:D + 2], 1.0).then_inc(s_c, 1)
            pool.wait_ge(s_tab, 16)
            n = pool.alloc_register("pool_chunks")
            pool.reg_mov(n, 0)
            with pool.Fori(0, NT) as j:
                t0, end = ranges(pool, j)
                with pool.Fori(t0, end, ECH):
                    pool.reg_add(n, n, 16)
                    c = pool.snap(n)
                    for k in range(3):
                        pool.wait_ge(s_ix[k], c)
                        pool.sem_inc(s_gs, 1)
                        for u in range(2):
                            nc.gpsimd.indirect_dma_start(
                                R[:, k, u, :], None, P_d,
                                bass.IndirectOffsetOnAxis(ap=srcs[:, k, u:u + 1], axis=0)).then_inc(s_R[k], 16)

        @block.vector
        def _(dve):
            do = Chain(dve, s_v)
            dve.wait_ge(s_c, 3)
            dve.wait_ge(s_dst, 16)
            do(nc.vector.tensor_copy(dstF[:, :], dstI[:, :]))
            dve.wait_ge(s_ew, 16)
            dve.wait_ge(s_tab, 16)
            n = dve.alloc_register("dve_pairs")
            dve.reg_mov(n, 0)
            gathered = dve.alloc_register("dve_gathered")
            dve.reg_mov(gathered, 0)

            def relative(t, j, c):
                dve.wait_ge(s_hot, c + 1)
                nc.vector.tensor_scalar(rel[:, :], dstF[:, bass.ds(t, ECH)], jbase[:, bass.ds(j, 1)], None,
                                        ALU.subtract).then_inc(s_rel, 3)
                dve.wait_ge(s_rel, c + 3)

            def onehots(k, t, p):
                dve.wait_ge(s_seg, p + 1)
                nc.vector.tensor_copy(G[:, k, :, D:D + 1], ew[:, bass.ds(t + 2 * k, 2)].unsqueeze(2))
                nc.vector.tensor_tensor(hot[:, k, :, :], colno[:, :].unsqueeze(1).to_broadcast([P, 2, P]),
                                        rel[:, 2 * k:2 * k + 2].unsqueeze(2).to_broadcast([P, 2, P]),
                                        ALU.is_equal).then_inc(s_hot, 1)

            def add(k, p, c):
                dve.wait_ge(s_z, p + 1)
                dve.wait_ge(s_R[k], c)
                nc.vector.tensor_tensor(z[:, k, :, :], zp[:, k, 0:2 * D2].rearrange("p (u f) -> p u f", u=2),
                                        R[:, k, :, :], ALU.add).then_inc(s_add, 1)

            def logs(k, p):
                dve.wait_ge(s_l, p + 1)
                nc.vector.scalar_tensor_tensor(z[:, k, :, 0:D], z[:, k, :, 0:D], 0.0, y[:, k, :, 0:D],
                                               ALU.min, ALU.subtract)
                nc.vector.scalar_tensor_tensor(z[:, k, :, D:], z[:, k, :, D:], 0.0, y[:, k, :, D:],
                                               ALU.max, ALU.add).then_inc(s_ms, 1)

            def gated(k, p):
                dve.wait_ge(s_g, p + 1)
                nc.vector.tensor_tensor(G[:, k, :, 0:D], y[:, k, :, 0:D], z[:, k, :, D:],
                                        ALU.mult).then_inc(s_G, 1)

            with dve.Fori(0, NT) as j:
                t0, end = ranges(dve, j)
                a = dve.snap(n)
                dve.reg_add(gathered, gathered, 32)
                now = dve.snap(gathered)
                relative(t0, j, a)
                for k in range(3):
                    onehots(k, t0, a + k)
                    if k >= 1:
                        add(k - 1, a + (k - 1), now)
                    if k >= 2:
                        logs(k - 2, a + (k - 2))
                        gated(k - 2, a + (k - 2))
                with dve.Fori(t0 + ECH, end, ECH) as t:
                    c = dve.snap(n) + 3
                    before = dve.snap(gathered)
                    dve.reg_add(gathered, gathered, 32)
                    now = dve.snap(gathered)
                    relative(t, j, c)
                    for k in range(3):
                        onehots(k, t, c + k)
                        add((k + 2) % 3, c + (k - 1), before if k == 0 else now)
                        logs((k + 1) % 3, c + (k - 2))
                        gated((k + 1) % 3, c + (k - 2))
                    dve.reg_add(n, n, 3)
                b = dve.snap(n) + 3
                add(2, b - 1, dve.snap(gathered))
                logs(1, b - 2)
                gated(1, b - 2)
                logs(2, b - 1)
                gated(2, b - 1)
                dve.wait_ge(s_seg, b + 3)
                nc.vector.tensor_copy(agg[:, bass.ds(j, 1), :], acc[:, 0:D + 2].unsqueeze(1)).then_inc(s_agg, 1)
                dve.reg_add(n, n, 3)
            dve.wait_ge(s_agg, NT + 1)
            cnt = count[:, :]
            do(nc.vector.tensor_copy(wdeg[:, :], agg[:, :, D]))
            do(nc.vector.tensor_scalar(cnt, agg[:, :, D + 1], 1.0, None, ALU.max))
            do(nc.vector.reciprocal(cnt, cnt))
            do(nc.vector.tensor_tensor(agg[:, :, 0:D], agg[:, :, 0:D], cnt.unsqueeze(2).to_broadcast([P, NT, D]), ALU.mult))
            nc.vector.tensor_tensor(x[:, :, :], x[:, :, :], agg[:, :, 0:D], ALU.add).then_inc(s_fin, 1)

        @block.scalar
        def _(act):
            act.preload_act_table_set("natural_log_exp_and_others")
            act.wait_ge(s_tab, 16)
            n = act.alloc_register("act_pairs")
            act.reg_mov(n, 0)

            def turned(k, p):
                act.wait_ge(s_tp, p + 1)
                nc.scalar.activation(hotT[:, k, :, :], tp[:, 0:2 * P].rearrange("p (u e) -> p u e", u=2),
                                     ACT.Copy).then_inc(s_hT, 1)

            def magnitude(k, p):
                act.wait_ge(s_add, p + 1 + 3)
                nc.scalar.activation(y[:, k, :, :], z[:, k, :, :], ACT.Abs).then_inc(s_abs, 1)

            def gates(k, p):
                act.wait_ge(s_ms, p + 1)
                nc.scalar.activation(y[:, k, :, 0:D], z[:, k, :, 0:D], ACT.Exp).then_inc(s_g, 1)

            def softplus(k, p):
                act.wait_ge(s_abs, p + 1)
                nc.scalar.activation(y[:, k, :, :], y[:, k, :, :], ACT.Exp, scale=-1.0).then_inc(s_e, 1)
                act.wait_ge(s_e, p + 1)
                nc.scalar.activation(y[:, k, :, :], y[:, k, :, :], ACT.Ln, bias=1.0).then_inc(s_l, 1)

            with act.Fori(0, NT) as j:
                t0, end = ranges(act, j)
                a = act.snap(n)
                for k in range(3):
                    turned(k, a + k)
                    if k >= 1:
                        magnitude(k - 1, a + (k - 1))
                    if k >= 2:
                        gates(k - 2, a + (k - 2))
                    if k >= 1:
                        softplus(k - 1, a + (k - 1))
                with act.Fori(t0 + ECH, end, ECH):
                    c = act.snap(n) + 3
                    for k in range(3):
                        turned(k, c + k)
                        magnitude((k + 2) % 3, c + (k - 1))
                        gates((k + 1) % 3, c + (k - 2))
                        softplus((k + 2) % 3, c + (k - 1))
                    act.reg_add(n, n, 3)
                b = act.snap(n) + 3
                magnitude(2, b - 1)
                gates(1, b - 2)
                softplus(2, b - 1)
                gates(2, b - 1)
                act.reg_add(n, n, 3)

        @block.tensor
        def _(pe):
            pe.sem_inc(s_add, 3)
            pe.sem_inc(s_att, 3)
            pe.sem_inc(s_seg, 3)
            pe.sem_inc(s_hT, 1)
            pe.sem_inc(s_hot, 1)
            pe.sem_inc(s_agg, 1)
            pe.wait_ge(s_c, 3)
            pe.wait_ge(s_w, 32)
            pe.wait_ge(s_tab, 16)
            n = pe.alloc_register("pe_pairs")
            pe.reg_mov(n, 0)
            loads = pe.alloc_register("pe_loads")
            pe.reg_mov(loads, 0)

            def sums(k, p, c, j):
                pe.wait_ge(s_hot, p + 2)
                pe.wait_ge(s_hT, p + 1)
                for u in range(2):
                    mm = pe.transpose(tp[:, u * P:(u + 1) * P], hot[:, k, u, :], ident[:, :])
                mm.then_inc(s_tp, 1)
                pe.wait_ge(s_add, p + 1)
                pe.wait_ge(s_at[k], c)
                for u in range(2):
                    mm = pe.matmul(zp[:, k, u * D2:(u + 1) * D2], at[:, k, u * P:(u + 1) * P], Wa[:, :],
                                   start=(u == 0), stop=False, skip_group_check=True)
                mm.then_inc(s_att, 1)
                pe.wait_ge(s_hT, p + 2)
                for u in range(2):
                    for part in range(3):
                        mm = pe.matmul(zp[:, k, u * D2:(u + 1) * D2], hotT[:, k, u, :],
                                       Q3[:, bass.ds(j, 1), part, :].rearrange("p o f -> p (o f)"),
                                       start=False, stop=(part == 2), skip_group_check=True)
                mm.then_inc(s_z, 1)

            def aggregate(k, p):
                pe.wait_ge(s_G, p + 1)
                for u in range(2):
                    mm = pe.matmul(acc[:, 0:D + 2], hot[:, k, u, :], G[:, k, u, :],
                                   start=False, stop=(u == 1), skip_group_check=True)
                mm.then_inc(s_seg, 1)

            with pe.Fori(0, NT) as j:
                t0, end = ranges(pe, j)
                pe.wait_ge(s_agg, j + 1)
                pe.matmul(acc[:, 0:D + 2], zero[:, :], zero[:, 0:D + 2], start=True, stop=False,
                          skip_group_check=True)
                a = pe.snap(n)
                pe.reg_add(loads, loads, 16)
                l0 = pe.snap(loads)
                for k in range(3):
                    sums(k, a + k, l0, j)
                    if k >= 2:
                        aggregate(k - 2, a + (k - 2))
                with pe.Fori(t0 + ECH, end, ECH):
                    c = pe.snap(n) + 3
                    pe.reg_add(loads, loads, 16)
                    lc = pe.snap(loads)
                    for k in range(3):
                        sums(k, c + k, lc, j)
                        aggregate((k + 1) % 3, c + (k - 2))
                    pe.reg_add(n, n, 3)
                b = pe.snap(n) + 3
                aggregate(1, b - 2)
                aggregate(2, b - 1)
                pe.reg_add(n, n, 3)


def residual_gcn(nc, x_in, C_d, layers, x_out_d):
    with ExitStack() as ctx:
        m = Scope(nc, ctx, "layer2")
        C = m.sb("C", [P, NT, NT, P], F16)
        x = m.sb("x", [P, NT, D], F32)
        h = m.sb("h", [P, NT, D], F32)
        cv = m.sb("cv", [P, NT, D], F32)
        U = m.sb("U", [P, NT, 3, D], BF16)
        ident = m.sb("ident", [P, P], F32)
        mask = m.sb("mask", [P, 2, P], F32)
        W = m.sb("W", [D, 2, D], F32)
        vec = m.sb("vec", [P, 2, 4, D], F32)
        stat = m.sb("stat", [P, 3, NT], F32)
        hT = m.sb("hT", [D, 2, P], F32)
        rest = m.sb("rest", [P, 2, D], F32)
        part = m.sb("part", [P, 2, D], F32)
        sq = U[:, :, :, :].rearrange("p k a f -> p (k a f)").bitcast(F32)[:, 0:NT * D].rearrange("p (k f) -> p k f", f=D)
        mu = m.sb("mu", [P, D], F32)
        sd = m.sb("sd", [P, D], F32)
        tp = m.ps("tp", [P, 2, 512])
        acc = m.ps("acc", [P, 4, 512])
        tot = m.ps("tot", [P, 2, 512])
        s_x = m.sem("x_loaded")
        s_par = m.sem("parameters_loaded")
        s_C = [m.sem(f"C_loaded{q}") for q in range(5)]
        s_c = m.sem("iotas_made")
        s_id = m.sem("identity_made")
        s_v = m.sem("dve_chain")
        s_a = m.sem("act_chain")
        s_var = m.sem("root_wanted")
        s_root = m.sem("root_made")
        s_h = m.sem("h_made")
        s_tp = m.sem("h_turned")
        s_hT = m.sem("turned_h_out")
        s_pr = m.sem("hW_done")
        s_u0 = m.sem("first_parts_made")
        s_r = m.sem("rests_made")
        s_u1 = m.sem("second_parts_made")
        s_u2 = m.sem("third_parts_made")
        s_acc = m.sem("aggregates_done")
        s_p2 = m.sem("third_sums_out")
        s_cv = m.sem("conv_tiles_made")
        s_sum = m.sem("column_sums_done")
        s_xc = m.sem("centred")
        s_sq = m.sem("squares_made")
        s_sqs = m.sem("squares_summed")
        s_st = m.sem("x_stored")
        s_fin = m.sem("x_updated")
        block = ctx.enter_context(nc.Block())
        NL = len(layers)

        @block.sync
        def _(sp):
            sp.dma_start(x[:, :, :], x_in.rearrange("(k p) f -> p k f", p=P)).then_inc(s_x, 16)
            for i, (w, b, gw, gb, ga) in enumerate(layers):
                sp.dma_start(W[:, i, :], w).then_inc(s_par, 16)
                for q, vct in enumerate((b, gw, gb, ga)):
                    sp.dma_start(vec[:, i, q, :], vct.rearrange("(o f) -> o f", o=1).to_broadcast([P, D])).then_inc(s_par, 16)
            for j in range(NT):
                sp.dma_start(C[:, j, :, :].rearrange("p k d -> p (k d)"), C_d[j, :, :]).then_inc(s_C[j // 5], 16)
            sp.wait_ge(s_fin, 1)
            sp.dma_start(x_out_d.rearrange("(k p) f -> p k f", p=P), x[:, :, :]).then_inc(s_st, 16)
            sp.wait_ge(s_st, 16)

        @block.gpsimd
        def _(pool):
            nc.gpsimd.iota(mask[:, 0, :], pattern=[[1, P]], base=0, channel_multiplier=0,
                           allow_small_or_imprecise_dtypes=True).then_inc(s_c, 1)
            nc.gpsimd.iota(mask[:, 1, :], pattern=[[0, P]], base=0, channel_multiplier=1,
                           allow_small_or_imprecise_dtypes=True).then_inc(s_c, 1)

        @block.vector
        def _(dve):
            do = Chain(dve, s_v)

            def root(n):
                def wait():
                    dve.sem_inc(s_var, 1)
                    dve.wait_ge(s_root, n)
                return wait

            dve.wait_ge(s_c, 2)
            do(nc.vector.tensor_tensor(ident[:, :], mask[:, 0, :], mask[:, 1, :], ALU.is_equal))
            do(nc.vector.memset(mask[:, 0, :], 1.0))
            nc.vector.tensor_scalar(mask[:, 1, :], mask[:, 1, :], float(LAST), None, ALU.is_lt).then_inc(s_id, 1)
            dve.wait_ge(s_x, 16)
            layernorm_relu(nc, do, root(1), x[:, :, :], h[:, :, :], stat, cv[:, :, :])
            dve.wait_ge(s_par, 16 * 5 * NL)
            for i in range(NL):
                base = i * NT
                dve.sem_inc(s_h, 1)
                for k in range(NT):
                    dve.wait_ge(s_u0, base + k + 1)
                    nc.vector.tensor_tensor(rest[:, k % 2, :], tp[:, k % 2, P:P + D], U[:, k, 0, :],
                                            ALU.subtract).then_inc(s_r, 1)
                    dve.wait_ge(s_u1, base + k + 1)
                    nc.vector.tensor_tensor(U[:, k, 2, :], rest[:, k % 2, :], U[:, k, 1, :],
                                            ALU.subtract).then_inc(s_u2, 1)
                for j in range(NT):
                    dve.wait_ge(s_p2, base + j + 1)
                    do(nc.vector.scalar_tensor_tensor(part[:, j % 2, :], acc[:, j % 4, D:2 * D], 2.0,
                                                      part[:, j % 2, :], ALU.mult, ALU.add))
                    do(nc.vector.scalar_tensor_tensor(part[:, j % 2, :], acc[:, j % 4, 0:D], 2.0,
                                                      part[:, j % 2, :], ALU.mult, ALU.add))
                    nc.vector.tensor_tensor(cv[:, j, :], part[:, j % 2, :], vec[:, i, 0, :], ALU.add).then_inc(s_cv, 1)
                dve.wait_ge(s_sum, i + 1)
                do(nc.vector.scalar_tensor_tensor(mu[:, :], tot[:, 0, 0:D], 1.0 / N, vec[:, i, 3, :], ALU.mult, ALU.mult))
                do(nc.vector.tensor_tensor(cv[:, :, :], cv[:, :, :], mu[:, :].unsqueeze(1).to_broadcast([P, NT, D]), ALU.subtract))
                dve.sem_inc(s_xc, 1)
                dve.wait_ge(s_sqs, (i + 1) * 5)
                do(nc.vector.tensor_scalar(mu[:, :], tot[:, 1, 0:D], 1.0 / N, LN_EPS, ALU.mult, ALU.add))
                root(2 + i)()
                do(nc.vector.reciprocal(sd[:, :], sd[:, :]))
                do(nc.vector.tensor_tensor(sd[:, :], sd[:, :], vec[:, i, 1, :], ALU.mult))
                do(nc.vector.tensor_tensor(cv[:, :, :], cv[:, :, :], sd[:, :].unsqueeze(1).to_broadcast([P, NT, D]), ALU.mult))
                do(nc.vector.tensor_tensor(cv[:, :, :], cv[:, :, :], vec[:, i, 2, :].unsqueeze(1).to_broadcast([P, NT, D]), ALU.add))
                do(nc.vector.scalar_tensor_tensor(h[:, :, :], cv[:, :, :], 0.0, h[:, :, :], ALU.max, ALU.add))
            nc.vector.tensor_tensor(x[:, :, :], x[:, :, :], h[:, :, :], ALU.add).then_inc(s_fin, 1)

        @block.scalar
        def _(act):
            act.wait_ge(s_var, 1)
            nc.scalar.sqrt(stat[:, 2, :], stat[:, 1, :]).then_inc(s_root, 1)
            for i in range(NL):
                base = i * NT
                for k in range(NT):
                    act.wait_ge(s_tp, base + k + 1)
                    nc.scalar.activation(hT[:, k % 2, :], tp[0:D, k % 2, 0:P], ACT.Copy).then_inc(s_hT, 1)
                    act.wait_ge(s_pr, base + k + 1)
                    nc.scalar.activation(U[:, k, 0, :], tp[:, k % 2, P:P + D], ACT.Copy).then_inc(s_u0, 1)
                    act.wait_ge(s_r, base + k + 1)
                    nc.scalar.activation(U[:, k, 1, :], rest[:, k % 2, :], ACT.Copy).then_inc(s_u1, 1)
                for j in range(NT):
                    act.wait_ge(s_acc, base + j + 1)
                    if base + j >= 2:
                        act.wait_ge(s_cv, base + j - 1)
                    nc.scalar.activation(part[:, j % 2, :], acc[:, j % 4, 2 * D:3 * D], ACT.Copy,
                                         scale=2.0).then_inc(s_p2, 1)
                act.wait_ge(s_xc, i + 1)
                for q in range(5):
                    nc.scalar.activation(sq[:, 5 * q:5 * q + 5, :], cv[:, 5 * q:5 * q + 5, :], ACT.Square).then_inc(s_sq, 1)
                act.wait_ge(s_var, 2 + i)
                nc.scalar.sqrt(sd[:, :], mu[:, :]).then_inc(s_root, 1)

        @block.tensor
        def _(pe):
            pe.wait_ge(s_id, 1)
            pe.wait_ge(s_par, 16 * 5 * NL)
            for i in range(NL):
                base = i * NT
                pe.wait_ge(s_h, i + 1)
                for k in range(NT):
                    if k >= 2:
                        pe.wait_ge(s_r, base + k - 1)
                    pe.transpose(tp[0:D, k % 2, 0:P], h[:, k, :], ident[:, :]).then_inc(s_tp, 1)
                    pe.wait_ge(s_hT, base + k + 1)
                    pe.matmul(tp[:, k % 2, P:P + D], hT[:, k % 2, :], W[:, i, :], start=True, stop=True).then_inc(s_pr, 1)
                for j in range(NT + 2):
                    if j < NT:
                        if base + j >= 4:
                            pe.wait_ge(s_cv, base + j - 3)
                        if i == 0 and j % 5 == 0:
                            pe.wait_ge(s_C[j // 5], 5 * 16)
                        for k in range(NT):
                            if j == 0:
                                pe.wait_ge(s_u2, base + k + 1)
                            mm = pe.matmul(acc[:, j % 4, 0:3 * D], C[:, j, k, :],
                                           U[:, k, :, :].rearrange("p a f -> p (a f)"),
                                           start=(k == 0), stop=(k == NT - 1))
                        mm.then_inc(s_acc, 1)
                    if j >= 2:
                        t = j - 2
                        pe.wait_ge(s_cv, base + t + 1)
                        mm = pe.matmul(tot[:, 0, 0:D], mask[:, int(t == NT - 1), :], cv[:, t, :],
                                       start=(t == 0), stop=(t == NT - 1))
                mm.then_inc(s_sum, 1)
                for q in range(5):
                    pe.wait_ge(s_sq, i * 5 + q + 1)
                    for u in range(5):
                        t = 5 * q + u
                        mm = pe.matmul(tot[:, 1, 0:D], mask[:, int(t == NT - 1), :], sq[:, t, :],
                                       start=(t == 0), stop=(t == NT - 1))
                    mm.then_inc(s_sqs, 1)


def stream_plan(orders, slots):
    holder, last, uses, loads = [None] * slots, [None] * slots, [], []
    for u, j in enumerate(j for order in orders for j in order):
        hit = j in holder
        if not hit:
            s = holder.index(None) if None in holder else min(range(slots), key=lambda q: last[q])
            loads.append((j, s, last[s]))
            holder[s] = j
        s = holder.index(j)
        last[s] = u
        uses.append((j, s, not hit))
    return uses, loads


def weighted_gcn(nc, x_in, W_d, wdeg, layers, out):
    RW = 12
    orders = (list(range(NT)), list(range(NT))[::-1])
    uses, loads = stream_plan(orders, RW)
    with ExitStack() as ctx:
        m = Scope(nc, ctx, "layer3")
        ring = m.sb("ring", [P, RW, NT, P], F32)
        x = m.sb("x", [P, NT, D], F32)
        h = m.sb("h", [P, NT, D], F32)
        V = m.sb("V", [P, NT, D], F32)
        ident = m.sb("ident", [P, P], F32)
        colno = m.sb("colno", [P, P], F32)
        W = m.sb("W", [D, 2, D], F32)
        bias = m.sb("bias", [P, 2, D], F32)
        stat = m.sb("stat", [P, 3, NT], F32)
        dinv = m.sb("dinv", [P, NT], F32)
        pos = m.sb("pos", [P, NT], F32)
        hT = m.sb("hT", [D, 2, P], F32)
        part = m.sb("part", [P, 2, D], F32)
        tp = m.ps("tp", [P, 2, 512])
        acc = m.ps("acc", [P, 4, 512])
        s_x = m.sem("x_loaded")
        s_par = m.sem("parameters_loaded")
        s_W = [m.sem(f"W_slot{s}_loaded") for s in range(RW)]
        s_c = m.sem("iotas_made")
        s_v = m.sem("dve_chain")
        s_var = m.sem("root_wanted")
        s_root = m.sem("root_made")
        s_h = m.sem("h_made")
        s_tp = m.sem("h_turned")
        s_hT = m.sem("turned_h_out")
        s_pr = m.sem("hV_done")
        s_V = m.sem("scaled_made")
        s_acc = m.sem("aggregates_done")
        s_o = m.sem("conv_tiles_made")
        s_exp = m.sem("exponentials_wanted")
        s_e = m.sem("exponentials_made")
        s_st = m.sem("out_stored")
        s_fin = m.sem("out_made")
        block = ctx.enter_context(nc.Block())
        NL = len(layers)

        @block.sync
        def _(sp):
            sp.dma_start(x[:, :, :], x_in.rearrange("(k p) f -> p k f", p=P)).then_inc(s_x, 16)
            for i, (w, b) in enumerate(layers):
                sp.dma_start(W[:, i, :], w).then_inc(s_par, 16)
                sp.dma_start(bias[:, i, :], b.rearrange("(o f) -> o f", o=1).to_broadcast([P, D])).then_inc(s_par, 16)
            for j, s, freed in loads:
                if freed is not None:
                    sp.wait_ge(s_acc, freed + 1)
                sp.dma_start(ring[:, s, :, :].rearrange("p k d -> p (k d)"), W_d[j, :, :]).then_inc(s_W[s], 16)
            sp.wait_ge(s_fin, 1)
            sp.dma_start(out.rearrange("(k p) f -> p k f", p=P), x[:, :, :]).then_inc(s_st, 16)
            sp.wait_ge(s_st, 16)

        @block.gpsimd
        def _(pool):
            nc.gpsimd.iota(colno[:, :], pattern=[[1, P]], base=0, channel_multiplier=0,
                           allow_small_or_imprecise_dtypes=True).then_inc(s_c, 1)
            nc.gpsimd.iota(ident[:, :], pattern=[[0, P]], base=0, channel_multiplier=1,
                           allow_small_or_imprecise_dtypes=True).then_inc(s_c, 1)

        @block.vector
        def _(dve):
            do = Chain(dve, s_v)

            def root(n):
                def wait():
                    dve.sem_inc(s_var, 1)
                    dve.wait_ge(s_root, n)
                return wait

            dve.wait_ge(s_c, 2)
            do(nc.vector.tensor_tensor(ident[:, :], ident[:, :], colno[:, :], ALU.is_equal))
            do(nc.vector.tensor_scalar(dinv[:, :], wdeg[:, :], 1.0, None, ALU.add))
            do(nc.vector.tensor_scalar(pos[:, :], dinv[:, :], 0.0, None, ALU.is_gt))
            do(nc.vector.tensor_scalar(dinv[:, :], dinv[:, :], 1e-30, None, ALU.max))
            root(1)()
            do(nc.vector.reciprocal(dinv[:, :], dinv[:, :]))
            do(nc.vector.tensor_tensor(dinv[:, :], dinv[:, :], pos[:, :], ALU.mult))
            dve.wait_ge(s_x, 16)
            layernorm_relu(nc, do, root(2), x[:, :, :], h[:, :, :], stat, V[:, :, :])
            dve.wait_ge(s_par, 16 * 2 * NL)
            for i in range(NL):
                base = i * NT
                dve.sem_inc(s_h, 1)
                for k in range(NT):
                    dve.wait_ge(s_pr, base + k + 1)
                    nc.vector.tensor_scalar(V[:, k, :], tp[:, k % 2, P:P + D], dinv[:, k:k + 1], None,
                                            ALU.mult).then_inc(s_V, 1)
                for n, j in enumerate(orders[i]):
                    dve.wait_ge(s_acc, base + n + 1)
                    if n == 0:
                        dve.wait_ge(s_V, base + NT)
                    do(nc.vector.tensor_tensor(part[:, n % 2, :], acc[:, n % 4, 0:D], V[:, j, :], ALU.add))
                    nc.vector.scalar_tensor_tensor(h[:, j, :], part[:, n % 2, :], dinv[:, j:j + 1], bias[:, i, :],
                                                   ALU.mult, ALU.add).then_inc(s_o, 1)
                dve.wait_ge(s_o, base + NT)
                if i == 0:
                    do(nc.vector.tensor_scalar(h[:, :, :], h[:, :, :], 0.0, None, ALU.max))
            top, tot = stat[:, 0, :], stat[:, 1, :]
            do(nc.vector.tensor_reduce(top, h[:, :, :], AX.X, ALU.max))
            do(nc.vector.tensor_tensor(h[:, :, :], h[:, :, :], top.unsqueeze(2).to_broadcast([P, NT, D]), ALU.subtract))
            dve.sem_inc(s_exp, 1)
            do(nc.vector.tensor_tensor(x[:, :, :], x[:, :, :], h[:, :, :], ALU.add))
            dve.wait_ge(s_e, 1)
            do(nc.vector.tensor_reduce(tot, V[:, :, :], AX.X, ALU.add))
            dve.sem_inc(s_exp, 1)
            dve.wait_ge(s_e, 2)
            nc.vector.tensor_tensor(x[:, :, :], x[:, :, :], stat[:, 2, :].unsqueeze(2).to_broadcast([P, NT, D]),
                                    ALU.subtract).then_inc(s_fin, 1)

        @block.scalar
        def _(act):
            act.wait_ge(s_var, 1)
            nc.scalar.sqrt(dinv[:, :], dinv[:, :]).then_inc(s_root, 1)
            act.wait_ge(s_var, 2)
            nc.scalar.sqrt(stat[:, 2, :], stat[:, 1, :]).then_inc(s_root, 1)
            for i in range(NL):
                for k in range(NT):
                    act.wait_ge(s_tp, i * NT + k + 1)
                    nc.scalar.activation(hT[:, k % 2, :], tp[0:D, k % 2, 0:P], ACT.Copy).then_inc(s_hT, 1)
            act.wait_ge(s_exp, 1)
            nc.scalar.activation(V[:, :, :], h[:, :, :], ACT.Exp).then_inc(s_e, 1)
            act.wait_ge(s_exp, 2)
            nc.scalar.activation(stat[:, 2, :], stat[:, 1, :], ACT.Ln).then_inc(s_e, 1)

        @block.tensor
        def _(pe):
            pe.wait_ge(s_par, 16 * 2 * NL)
            seen = {}
            for i in range(NL):
                base = i * NT
                pe.wait_ge(s_h, i + 1)
                for k in range(NT):
                    if k >= 2:
                        pe.wait_ge(s_V, base + k - 1)
                    pe.transpose(tp[0:D, k % 2, 0:P], h[:, k, :], ident[:, :]).then_inc(s_tp, 1)
                    pe.wait_ge(s_hT, base + k + 1)
                    pe.matmul(tp[:, k % 2, P:P + D], hT[:, k % 2, :], W[:, i, :], start=True, stop=True).then_inc(s_pr, 1)
                for n in range(NT):
                    j, s, load = uses[base + n]
                    if base + n >= 4:
                        pe.wait_ge(s_o, base + n - 3)
                    if load:
                        seen[s] = seen.get(s, 0) + 16
                        pe.wait_ge(s_W[s], seen[s])
                    for k in range(NT):
                        if n == 0:
                            pe.wait_ge(s_V, base + k + 1)
                        mm = pe.matmul(acc[:, n % 4, 0:D], ring[:, s, k, :], V[:, k, :],
                                       start=(k == 0), stop=(k == NT - 1))
                    mm.then_inc(s_acc, 1)


def gnn(nc, x, src_cols, dst_cols, dst_rows, attr, w_cols, We, be, Wn, bn, W1, b1, W2, b2,
        g1w, g1b, g1a, g2w, g2b, g2a, V1, c1, V2, c2, out):
    tab_d = nc.dram_tensor("range_table", [QG * P, 2], I32, kind="Internal").ap()
    C_d = nc.dram_tensor("C_blocks", [NT, P, NP], F16, kind="Internal").ap()
    W_d = nc.dram_tensor("W_blocks", [NT, P, NP], F32, kind="Internal").ap()
    P_d = nc.dram_tensor("source_terms", [NP, 2 * D], F32, kind="Internal").ap()
    x1_d, x2_d, x3_d = (nc.dram_tensor(f"x_after_{i}", [NP, D], F32, kind="Internal").ap() for i in range(3))
    with ExitStack() as outer:
        o = Scope(nc, outer, "all6")
        indeg = o.sb("indeg", [P, NT * 5], F32)
        CT = o.sb("CT", [P, NT, NP], F16)
        with ExitStack() as ctx:
            m = Scope(nc, ctx, "all7")
            key = m.sb("key", [P, ETC], F32)
            smod = m.sb("smod", [P, ETC], F16)
            wpart = m.sb("wpart", [P, 3, ETC], BF16)
            edge_ranges(nc, src_cols, dst_cols, dst_rows, w_cols, tab_d, key, smod, wpart)
            build_matrices(nc, tab_d, key, smod, wpart, CT, indeg, C_d, W_d)
        propagate(nc, x, CT, indeg, x1_d)
    with ExitStack() as outer:
        o = Scope(nc, outer, "all8")
        wdeg = o.sb("wdeg", [P, NT], F32)
        gated_edges(nc, x1_d, src_cols, dst_cols, w_cols, attr, We, be, Wn, bn, tab_d, P_d, x2_d, wdeg)
        residual_gcn(nc, x2_d, C_d, ((W1, b1, g1w, g1b, g1a), (W2, b2, g2w, g2b, g2a)), x3_d)
        weighted_gcn(nc, x3_d, W_d, wdeg, ((V1, c1), (V2, c2)), out)


def kernel(x, src, dst, edge_attr_64, edge_weight, L1_gnn_W_e, L1_gnn_b_e, L1_gnn_W_n, L1_gnn_b_n,
           L2_gnn_W1, L2_gnn_b1, L2_gnn_W2, L2_gnn_b2, L2_gnn_gn1_w, L2_gnn_gn1_b, L2_gnn_gn1_a,
           L2_gnn_gn2_w, L2_gnn_gn2_b, L2_gnn_gn2_a, L3_gnn_W1, L3_gnn_b1, L3_gnn_W2, L3_gnn_b2):
    import numpy as np
    import concourse.bacc as bacc
    from concourse.bass_utils import run_bass_kernel_spmd

    def padded(a, n, value=0):
        a = np.asarray(a)
        out = np.full((n,) + a.shape[1:], value, a.dtype)
        out[:len(a)] = a
        return out

    def columns(a):
        return np.ascontiguousarray(a.reshape(ET, P)[:ETC].T)

    dst_p = padded(dst, ET * P, NO_NODE)
    arrays = {
        "x": padded(x, NP),
        "src_cols": columns(padded(src, ET * P)),
        "dst_cols": columns(dst_p),
        "dst_rows": dst_p.reshape(ET, P),
        "attr": np.ascontiguousarray(padded(edge_attr_64, ET * P).T),
        "w_cols": columns(padded(edge_weight, ET * P)),
        "We": L1_gnn_W_e, "be": L1_gnn_b_e, "Wn": L1_gnn_W_n, "bn": L1_gnn_b_n,
        "W1": L2_gnn_W1, "b1": L2_gnn_b1, "W2": L2_gnn_W2, "b2": L2_gnn_b2,
        "g1w": L2_gnn_gn1_w, "g1b": L2_gnn_gn1_b, "g1a": L2_gnn_gn1_a,
        "g2w": L2_gnn_gn2_w, "g2b": L2_gnn_gn2_b, "g2a": L2_gnn_gn2_a,
        "V1": L3_gnn_W1, "c1": L3_gnn_b1, "V2": L3_gnn_W2, "c2": L3_gnn_b2,
    }
    nc = bacc.Bacc("TRN2", target_bir_lowering=False, num_devices=1)
    args = {}
    for name, a in arrays.items():
        a = arrays[name] = np.ascontiguousarray(a)
        args[name] = nc.dram_tensor(f"in_{name}", a.shape, mybir.dt.from_np(a.dtype), kind="ExternalInput").ap()
    out = nc.dram_tensor("out", (NP, D), F32, kind="ExternalOutput").ap()
    gnn(nc, out=out, **args)
    r = run_bass_kernel_spmd(nc, [{f"in_{name}": a for name, a in arrays.items()}], core_ids=[0])
    return r.results[0]["out"][:N]
```

```python
from contextlib import ExitStack

import concourse.bass as bass
from concourse import mybir

F32, F16, BF16 = mybir.dt.float32, mybir.dt.float16, mybir.dt.bfloat16
I32, I16 = mybir.dt.int32, mybir.dt.int16
ALU = mybir.AluOpType
ACT = mybir.ActivationFunctionType
AX = mybir.AxisListType

P = 128
N, D, E, DE = 3125, 96, 103125, 64
NT = -(-N // P)
NP = NT * P
LAST = N - (NT - 1) * P
ET = 896
EG = ET // P
WIN = 8
NW = NP // WIN
WPT = P // WIN
WC = WIN * NT
CH = 4
SE = 6
NO_NODE = 4000
QG = 5
TCLAMP = -(-E // P)
ETC = TCLAMP + 16
K_STEPS, ALPHA, BETA = 10, 0.1, 0.9
THETA = BETA ** K_STEPS + ALPHA * sum(BETA ** i for i in range(K_STEPS))
LN_EPS = 1e-5
USCALE = 64.0
RING = 5
EVAC0 = 7
LOSCALE = 2048.0


class Scope:

    def __init__(self, nc, ctx, stage):
        self.nc, self.ctx, self.stage = nc, ctx, stage

    def sb(self, name, shape, dt):
        return self.ctx.enter_context(self.nc.sbuf_tensor(f"{self.stage}_{name}", shape, dt))

    def ps(self, name, shape, dt=F32):
        return self.ctx.enter_context(self.nc.psum_tensor(f"{self.stage}_{name}", shape, dt))

    def sem(self, name):
        return self.ctx.enter_context(self.nc.semaphore(f"{self.stage}_{name}"))


class Chain:

    def __init__(self, eng, sem):
        self.eng, self.sem, self.n = eng, sem, 0

    def __call__(self, ins):
        self.n += 1
        ins.then_inc(self.sem, 1)
        self.eng.wait_ge(self.sem, self.n)


def edge_ranges(nc, src_cols, dst_cols, dst_rows, w_cols, tab_d, row_d, key, smod, wpart):
    with ExitStack() as ctx:
        m = Scope(nc, ctx, "ranges")
        srcI = m.sb("srcI", [P, ETC], I32)
        dstI = m.sb("dstI", [P, ETC], I32)
        rowsI = m.sb("rowsI", [P, EG, P], I32)
        rows16 = m.sb("rows16", [P, EG, P], I16)
        weight = m.sb("weight", [P, ETC], F32)
        least = m.sb("least", [P, EG], F32)
        most = m.sb("most", [P, EG], F32)
        rowno = m.sb("rowno", [P, P], F32)
        colno = m.sb("colno", [P, P], F32)
        ident = m.sb("ident", [P, P], F32)
        ones = m.sb("ones", [P, P], F32)
        spread = m.sb("spread", [P, 2, EG, P], F32)
        up = m.sb("up", [P, ET], F32)
        down = m.sb("down", [P, ET], F32)
        low = m.sb("low", [P, QG], F32)
        high = m.sb("high", [P, QG], F32)
        below = m.sb("below", [P, ET], F32)
        touch = m.sb("touch", [P, ET], F32)
        tileI = rowsI[:, :, :].rearrange("p c e -> p (c e)")[:, 0:ETC]
        left = spread[:, 0, :, :].rearrange("p c e -> p (c e)")[:, 0:ETC]
        r1 = m.sb("r1", [P, QG], F32)
        r2 = m.sb("r2", [P, QG], F32)
        bounds = m.sb("bounds", [P, QG, 2], F32)
        boundsI = m.sb("boundsI", [P, QG, 2], I16)
        bc = m.ps("bc", [P, 4, 512])
        s_in = [m.sem(f"edges_loaded{i}") for i in range(4)]
        s_iota = m.sem("iotas_made")
        s_diag = m.sem("diagonals_made")
        s_bc = m.sem("bounds_broadcast")
        s_r16 = m.sem("small_targets_made")
        s_bounds = m.sem("bounds_made")
        s_tab = m.sem("bounds_stored")
        s_v = m.sem("ranges_dve_chain")
        block = ctx.enter_context(nc.Block())

        @block.sync
        def _(sp):
            sp.dma_start(rowsI[:, :, :], dst_rows.rearrange("(c p) e -> p c e", p=P)).then_inc(s_in[0], 16)
            sp.dma_start(srcI[:, :], src_cols).then_inc(s_in[1], 16)
            sp.dma_start(dstI[:, :], dst_cols).then_inc(s_in[2], 16)
            sp.dma_start(weight[:, :], w_cols).then_inc(s_in[3], 16)
            sp.wait_ge(s_r16, 1)
            sp.dma_start(row_d.rearrange("o (c p e) -> p (o c) e", p=P, e=P), rows16[:, :, :]).then_inc(s_tab, 16)
            sp.wait_ge(s_bounds, 1)
            sp.dma_start(tab_d.rearrange("(q p) b -> p q b", p=P), boundsI[:, :, :]).then_inc(s_tab, 16)
            sp.wait_ge(s_tab, 32)

        @block.gpsimd
        def _(pool):
            nc.gpsimd.iota(colno[:, :], pattern=[[1, P]], base=0, channel_multiplier=0,
                           allow_small_or_imprecise_dtypes=True).then_inc(s_iota, 1)
            nc.gpsimd.iota(rowno[:, :], pattern=[[0, P]], base=0, channel_multiplier=1,
                           allow_small_or_imprecise_dtypes=True).then_inc(s_iota, 1)
            nc.gpsimd.iota(up[:, :], pattern=[[1, ET]], base=1, channel_multiplier=0,
                           allow_small_or_imprecise_dtypes=True).then_inc(s_iota, 1)
            nc.gpsimd.iota(down[:, :], pattern=[[-1, ET]], base=ET, channel_multiplier=0,
                           allow_small_or_imprecise_dtypes=True).then_inc(s_iota, 1)
            nc.gpsimd.iota(low[:, 0:QG - 1], pattern=[[WIN * P, QG - 1]], base=0, channel_multiplier=WIN,
                           allow_small_or_imprecise_dtypes=True).then_inc(s_iota, 1)
            nc.gpsimd.iota(high[:, 0:QG - 1], pattern=[[WIN * P, QG - 1]], base=WIN, channel_multiplier=WIN,
                           allow_small_or_imprecise_dtypes=True).then_inc(s_iota, 1)
            nc.gpsimd.iota(low[:, QG - 1:QG], pattern=[[0, 1]], base=0, channel_multiplier=P,
                           allow_small_or_imprecise_dtypes=True).then_inc(s_iota, 1)
            nc.gpsimd.iota(high[:, QG - 1:QG], pattern=[[0, 1]], base=P, channel_multiplier=P,
                           allow_small_or_imprecise_dtypes=True).then_inc(s_iota, 1)

        @block.tensor
        def _(pe):
            for b in range(2):
                pe.wait_ge(s_diag, b + 1)
                flat = spread[:, b, :, :].rearrange("p c e -> p (c e)")
                for h in range(2):
                    pe.matmul(bc[:, 2 * b + h, 0:ET // 2], ones[:, :], flat[:, h * ET // 2:(h + 1) * ET // 2],
                              start=True, stop=True).then_inc(s_bc, 1)

        @block.vector
        def _(dve):
            do = Chain(dve, s_v)
            dve.wait_ge(s_iota, 8)
            do(nc.vector.tensor_tensor(ident[:, :], rowno[:, :], colno[:, :], ALU.is_equal))
            do(nc.vector.memset(ones[:, :], 1.0))
            dve.wait_ge(s_in[0], 16)
            do(nc.vector.tensor_reduce(least[:, :], rowsI[:, :, :], AX.X, ALU.min))
            nc.vector.tensor_tensor(spread[:, 0, :, :], ident[:, :].unsqueeze(1).to_broadcast([P, EG, P]),
                                    least[:, :].unsqueeze(2).to_broadcast([P, EG, P]), ALU.mult).then_inc(s_diag, 1)
            do(nc.vector.tensor_reduce(most[:, :], rowsI[:, :, :], AX.X, ALU.max))
            nc.vector.tensor_tensor(spread[:, 1, :, :], ident[:, :].unsqueeze(1).to_broadcast([P, EG, P]),
                                    most[:, :].unsqueeze(2).to_broadcast([P, EG, P]), ALU.mult).then_inc(s_diag, 1)
            do(nc.vector.tensor_copy(rows16[:, :, :], rowsI[:, :, :]))
            dve.sem_inc(s_r16, 1)
            dve.wait_ge(s_bc, 4)
            for q in range(QG):
                for h in range(2):
                    cols = slice(h * ET // 2, (h + 1) * ET // 2)
                    do(nc.vector.tensor_scalar(below[:, cols], bc[:, h, 0:ET // 2], high[:, q:q + 1], None,
                                               ALU.is_lt))
                    do(nc.vector.scalar_tensor_tensor(touch[:, cols], bc[:, 2 + h, 0:ET // 2], low[:, q:q + 1],
                                                      below[:, cols], ALU.is_ge, ALU.mult))
                do(nc.vector.tensor_tensor(below[:, :], touch[:, :], down[:, :], ALU.mult))
                do(nc.vector.tensor_reduce(r1[:, q:q + 1], below[:, :], AX.X, ALU.max))
                do(nc.vector.tensor_tensor(touch[:, :], touch[:, :], up[:, :], ALU.mult))
                do(nc.vector.tensor_reduce(r2[:, q:q + 1], touch[:, :], AX.X, ALU.max))
            do(nc.vector.tensor_scalar(bounds[:, :, 0], r1[:, :], -1.0, float(ET), ALU.mult, ALU.add))
            do(nc.vector.tensor_scalar(bounds[:, :, 0], bounds[:, :, 0], float(TCLAMP), None, ALU.min))
            do(nc.vector.scalar_tensor_tensor(bounds[:, :, 1], bounds[:, :, 0], 1.0, r2[:, :], ALU.add, ALU.max))
            nc.vector.tensor_copy(boundsI[:, :, :], bounds[:, :, :]).then_inc(s_bounds, 1)
            dve.wait_ge(s_in[1], 16)
            dve.wait_ge(s_in[2], 16)
            do(nc.vector.tensor_scalar(tileI, srcI[:, :], 7, None, ALU.logical_shift_right))
            do(nc.vector.tensor_scalar(srcI[:, :], srcI[:, :], P - 1, None, ALU.bitwise_and))
            do(nc.vector.scalar_tensor_tensor(key[:, :], dstI[:, :], float(NT), tileI, ALU.mult, ALU.add))
            do(nc.vector.tensor_copy(smod[:, :], srcI[:, :]))
            dve.wait_ge(s_in[3], 16)
            do(nc.vector.tensor_copy(wpart[:, 0, :], weight[:, :]))
            do(nc.vector.tensor_tensor(left, weight[:, :], wpart[:, 0, :], ALU.subtract))
            do(nc.vector.tensor_copy(wpart[:, 1, :], left))
            do(nc.vector.tensor_tensor(left, left, wpart[:, 1, :], ALU.subtract))
            do(nc.vector.tensor_copy(wpart[:, 2, :], left))


def build_matrices(nc, tab_d, key, smod, wpart, CT, indeg, C_d, W_d):
    with ExitStack() as ctx:
        m = Scope(nc, ctx, "build")
        tab = m.sb("tab", [1, NW, 2], I16)
        colsM = m.sb("colsM", [P, WC, CH], F16)
        colsS = m.sb("colsS", [P, P, CH], F16)
        wbase = m.sb("wbase", [P, NW], F32)
        ident = m.sb("ident16", [P, P], F16)
        kw = m.sb("kw", [P, 3, CH], F16)
        M = m.sb("M", [P, 3, WC, CH], BF16)
        S = m.sb("S", [P, 3, 4, P, CH], BF16)
        Cblk = m.sb("Cblk", [P, NT, P], F16)
        Wblk = m.sb("Wblk", [P, NT, P], F32)
        rowh = Cblk[:, 0, :]
        win = m.ps("win", [P, 4, 512])
        tp = m.ps("tp", [P, 2, 8, P], F16)
        s_const = m.sem("constants_made")
        s_tab = m.sem("table_loaded")
        s_key = m.sem("window_keys")
        s_hot = m.sem("source_onehots")
        s_made = m.sem("operands_made")
        s_built = m.sem("window_built")
        s_evac = m.sem("window_out")
        s_xkey = m.sem("more_keys")
        s_xhot = m.sem("more_source_onehots")
        s_xmade = m.sem("more_operands_made")
        s_xused = m.sem("more_operands_used")
        s_tp = m.sem("tile_transposed")
        s_ct = m.sem("transposed_out")
        s_cst = m.sem("C_stored")
        s_wst = m.sem("W_stored")
        block = ctx.enter_context(nc.Block())

        def window_ranges(eng, regs, w0):
            eng.load(regs, tab[0:1, bass.ds(w0, 4), :])
            why = "edge_ranges clamps the tables"
            return [(nc.s_assert_within(eng.snap(regs[2 * b]), 0, TCLAMP, skip_runtime_bounds_check_because=why),
                     nc.s_assert_within(eng.snap(regs[2 * b + 1]), 1, TCLAMP + 1,
                                        skip_runtime_bounds_check_because=why)) for b in range(4)]

        @block.gpsimd
        def _(pool):
            small = dict(allow_small_or_imprecise_dtypes=True)
            for k in range(NT):
                nc.gpsimd.iota(colsM[:, k * WIN:(k + 1) * WIN, :], pattern=[[NT, WIN], [0, CH]], base=k,
                               channel_multiplier=0, **small).then_inc(s_const, 1)
            nc.gpsimd.iota(colsS[:, :, :], pattern=[[1, P], [0, CH]], base=0, channel_multiplier=0,
                           **small).then_inc(s_const, 1)
            nc.gpsimd.iota(wbase[:, :], pattern=[[WC, NW]], base=0, channel_multiplier=0,
                           **small).then_inc(s_const, 1)
            nc.gpsimd.iota(rowh, pattern=[[0, P]], base=0, channel_multiplier=1,
                           **small).then_inc(s_const, 1)

        @block.sync
        def _(sp):
            sp.dma_start(tab[:, :, :], tab_d[0:NW, :].rearrange("(o q) b -> o q b", o=1)).then_inc(s_tab, 16)
            with sp.Fori(0, NT) as j:
                sp.wait_ge(s_evac, j * (2 * WPT) + 2 * WPT + EVAC0)
                sp.dma_start(C_d[bass.ds(j, 1), :, :].rearrange("o p c -> p (o c)"),
                             Cblk[:, :, :].rearrange("p k d -> p (k d)")).then_inc(s_cst, 16)
                sp.dma_start(W_d[bass.ds(j, 1), :, :].rearrange("o p c -> p (o c)"),
                             Wblk[:, :, :].rearrange("p k d -> p (k d)")).then_inc(s_wst, 16)
            sp.wait_ge(s_cst, 16 * NT + 1)
            sp.wait_ge(s_wst, 16 * NT + 1)

        @block.vector
        def _(dve):
            dve.wait_ge(s_const, NT + 3)
            nc.vector.tensor_tensor(ident[:, :], rowh, colsS[:, :, 0], ALU.is_equal).then_inc(s_const, 1)
            dve.wait_ge(s_tab, 16)

            def operands(slot, w, t, keys, hots, made, n):
                nc.vector.tensor_scalar(kw[:, slot, :], key[:, bass.ds(t, CH)], wbase[:, bass.ds(w, 1)], 1000.0,
                                        ALU.subtract, ALU.min).then_inc(keys, 1)
                nc.vector.tensor_tensor(S[:, slot, 0, :, :], colsS[:, :, :],
                                        smod[:, bass.ds(t, CH)].unsqueeze(1).to_broadcast([P, P, CH]),
                                        ALU.is_equal).then_inc(hots, 1)
                dve.wait_ge(keys, n)
                nc.vector.tensor_tensor(M[:, slot, :, :], colsM[:, :, :],
                                        kw[:, slot, :].unsqueeze(1).to_broadcast([P, WC, CH]), ALU.is_equal)
                dve.wait_ge(hots, n)
                nc.vector.tensor_tensor(
                    S[:, slot, 1:4, :, :], S[:, slot, 0, :, :].unsqueeze(1).to_broadcast([P, 3, P, CH]),
                    wpart[:, :, bass.ds(t, CH)].unsqueeze(2).to_broadcast([P, 3, P, CH]),
                    ALU.mult).then_inc(made, 1)

            regs = [dve.alloc_register(f"dve_bound{r}") for r in range(8)]
            more = dve.alloc_register("dve_more")
            dve.reg_mov(more, 0)
            with dve.Fori(0, NW // 4) as i:
                w0 = i * 4
                bounds = window_ranges(dve, regs, w0)
                for b in range(4):
                    t, end = bounds[b]
                    dve.wait_ge(s_built, w0 + b + 1)
                    operands(b % 2, w0 + b, t, s_key, s_hot, s_made, w0 + b + 1)
                    with dve.If(end > t + CH):
                        with dve.Fori(t + CH, end, CH) as tx:
                            dve.wait_ge(s_xused, dve.snap(more) + 1)
                            dve.reg_add(more, more, 1)
                            operands(2, w0 + b, tx, s_xkey, s_xhot, s_xmade, dve.snap(more))

        @block.tensor
        def _(pe):
            pe.sem_inc(s_built, 2)
            pe.sem_inc(s_xused, 1)
            pe.sem_inc(s_evac, EVAC0)
            pe.sem_inc(s_ct, 2)
            pe.sem_inc(s_cst, 1)
            pe.sem_inc(s_wst, 1)
            pe.wait_ge(s_tab, 16)
            pe.wait_ge(s_const, NT + 4)

            def products(slot, bank, tiles, first):
                for u in tiles:
                    for part in range(4):
                        out = win[:, bank, 0:WC] if part == 0 else win[:, bank, WC:2 * WC]
                        mm = pe.matmul(out, S[:, slot, part, :, u], M[:, slot, :, u],
                                       start=(first and u == 0 and part == 0),
                                       stop=(u == CH - 1 and part in (0, 3)), skip_group_check=True)
                return mm

            regs = [pe.alloc_register(f"pe_bound{r}") for r in range(8)]
            more = pe.alloc_register("pe_more")
            pe.reg_mov(more, 0)
            with pe.Fori(0, NT) as j:
                with pe.Fori(0, WPT // 4) as q:
                    w0 = j * WPT + q * 4
                    bounds = window_ranges(pe, regs, w0)
                    for b in range(4):
                        t, end = bounds[b]
                        pe.wait_ge(s_evac, 2 * w0 + 2 * b + 1)
                        pe.wait_ge(s_made, w0 + b + 1)
                        products(b % 2, b, range(CH - 1), True)
                        with pe.If(end > t + CH):
                            with pe.Fori(t + CH, end, CH):
                                pe.reg_add(more, more, 1)
                                pe.wait_ge(s_xmade, pe.snap(more))
                                products(2, b, range(CH), False).then_inc(s_xused, 1)
                        products(b % 2, b, range(CH - 1, CH), False).then_inc(s_built, 1)
                pe.wait_ge(s_evac, j * (2 * WPT) + 2 * WPT + EVAC0)
                for g in range(5):
                    pe.wait_ge(s_ct, j * 5 + g + 1)
                    for k in range(5):
                        mm = pe.transpose(tp[:, g % 2, k, :], Cblk[:, 5 * g + k, :], ident[:, :])
                    mm.then_inc(s_tp, 1)

        @block.scalar
        def _(act):
            act.preload_act_table(ACT.Copy)
            with act.Fori(0, NT) as j:
                act.wait_ge(s_cst, j * 16 + 1)
                act.wait_ge(s_wst, j * 16 + 1)
                with act.Fori(0, WPT // 4) as q:
                    w0 = j * WPT + q * 4
                    for b in range(4):
                        at = q * (4 * WIN) + b * WIN
                        act.wait_ge(s_built, w0 + b + 3)
                        nc.scalar.activation(Cblk[:, :, bass.ds(at, WIN)],
                                             win[:, b, 0:WC].rearrange("p (k d) -> p k d", d=WIN),
                                             ACT.Copy, scale=0.5).then_inc(s_evac, 1)
                        nc.scalar.activation(Wblk[:, :, bass.ds(at, WIN)],
                                             win[:, b, WC:2 * WC].rearrange("p (k d) -> p k d", d=WIN),
                                             ACT.Copy).then_inc(s_evac, 1)
                for g in range(5):
                    act.wait_ge(s_tp, j * 5 + g + 1)
                    nc.scalar.activation(CT[:, bass.ds(j, 1), g * 5 * P:(g + 1) * 5 * P],
                                         tp[:, g % 2, 0:5, :].rearrange("p k d -> p (k d)").unsqueeze(1), ACT.Copy,
                                         accum_out=indeg[:, bass.ds(j * 5 + g, 1)]).then_inc(s_ct, 1)


def layernorm_relu(nc, do, act_do, x, out, stat, scratch, eps=LN_EPS):
    mean, var, rstd = stat[:, 0, :], stat[:, 1, :], stat[:, 2, :]
    do(nc.vector.tensor_reduce(mean, x, AX.X, ALU.add))
    do(nc.vector.tensor_scalar(mean, mean, 1.0 / D, None, ALU.mult))
    do(nc.vector.tensor_tensor(out, x, mean.unsqueeze(2).to_broadcast([P, NT, D]), ALU.subtract))
    do(nc.vector.tensor_tensor(scratch, out, out, ALU.mult))
    do(nc.vector.tensor_reduce(var, scratch, AX.X, ALU.add))
    do(nc.vector.tensor_scalar(var, var, 1.0 / D, eps, ALU.mult, ALU.add))
    act_do()
    do(nc.vector.reciprocal(rstd, rstd))
    do(nc.vector.tensor_tensor(out, out, rstd.unsqueeze(2).to_broadcast([P, NT, D]), ALU.mult))
    do(nc.vector.tensor_scalar(out, out, 0.0, None, ALU.max))


def propagate(nc, x_in, CT, indeg, x_out_d):
    with ExitStack() as ctx:
        m = Scope(nc, ctx, "layer0")
        x = m.sb("x", [P, NT, D], F32)
        h = m.sb("h", [P, NT, D], F32)
        g = m.sb("g", [P, NT, D], F32)
        U = m.sb("U", [P, 2, NT, 2, D], F16)
        one = m.sb("one", [P, 1], F16)
        stat = m.sb("stat", [P, 3, NT], F32)
        dc = m.sb("dc", [P, NT], F32)
        dr = m.sb("dr", [P, NT], F32)
        gd = m.sb("gd", [P, NT], F32)
        a = m.sb("a", [P, NT], F32)
        c = m.sb("c", [P, NT], F32)
        lo, s, v, d = (h[:, i * RING:(i + 1) * RING, :] for i in range(4))
        acc = m.ps("acc", [P, RING, 512])
        deg = m.ps("deg", [P, 512])
        s_x = m.sem("x_loaded")
        s_one = m.sem("one_made")
        s_deg = m.sem("out_degrees")
        s_v = m.sem("dve_chain")
        s_var = m.sem("root_wanted")
        s_root = m.sem("root_made")
        s_u = m.sem("part_pairs_made")
        s_acc = m.sem("products_done")
        s_lo = m.sem("low_sums_out")
        s_s = m.sem("sums_made")
        s_new = m.sem("values_made")
        s_hi = m.sem("high_parts_made")
        s_d = m.sem("rests_made")
        s_fin = m.sem("x_updated")
        s_st = m.sem("x_stored")
        block = ctx.enter_context(nc.Block())

        @block.sync
        def _(sp):
            sp.dma_start(x[:, :, :], x_in.rearrange("(k p) f -> p k f", p=P)).then_inc(s_x, 16)
            sp.wait_ge(s_fin, NT)
            sp.dma_start(x_out_d.rearrange("(k p) f -> p k f", p=P), x[:, :, :]).then_inc(s_st, 16)
            sp.wait_ge(s_st, 16)

        @block.vector
        def _(dve):
            do = Chain(dve, s_v)

            def root(n):
                def wait():
                    dve.sem_inc(s_var, 1)
                    dve.wait_ge(s_root, n)
                return wait

            nc.vector.memset(one[:, :], 1.0).then_inc(s_one, 1)
            dve.wait_ge(s_x, 16)
            layernorm_relu(nc, do, root(1), x[:, :, :], h[:, :, :], stat, g[:, :, :])
            do(nc.vector.tensor_reduce(dc[:, :], indeg[:, :].rearrange("p (j g) -> p j g", g=5), AX.X, ALU.add))
            dve.wait_ge(s_deg, 1)
            do(nc.vector.tensor_scalar(dr[:, :], deg[:, 0:NT], 2.0, 1.0, ALU.mult, ALU.max))
            do(nc.vector.tensor_scalar(dc[:, :], dc[:, :], 2.0, 1.0, ALU.mult, ALU.max))
            root(3)()
            do(nc.vector.reciprocal(dc[:, :], dc[:, :]))
            do(nc.vector.reciprocal(dr[:, :], dr[:, :]))
            do(nc.vector.tensor_scalar(gd[:, :], dc[:, :], ALPHA * USCALE, None, ALU.mult))
            do(nc.vector.scalar_tensor_tensor(a[:, :], dr[:, :], 2.0 * BETA, dc[:, :], ALU.mult, ALU.mult))
            do(nc.vector.tensor_scalar(c[:, :], dr[:, :], 2.0 * BETA / USCALE / THETA, None, ALU.mult))
            do(nc.vector.tensor_tensor(g[:, :, :], h[:, :, :], gd[:, :].unsqueeze(2).to_broadcast([P, NT, D]), ALU.mult))
            do(nc.vector.scalar_tensor_tensor(x[:, :, :], h[:, :, :], ALPHA / THETA, x[:, :, :], ALU.mult, ALU.add))
            do(nc.vector.tensor_scalar(h[:, :, :], g[:, :, :], 1.0 / ALPHA, None, ALU.mult))
            do(nc.vector.tensor_copy(U[:, 0, :, 0, :], h[:, :, :]))
            do(nc.vector.tensor_tensor(h[:, :, :], h[:, :, :], U[:, 0, :, 0, :], ALU.subtract))
            do(nc.vector.tensor_scalar(U[:, 0, :, 1, :], h[:, :, :], LOSCALE, None, ALU.mult))
            dve.sem_inc(s_u, NT)

            def step(nxt, at, n):
                for k in range(NT):
                    dve.wait_ge(s_lo, n + k + 1 + RING)
                    nc.vector.tensor_tensor(s[:, k % RING, :], lo[:, k % RING, :], acc[:, k % RING, 0:D], ALU.add).then_inc(s_s, 1)
                    dve.wait_ge(s_s, n + k + 1 + RING)
                    if nxt is None:
                        nc.vector.scalar_tensor_tensor(x[:, k, :], s[:, k % RING, :], c[:, k:k + 1], x[:, k, :],
                                                       ALU.mult, ALU.add).then_inc(s_fin, 1)
                        continue
                    nc.vector.scalar_tensor_tensor(v[:, k % RING, :], s[:, k % RING, :], a[:, k:k + 1], g[:, k, :],
                                                   ALU.mult, ALU.add).then_inc(s_new, 1)
                    dve.wait_ge(s_hi, n + k + 1)
                    nc.vector.tensor_tensor(d[:, k % RING, :], v[:, k % RING, :], U[:, nxt, k, 0, :], ALU.subtract).then_inc(s_d, 1)

            with dve.Fori(0, K_STEPS - 2, 2) as i:
                for b in range(2):
                    step(1 - b, b, i * NT + b * NT)
            step(1, 0, (K_STEPS - 2) * NT)
            step(None, 1, (K_STEPS - 1) * NT)

        @block.scalar
        def _(act):
            act.wait_ge(s_var, 1)
            nc.scalar.sqrt(stat[:, 2, :], stat[:, 1, :]).then_inc(s_root, 1)
            act.wait_ge(s_var, 2)
            nc.scalar.sqrt(dc[:, :], dc[:, :]).then_inc(s_root, 1)
            nc.scalar.sqrt(dr[:, :], dr[:, :]).then_inc(s_root, 1)

            def step(nxt, n):
                for k in range(NT + 1):
                    if k < NT:
                        act.wait_ge(s_acc, n + k + 1)
                        nc.scalar.activation(lo[:, k % RING, :], acc[:, k % RING, D:2 * D], ACT.Copy,
                                             scale=1.0 / LOSCALE).then_inc(s_lo, 1)
                        if nxt is not None:
                            act.wait_ge(s_new, n + k + 1)
                            nc.scalar.activation(U[:, nxt, k, 0, :], v[:, k % RING, :], ACT.Copy).then_inc(s_hi, 1)
                    if k >= 1 and nxt is not None:
                        act.wait_ge(s_d, n + k)
                        nc.scalar.activation(U[:, nxt, k - 1, 1, :], d[:, (k - 1) % RING, :], ACT.Copy,
                                             scale=LOSCALE).then_inc(s_u, 1)

            with act.Fori(0, K_STEPS - 2, 2) as i:
                for b in range(2):
                    step(1 - b, i * NT + b * NT)
            step(1, (K_STEPS - 2) * NT)
            step(None, (K_STEPS - 1) * NT)

        @block.tensor
        def _(pe):
            pe.sem_inc(s_lo, RING)
            pe.sem_inc(s_s, RING)
            pe.wait_ge(s_one, 1)
            for k in range(NT):
                for t in range(NT):
                    mm = pe.matmul(deg[:, k:k + 1], CT[:, t, k * P:(k + 1) * P], one[:, :],
                                   start=(t == 0), stop=(t == NT - 1))
            mm.then_inc(s_deg, 1)

            def step(cur, n):
                for k in range(NT):
                    pe.wait_ge(s_lo, n + k + 1)
                    pe.wait_ge(s_s, n + k + 1)
                    for t in range(NT):
                        if k == 0:
                            pe.wait_ge(s_u, n + t + 1)
                        mm = pe.matmul(acc[:, k % RING, 0:2 * D], CT[:, t, k * P:(k + 1) * P],
                                       U[:, cur, t, :, :].rearrange("p a f -> p (a f)"),
                                       start=(t == 0), stop=(t == NT - 1))
                    mm.then_inc(s_acc, 1)

            with pe.Fori(0, K_STEPS - 2, 2) as i:
                for b in range(2):
                    step(b, i * NT + b * NT)
            step(0, (K_STEPS - 2) * NT)
            step(1, (K_STEPS - 1) * NT)


def node_terms(nc, x_in, We, be, Wn, bn, P_d, x, Q3):
    D2 = 2 * D
    with ExitStack() as ctx:
        m = Scope(nc, ctx, "terms1")
        h = m.sb("h", [P, NT, D], F32)
        stat = m.sb("stat", [P, 3, NT], F32)
        rowno = m.sb("rowno", [P, P], F32)
        colno = m.sb("colno", [P, P], F32)
        ident = m.sb("ident", [P, P], F32)
        W = m.sb("W", [D, 2, D2], F32)
        bias = m.sb("bias", [P, D2], F32)
        hT = m.sb("hT", [D, 2, P], F32)
        Pn = m.sb("Pn", [P, NT, D2], F32)
        Qf = m.sb("Qf", [P, NT, D2], F32)
        tp = m.ps("tp", [P, 2, 512])
        prod = m.ps("prod", [P, 2, 512])
        s_x = m.sem("x_loaded")
        s_w = m.sem("weights_loaded")
        s_c = m.sem("iotas_made")
        s_id = m.sem("identity_made")
        s_v = m.sem("dve_chain")
        s_var = m.sem("root_wanted")
        s_root = m.sem("root_made")
        s_h = m.sem("h_made")
        s_tp = m.sem("h_turned")
        s_hT = m.sem("turned_h_out")
        s_pr = m.sem("products_done")
        s_P = m.sem("source_terms_out")
        s_Q = m.sem("target_terms_out")
        s_st = m.sem("source_terms_stored")
        block = ctx.enter_context(nc.Block())

        @block.sync
        def _(sp):
            sp.dma_start(x[:, :, :], x_in.rearrange("(k p) f -> p k f", p=P)).then_inc(s_x, 16)
            for i, (w, b) in enumerate(((We, be), (Wn, bn))):
                sp.dma_start(W[:, 0, i * D:(i + 1) * D], w[0:D, :]).then_inc(s_w, 16)
                sp.dma_start(W[:, 1, i * D:(i + 1) * D], w[D:2 * D, :]).then_inc(s_w, 16)
                sp.dma_start(bias[:, i * D:(i + 1) * D],
                             b.rearrange("(o f) -> o f", o=1).to_broadcast([P, D])).then_inc(s_w, 16)
            sp.wait_ge(s_P, NT)
            sp.dma_start(P_d.rearrange("(k p) f -> p k f", p=P), Pn[:, :, :]).then_inc(s_st, 16)
            sp.wait_ge(s_st, 16)

        @block.gpsimd
        def _(pool):
            nc.gpsimd.iota(colno[:, :], pattern=[[1, P]], base=0, channel_multiplier=0,
                           allow_small_or_imprecise_dtypes=True).then_inc(s_c, 1)
            nc.gpsimd.iota(rowno[:, :], pattern=[[0, P]], base=0, channel_multiplier=1,
                           allow_small_or_imprecise_dtypes=True).then_inc(s_c, 1)

        @block.vector
        def _(dve):
            do = Chain(dve, s_v)

            def root():
                dve.sem_inc(s_var, 1)
                dve.wait_ge(s_root, 1)

            dve.wait_ge(s_c, 2)
            nc.vector.tensor_tensor(ident[:, :], rowno[:, :], colno[:, :], ALU.is_equal).then_inc(s_id, 1)
            dve.wait_ge(s_x, 16)
            layernorm_relu(nc, do, root, x[:, :, :], h[:, :, :], stat, Qf[:, :, 0:D])
            dve.sem_inc(s_h, 1)
            do(nc.vector.tensor_tensor(x[:, :, :], x[:, :, :], h[:, :, :], ALU.add))
            dve.wait_ge(s_w, 96)
            for k in range(NT):
                dve.wait_ge(s_P, k + 1)
                nc.vector.tensor_tensor(Qf[:, k, :], prod[:, k % 2, D2:2 * D2], bias[:, :], ALU.add).then_inc(s_Q, 1)
            dve.wait_ge(s_Q, NT)
            do(nc.vector.tensor_copy(Q3[:, :, 0, :], Qf[:, :, :]))
            do(nc.vector.tensor_tensor(Qf[:, :, :], Qf[:, :, :], Q3[:, :, 0, :], ALU.subtract))
            do(nc.vector.tensor_copy(Q3[:, :, 1, :], Qf[:, :, :]))
            do(nc.vector.tensor_tensor(Qf[:, :, :], Qf[:, :, :], Q3[:, :, 1, :], ALU.subtract))
            do(nc.vector.tensor_copy(Q3[:, :, 2, :], Qf[:, :, :]))

        @block.scalar
        def _(act):
            act.wait_ge(s_var, 1)
            nc.scalar.sqrt(stat[:, 2, :], stat[:, 1, :]).then_inc(s_root, 1)
            for k in range(NT):
                act.wait_ge(s_tp, k + 1)
                nc.scalar.activation(hT[:, k % 2, :], tp[0:D, k % 2, 0:P], ACT.Copy).then_inc(s_hT, 1)
                act.wait_ge(s_pr, k + 1)
                nc.scalar.activation(Pn[:, k, :], prod[:, k % 2, 0:D2], ACT.Copy).then_inc(s_P, 1)

        @block.tensor
        def _(pe):
            pe.wait_ge(s_id, 1)
            pe.wait_ge(s_w, 96)
            pe.wait_ge(s_h, 1)
            for k in range(NT + 1):
                if k < NT:
                    if k >= 2:
                        pe.wait_ge(s_hT, k - 1)
                    pe.transpose(tp[0:D, k % 2, 0:P], h[:, k, :], ident[:, :]).then_inc(s_tp, 1)
                if k >= 1:
                    pe.wait_ge(s_hT, k)
                    if k >= 3:
                        pe.wait_ge(s_Q, k - 2)
                    pe.matmul(prod[:, (k - 1) % 2, 0:2 * D2], hT[:, (k - 1) % 2, :],
                              W[:, :, :].rearrange("p s f -> p (s f)"), start=True, stop=True).then_inc(s_pr, 1)


def gated_edges(nc, x_in, src_cols, dst_cols, w_cols, attr, We, be, Wn, bn, tab_d, row_d, P_d, x_out_d, wdeg):
    D2 = 2 * D
    with ExitStack() as ctx:
        m = Scope(nc, ctx, "layer1")
        x = m.sb("x", [P, NT, D], F32)
        Q3 = m.sb("Q3", [P, NT, 3, D2], BF16)
        node_terms(nc, x_in, We, be, Wn, bn, P_d, x, Q3)
        agg = m.sb("agg", [P, NT, D + 2], F32)
        dstF = m.sb("dstF", [P, ETC], F32)
        dstI = m.sb("dstI", [P, ETC], I32)
        ew = m.sb("ew", [P, ETC], F32)
        tab = m.sb("tab", [1, NT, 2], I16)
        nodes = m.sb("nodes", [P, NP], F32)
        nodeno = m.sb("nodeno", [P, NT], F32)
        Wa = m.sb("Wa", [DE, D2], F32)
        count = m.sb("count", [P, NT], F32)
        srcs = m.sb("srcs", [P, 2, SE], I32)
        at = m.sb("at", [DE, 2, SE * P], F32)
        rows = m.sb("rows", [P, 2, SE * P], I16)
        R = m.sb("R", [P, 2, SE, D2], F32)
        hot = m.sb("hot", [P, 2, SE, P], F32)
        hotT = m.sb("hotT", [P, 2, SE, P], BF16)
        z = m.sb("z", [P, 2, SE, D2], F32)
        y = m.sb("y", [P, 2, SE, D2], F32)
        G = m.sb("G", [P, 2, SE, D + 2], F32)
        zp = [m.ps(f"zp{h}", [P, SE // 2, 512]) for h in range(2)]
        acc = [m.ps(f"acc{h}", [P, 512]) for h in range(2)]
        s_c = m.sem("constants_made")
        s_tab = m.sem("ranges_loaded")
        s_dst = m.sem("targets_loaded")
        s_w = m.sem("weights_loaded")
        s_ew = m.sem("edge_weights_loaded")
        s_at = [m.sem(f"attributes_loaded{h}") for h in range(2)]
        s_rows = [m.sem(f"target_rows_loaded{h}") for h in range(2)]
        s_ix = [m.sem(f"sources_loaded{h}") for h in range(2)]
        s_R = [m.sem(f"source_terms_gathered{h}") for h in range(2)]
        s_taken = m.sem("waits_taken")
        s_hot = m.sem("onehots_made")
        s_hT = m.sem("turned_onehots_made")
        s_att = m.sem("attribute_products_done")
        s_z = m.sem("z_summed")
        s_add = m.sem("z_out")
        s_abs = m.sem("magnitudes_made")
        s_e = m.sem("exponentials_made")
        s_l = m.sem("logarithms_made")
        s_ms = m.sem("gate_log_and_message_made")
        s_g = m.sem("gates_made")
        s_G = m.sem("gated_messages_made")
        s_seg = m.sem("step_aggregated")
        s_acc = m.sem("sums_accumulated")
        s_v = m.sem("dve_chain")
        s_st = m.sem("x_stored")
        s_fin = m.sem("x_updated")
        block = ctx.enter_context(nc.Block())

        def ranges(eng, j):
            t0 = eng.value_load(tab[0:1, bass.ds(j, 1), 0:1], min_val=0, max_val=TCLAMP)
            end = eng.value_load(tab[0:1, bass.ds(j, 1), 1:2], min_val=1, max_val=TCLAMP + 1)
            return t0, end


        @block.sync
        def _(sp):
            sp.dma_start(tab[:, :, :], tab_d[(QG - 1) * P:(QG - 1) * P + NT, :].rearrange("(o q) b -> o q b", o=1)).then_inc(s_tab, 16)
            sp.dma_start(dstI[:, :], dst_cols).then_inc(s_dst, 16)
            sp.dma_start(ew[:, :], w_cols).then_inc(s_ew, 16)
            sp.dma_start(Wa[:, 0:D], We[2 * D:, :]).then_inc(s_w, 16)
            sp.dma_start(Wa[:, D:], Wn[2 * D:, :]).then_inc(s_w, 16)
            sp.wait_ge(s_tab, 16)
            n = sp.alloc_register("sp_steps")
            sp.reg_mov(n, 0)
            with sp.Fori(0, NT) as j:
                t0, end = ranges(sp, j)
                with sp.Fori(t0, end, 2 * SE) as t:
                    p = sp.snap(n)
                    for h in range(2):
                        first = t + h * SE
                        sp.wait_ge(s_hT, p + h + 1)
                        sp.sem_inc(s_taken, 1)
                        sp.dma_start(rows[:, h, :], row_d[:, bass.ds(first * P, SE * P)].to_broadcast([P, SE * P])).then_inc(s_rows[h], 16)
                        sp.wait_ge(s_att, p + h + 1)
                        sp.sem_inc(s_taken, 1)
                        sp.dma_start(at[:, h, :], attr[:, bass.ds(first * P, SE * P)]).then_inc(s_at[h], 16)
                        sp.wait_ge(s_add, p + h + 1)
                        sp.sem_inc(s_taken, 1)
                        sp.dma_start(srcs[:, h, :], src_cols[:, bass.ds(first, SE)]).then_inc(s_ix[h], 16)
                    sp.reg_add(n, n, 2)
            sp.wait_ge(s_fin, 1)
            sp.dma_start(x_out_d.rearrange("(k p) f -> p k f", p=P), x[:, :, :]).then_inc(s_st, 16)
            sp.wait_ge(s_st, 16)

        @block.gpsimd
        def _(pool):
            nc.gpsimd.iota(nodes[:, :], pattern=[[1, NP]], base=0, channel_multiplier=0,
                           allow_small_or_imprecise_dtypes=True).then_inc(s_c, 1)
            nc.gpsimd.iota(nodeno[:, :], pattern=[[P, NT]], base=0, channel_multiplier=1,
                           allow_small_or_imprecise_dtypes=True).then_inc(s_c, 1)
            pool.wait_ge(s_tab, 16)
            loads = pool.alloc_register("pool_loads")
            pool.reg_mov(loads, 0)
            with pool.Fori(0, NT) as j:
                t0, end = ranges(pool, j)
                with pool.Fori(t0, end, 2 * SE):
                    pool.reg_add(loads, loads, 16)
                    loaded = pool.snap(loads)
                    for h in range(2):
                        pool.wait_ge(s_ix[h], loaded)
                        pool.sem_inc(s_taken, 1)
                        for u in range(SE):
                            nc.gpsimd.indirect_dma_start(
                                R[:, h, u, :], None, P_d,
                                bass.IndirectOffsetOnAxis(ap=srcs[:, h, u:u + 1], axis=0)).then_inc(s_R[h], 16)

        @block.vector
        def _(dve):
            do = Chain(dve, s_v)
            nc.vector.memset(agg[:, :, :], 0.0).then_inc(s_c, 1)
            nc.vector.memset(z[:, 1, :, :], 0.0).then_inc(s_c, 1)
            nc.vector.memset(y[:, 1, :, :], 0.0).then_inc(s_c, 1)
            nc.vector.memset(hot[:, :, :, :], 0.0).then_inc(s_c, 1)
            nc.vector.memset(G[:, :, :, :], 0.0).then_inc(s_c, 1)
            dve.wait_ge(s_c, 7)
            nc.vector.memset(G[:, :, :, D + 1:D + 2], 1.0).then_inc(s_c, 1)
            dve.wait_ge(s_dst, 16)
            do(nc.vector.tensor_copy(dstF[:, :], dstI[:, :]))
            dve.wait_ge(s_c, 8)
            dve.wait_ge(s_ew, 16)
            dve.wait_ge(s_tab, 16)
            n = dve.alloc_register("dve_steps")
            dve.reg_mov(n, 0)
            loads = dve.alloc_register("dve_loads")
            dve.reg_mov(loads, 0)
            gathered = dve.alloc_register("dve_gathered")
            dve.reg_mov(gathered, 0)
            last = dve.alloc_register("dve_last_node_tile")
            dve.reg_mov(last, 0)

            def turned(h, j, loaded):
                dve.wait_ge(s_rows[h], loaded)
                nc.vector.tensor_scalar(hotT[:, h, :, :].rearrange("p u e -> p (u e)"), rows[:, h, :],
                                        nodeno[:, bass.ds(j, 1)], None, ALU.is_equal).then_inc(s_hT, 1)

            def onehots(h, t, j):
                nc.vector.tensor_copy(G[:, h, :, D:D + 1], ew[:, bass.ds(t + h * SE, SE)].unsqueeze(2))
                nc.vector.tensor_tensor(hot[:, h, :, :],
                                        nodes[:, bass.ds(j * P, P)].unsqueeze(1).to_broadcast([P, SE, P]),
                                        dstF[:, bass.ds(t + h * SE, SE)].unsqueeze(2).to_broadcast([P, SE, P]),
                                        ALU.is_equal).then_inc(s_hot, 1)

            def add(h, p, arrived):
                dve.wait_ge(s_z, p + 1)
                dve.wait_ge(s_R[h], arrived)
                dve.wait_ge(s_G, p + 1)
                nc.vector.tensor_tensor(z[:, h, :, :].rearrange("p (b u) f -> p b (u f)", b=SE // 2),
                                        zp[h][:, :, 0:2 * D2],
                                        R[:, h, :, :].rearrange("p (b u) f -> p b (u f)", b=SE // 2),
                                        ALU.add).then_inc(s_add, 1)

            def logs(h, p):
                dve.wait_ge(s_l, p + 2)
                nc.vector.scalar_tensor_tensor(z[:, h, :, D:], z[:, h, :, D:], 0.0, y[:, h, :, D:],
                                               ALU.max, ALU.add)
                nc.vector.scalar_tensor_tensor(z[:, h, :, 0:D], z[:, h, :, 0:D], 0.0, y[:, h, :, 0:D],
                                               ALU.min, ALU.subtract).then_inc(s_ms, 1)

            def gated(h, p):
                dve.wait_ge(s_g, p + 2)
                nc.vector.tensor_tensor(G[:, h, :, 0:D], y[:, h, :, 0:D], z[:, h, :, D:],
                                        ALU.mult).then_inc(s_G, 1)

            def accumulate(h, p, j):
                dve.wait_ge(s_seg, p + 3)
                into = agg[:, bass.ds(j, 1), :]
                nc.vector.tensor_tensor(into, into, acc[h][:, 0:D + 2].unsqueeze(1), ALU.add).then_inc(s_acc, 1)

            with dve.Fori(0, NT) as j:
                t0, end = ranges(dve, j)
                with dve.Fori(t0, end, 2 * SE) as t:
                    p = dve.snap(n)
                    before = nc.s_assert_within(dve.snap(last), 0, NT - 1,
                                                skip_runtime_bounds_check_because="zero or a past j of the loop")
                    dve.reg_add(loads, loads, 16)
                    loaded = dve.snap(loads)
                    dve.reg_add(gathered, gathered, 16 * SE)
                    arrived = dve.snap(gathered)
                    for h in range(2):
                        turned(h, j, loaded)
                    for h in range(2):
                        add(h, p + h, arrived)
                        logs(1 - h, p + (h - 1))
                        accumulate(h, p + (h - 2), before)
                        onehots(h, t, j)
                        gated(1 - h, p + (h - 1))
                    dve.reg_mov(last, j)
                    dve.reg_add(n, n, 2)
            end = dve.snap(n)
            logs(1, end - 1)
            accumulate(0, end - 2, NT - 1)
            gated(1, end - 1)
            dve.wait_ge(s_acc, end + 3)
            accumulate(1, end - 1, NT - 1)
            dve.wait_ge(s_acc, end + 4)
            cnt = count[:, :]
            do(nc.vector.tensor_copy(wdeg[:, :], agg[:, :, D]))
            do(nc.vector.tensor_scalar(cnt, agg[:, :, D + 1], 1.0, None, ALU.max))
            do(nc.vector.reciprocal(cnt, cnt))
            do(nc.vector.tensor_tensor(agg[:, :, 0:D], agg[:, :, 0:D], cnt.unsqueeze(2).to_broadcast([P, NT, D]), ALU.mult))
            nc.vector.tensor_tensor(x[:, :, :], x[:, :, :], agg[:, :, 0:D], ALU.add).then_inc(s_fin, 1)

        @block.scalar
        def _(act):
            act.preload_act_table_set("natural_log_exp_and_others")
            act.sem_inc(s_l, 1)
            act.wait_ge(s_c, 8)
            act.wait_ge(s_tab, 16)
            n = act.alloc_register("act_steps")
            act.reg_mov(n, 0)

            def gates(h, p):
                act.wait_ge(s_ms, p + 2)
                nc.scalar.activation(y[:, h, :, 0:D], z[:, h, :, 0:D], ACT.Exp).then_inc(s_g, 1)

            def magnitude(h, p):
                act.wait_ge(s_add, p + 3)
                nc.scalar.activation(y[:, h, :, :], z[:, h, :, :], ACT.Abs).then_inc(s_abs, 1)

            def softplus(h, p):
                act.wait_ge(s_abs, p + 1)
                nc.scalar.activation(y[:, h, :, :], y[:, h, :, :], ACT.Exp, scale=-1.0).then_inc(s_e, 1)
                act.wait_ge(s_e, p + 1)
                nc.scalar.activation(y[:, h, :, :], y[:, h, :, :], ACT.Ln, bias=1.0).then_inc(s_l, 1)

            with act.Fori(0, NT) as j:
                t0, end = ranges(act, j)
                with act.Fori(t0, end, 2 * SE):
                    p = act.snap(n)
                    for h in range(2):
                        magnitude(h, p + h)
                        gates(1 - h, p + (h - 1))
                        softplus(h, p + h)
                    act.reg_add(n, n, 2)
            gates(1, act.snap(n) - 1)

        @block.tensor
        def _(pe):
            pe.sem_inc(s_add, 2)
            pe.sem_inc(s_att, 2)
            pe.sem_inc(s_hT, 2)
            pe.sem_inc(s_acc, 2)
            pe.sem_inc(s_hot, 2)
            pe.sem_inc(s_G, 1)
            pe.wait_ge(s_c, 8)
            pe.wait_ge(s_w, 32)
            pe.wait_ge(s_tab, 16)
            n = pe.alloc_register("pe_steps")
            pe.reg_mov(n, 0)
            loads = pe.alloc_register("pe_loads")
            pe.reg_mov(loads, 0)

            def sums(h, p, loaded, j):
                pe.wait_ge(s_add, p + 1)
                pe.wait_ge(s_at[h], loaded)
                for u in range(SE):
                    mm = pe.matmul(zp[h][:, u // 2, u % 2 * D2:(u % 2 + 1) * D2], at[:, h, u * P:(u + 1) * P],
                                   Wa[:, :], start=(u % 2 == 0), stop=False, skip_group_check=True)
                mm.then_inc(s_att, 1)
                pe.wait_ge(s_hT, p + 3)
                for u in range(SE):
                    for part in range(3):
                        mm = pe.matmul(zp[h][:, u // 2, u % 2 * D2:(u % 2 + 1) * D2], hotT[:, h, u, :],
                                       Q3[:, bass.ds(j, 1), part, :].rearrange("p o f -> p (o f)"),
                                       start=False, stop=(part == 2), skip_group_check=True)
                mm.then_inc(s_z, 1)

            def aggregate(h, p):
                pe.wait_ge(s_hot, p + 3)
                pe.wait_ge(s_acc, p + 3)
                pe.wait_ge(s_G, p + 3)
                for u in range(SE):
                    mm = pe.matmul(acc[h][:, 0:D + 2], hot[:, h, u, :], G[:, h, u, :],
                                   start=(u == 0), stop=(u == SE - 1))
                mm.then_inc(s_seg, 1)

            with pe.Fori(0, NT) as j:
                t0, end = ranges(pe, j)
                with pe.Fori(t0, end, 2 * SE):
                    p = pe.snap(n)
                    pe.reg_add(loads, loads, 16)
                    loaded = pe.snap(loads)
                    for h in range(2):
                        sums(h, p + h, loaded, j)
                        aggregate(h, p + (h - 2))
                    pe.reg_add(n, n, 2)
            for h in range(2):
                aggregate(h, pe.snap(n) + (h - 2))


def residual_gcn(nc, x_in, C_d, layers, x_out_d):
    with ExitStack() as ctx:
        m = Scope(nc, ctx, "layer2")
        C = m.sb("C", [P, NT, NT, P], F16)
        x = m.sb("x", [P, NT, D], F32)
        h = m.sb("h", [P, NT, D], F32)
        cv = m.sb("cv", [P, NT, D], F32)
        U = m.sb("U", [P, NT, 3, D], BF16)
        ident = m.sb("ident", [P, P], F32)
        mask = m.sb("mask", [P, 2, P], F32)
        W = m.sb("W", [D, 2, D], F32)
        vec = m.sb("vec", [P, 2, 4, D], F32)
        stat = m.sb("stat", [P, 3, NT], F32)
        hT = m.sb("hT", [D, 2, P], F32)
        rest = m.sb("rest", [P, 2, D], F32)
        part = m.sb("part", [P, 2, D], F32)
        sq = U[:, :, :, :].rearrange("p k a f -> p (k a f)").bitcast(F32)[:, 0:NT * D].rearrange("p (k f) -> p k f", f=D)
        mu = m.sb("mu", [P, D], F32)
        sd = m.sb("sd", [P, D], F32)
        tp = m.ps("tp", [P, 2, 512])
        acc = m.ps("acc", [P, 4, 512])
        tot = m.ps("tot", [P, 2, 512])
        s_x = m.sem("x_loaded")
        s_par = m.sem("parameters_loaded")
        s_C = [m.sem(f"C_loaded{q}") for q in range(5)]
        s_c = m.sem("iotas_made")
        s_id = m.sem("identity_made")
        s_v = m.sem("dve_chain")
        s_a = m.sem("act_chain")
        s_var = m.sem("root_wanted")
        s_root = m.sem("root_made")
        s_h = m.sem("h_made")
        s_tp = m.sem("h_turned")
        s_hT = m.sem("turned_h_out")
        s_pr = m.sem("hW_done")
        s_u0 = m.sem("first_parts_made")
        s_r = m.sem("rests_made")
        s_u1 = m.sem("second_parts_made")
        s_u2 = m.sem("third_parts_made")
        s_acc = m.sem("aggregates_done")
        s_p2 = m.sem("third_sums_out")
        s_cv = m.sem("conv_tiles_made")
        s_sum = m.sem("column_sums_done")
        s_xc = m.sem("centred")
        s_sq = m.sem("squares_made")
        s_sqs = m.sem("squares_summed")
        s_st = m.sem("x_stored")
        s_fin = m.sem("x_updated")
        block = ctx.enter_context(nc.Block())
        NL = len(layers)

        @block.sync
        def _(sp):
            sp.dma_start(x[:, :, :], x_in.rearrange("(k p) f -> p k f", p=P)).then_inc(s_x, 16)
            for i, (w, b, gw, gb, ga) in enumerate(layers):
                sp.dma_start(W[:, i, :], w).then_inc(s_par, 16)
                for q, vct in enumerate((b, gw, gb, ga)):
                    sp.dma_start(vec[:, i, q, :], vct.rearrange("(o f) -> o f", o=1).to_broadcast([P, D])).then_inc(s_par, 16)
            for j in range(NT):
                sp.dma_start(C[:, j, :, :].rearrange("p k d -> p (k d)"), C_d[j, :, :]).then_inc(s_C[j // 5], 16)
            sp.wait_ge(s_fin, 1)
            sp.dma_start(x_out_d.rearrange("(k p) f -> p k f", p=P), x[:, :, :]).then_inc(s_st, 16)
            sp.wait_ge(s_st, 16)

        @block.gpsimd
        def _(pool):
            nc.gpsimd.iota(mask[:, 0, :], pattern=[[1, P]], base=0, channel_multiplier=0,
                           allow_small_or_imprecise_dtypes=True).then_inc(s_c, 1)
            nc.gpsimd.iota(mask[:, 1, :], pattern=[[0, P]], base=0, channel_multiplier=1,
                           allow_small_or_imprecise_dtypes=True).then_inc(s_c, 1)

        @block.vector
        def _(dve):
            do = Chain(dve, s_v)

            def root(n):
                def wait():
                    dve.sem_inc(s_var, 1)
                    dve.wait_ge(s_root, n)
                return wait

            dve.wait_ge(s_c, 2)
            do(nc.vector.tensor_tensor(ident[:, :], mask[:, 0, :], mask[:, 1, :], ALU.is_equal))
            do(nc.vector.memset(mask[:, 0, :], 1.0))
            nc.vector.tensor_scalar(mask[:, 1, :], mask[:, 1, :], float(LAST), None, ALU.is_lt).then_inc(s_id, 1)
            dve.wait_ge(s_x, 16)
            layernorm_relu(nc, do, root(1), x[:, :, :], h[:, :, :], stat, cv[:, :, :])
            dve.wait_ge(s_par, 16 * 5 * NL)
            for i in range(NL):
                base = i * NT
                dve.sem_inc(s_h, 1)
                for k in range(NT):
                    dve.wait_ge(s_u0, base + k + 1)
                    nc.vector.tensor_tensor(rest[:, k % 2, :], tp[:, k % 2, P:P + D], U[:, k, 0, :],
                                            ALU.subtract).then_inc(s_r, 1)
                    dve.wait_ge(s_u1, base + k + 1)
                    nc.vector.tensor_tensor(U[:, k, 2, :], rest[:, k % 2, :], U[:, k, 1, :],
                                            ALU.subtract).then_inc(s_u2, 1)
                for j in range(NT):
                    dve.wait_ge(s_p2, base + j + 1)
                    do(nc.vector.scalar_tensor_tensor(part[:, j % 2, :], acc[:, j % 4, D:2 * D], 2.0,
                                                      part[:, j % 2, :], ALU.mult, ALU.add))
                    do(nc.vector.scalar_tensor_tensor(part[:, j % 2, :], acc[:, j % 4, 0:D], 2.0,
                                                      part[:, j % 2, :], ALU.mult, ALU.add))
                    nc.vector.tensor_tensor(cv[:, j, :], part[:, j % 2, :], vec[:, i, 0, :], ALU.add).then_inc(s_cv, 1)
                dve.wait_ge(s_sum, i + 1)
                do(nc.vector.scalar_tensor_tensor(mu[:, :], tot[:, 0, 0:D], 1.0 / N, vec[:, i, 3, :], ALU.mult, ALU.mult))
                do(nc.vector.tensor_tensor(cv[:, :, :], cv[:, :, :], mu[:, :].unsqueeze(1).to_broadcast([P, NT, D]), ALU.subtract))
                dve.sem_inc(s_xc, 1)
                dve.wait_ge(s_sqs, (i + 1) * 5)
                do(nc.vector.tensor_scalar(mu[:, :], tot[:, 1, 0:D], 1.0 / N, LN_EPS, ALU.mult, ALU.add))
                root(2 + i)()
                do(nc.vector.reciprocal(sd[:, :], sd[:, :]))
                do(nc.vector.tensor_tensor(sd[:, :], sd[:, :], vec[:, i, 1, :], ALU.mult))
                do(nc.vector.tensor_tensor(cv[:, :, :], cv[:, :, :], sd[:, :].unsqueeze(1).to_broadcast([P, NT, D]), ALU.mult))
                do(nc.vector.tensor_tensor(cv[:, :, :], cv[:, :, :], vec[:, i, 2, :].unsqueeze(1).to_broadcast([P, NT, D]), ALU.add))
                do(nc.vector.scalar_tensor_tensor(h[:, :, :], cv[:, :, :], 0.0, h[:, :, :], ALU.max, ALU.add))
            nc.vector.tensor_tensor(x[:, :, :], x[:, :, :], h[:, :, :], ALU.add).then_inc(s_fin, 1)

        @block.scalar
        def _(act):
            act.wait_ge(s_var, 1)
            nc.scalar.sqrt(stat[:, 2, :], stat[:, 1, :]).then_inc(s_root, 1)
            for i in range(NL):
                base = i * NT
                for k in range(NT):
                    act.wait_ge(s_tp, base + k + 1)
                    nc.scalar.activation(hT[:, k % 2, :], tp[0:D, k % 2, 0:P], ACT.Copy).then_inc(s_hT, 1)
                    act.wait_ge(s_pr, base + k + 1)
                    nc.scalar.activation(U[:, k, 0, :], tp[:, k % 2, P:P + D], ACT.Copy).then_inc(s_u0, 1)
                    act.wait_ge(s_r, base + k + 1)
                    nc.scalar.activation(U[:, k, 1, :], rest[:, k % 2, :], ACT.Copy).then_inc(s_u1, 1)
                for j in range(NT):
                    act.wait_ge(s_acc, base + j + 1)
                    if base + j >= 2:
                        act.wait_ge(s_cv, base + j - 1)
                    nc.scalar.activation(part[:, j % 2, :], acc[:, j % 4, 2 * D:3 * D], ACT.Copy,
                                         scale=2.0).then_inc(s_p2, 1)
                act.wait_ge(s_xc, i + 1)
                for q in range(5):
                    nc.scalar.activation(sq[:, 5 * q:5 * q + 5, :], cv[:, 5 * q:5 * q + 5, :], ACT.Square).then_inc(s_sq, 1)
                act.wait_ge(s_var, 2 + i)
                nc.scalar.sqrt(sd[:, :], mu[:, :]).then_inc(s_root, 1)

        @block.tensor
        def _(pe):
            pe.wait_ge(s_id, 1)
            pe.wait_ge(s_par, 16 * 5 * NL)
            for i in range(NL):
                base = i * NT
                pe.wait_ge(s_h, i + 1)
                for k in range(NT):
                    if k >= 2:
                        pe.wait_ge(s_r, base + k - 1)
                    pe.transpose(tp[0:D, k % 2, 0:P], h[:, k, :], ident[:, :]).then_inc(s_tp, 1)
                    pe.wait_ge(s_hT, base + k + 1)
                    pe.matmul(tp[:, k % 2, P:P + D], hT[:, k % 2, :], W[:, i, :], start=True, stop=True).then_inc(s_pr, 1)
                for j in range(NT + 2):
                    if j < NT:
                        if base + j >= 4:
                            pe.wait_ge(s_cv, base + j - 3)
                        if i == 0 and j % 5 == 0:
                            pe.wait_ge(s_C[j // 5], 5 * 16)
                        for k in range(NT):
                            if j == 0:
                                pe.wait_ge(s_u2, base + k + 1)
                            mm = pe.matmul(acc[:, j % 4, 0:3 * D], C[:, j, k, :],
                                           U[:, k, :, :].rearrange("p a f -> p (a f)"),
                                           start=(k == 0), stop=(k == NT - 1))
                        mm.then_inc(s_acc, 1)
                    if j >= 2:
                        t = j - 2
                        pe.wait_ge(s_cv, base + t + 1)
                        mm = pe.matmul(tot[:, 0, 0:D], mask[:, int(t == NT - 1), :], cv[:, t, :],
                                       start=(t == 0), stop=(t == NT - 1))
                mm.then_inc(s_sum, 1)
                for q in range(5):
                    pe.wait_ge(s_sq, i * 5 + q + 1)
                    for u in range(5):
                        t = 5 * q + u
                        mm = pe.matmul(tot[:, 1, 0:D], mask[:, int(t == NT - 1), :], sq[:, t, :],
                                       start=(t == 0), stop=(t == NT - 1))
                    mm.then_inc(s_sqs, 1)


def stream_plan(orders, slots):
    holder, last, uses, loads = [None] * slots, [None] * slots, [], []
    for u, j in enumerate(j for order in orders for j in order):
        hit = j in holder
        if not hit:
            s = holder.index(None) if None in holder else min(range(slots), key=lambda q: last[q])
            loads.append((j, s, last[s]))
            holder[s] = j
        s = holder.index(j)
        last[s] = u
        uses.append((j, s, not hit))
    return uses, loads


def weighted_gcn(nc, x_in, W_d, wdeg, layers, out):
    RW = 12
    orders = (list(range(NT)), list(range(NT))[::-1])
    uses, loads = stream_plan(orders, RW)
    with ExitStack() as ctx:
        m = Scope(nc, ctx, "layer3")
        ring = m.sb("ring", [P, RW, NT, P], F32)
        x = m.sb("x", [P, NT, D], F32)
        h = m.sb("h", [P, NT, D], F32)
        V = m.sb("V", [P, NT, D], F32)
        ident = m.sb("ident", [P, P], F32)
        colno = m.sb("colno", [P, P], F32)
        W = m.sb("W", [D, 2, D], F32)
        bias = m.sb("bias", [P, 2, D], F32)
        stat = m.sb("stat", [P, 3, NT], F32)
        dinv = m.sb("dinv", [P, NT], F32)
        pos = m.sb("pos", [P, NT], F32)
        hT = m.sb("hT", [D, 2, P], F32)
        part = m.sb("part", [P, 2, D], F32)
        tp = m.ps("tp", [P, 2, 512])
        acc = m.ps("acc", [P, 4, 512])
        s_x = m.sem("x_loaded")
        s_par = m.sem("parameters_loaded")
        s_W = [m.sem(f"W_slot{s}_loaded") for s in range(RW)]
        s_c = m.sem("iotas_made")
        s_v = m.sem("dve_chain")
        s_var = m.sem("root_wanted")
        s_root = m.sem("root_made")
        s_h = m.sem("h_made")
        s_tp = m.sem("h_turned")
        s_hT = m.sem("turned_h_out")
        s_pr = m.sem("hV_done")
        s_V = m.sem("scaled_made")
        s_acc = m.sem("aggregates_done")
        s_o = m.sem("conv_tiles_made")
        s_exp = m.sem("exponentials_wanted")
        s_e = m.sem("exponentials_made")
        s_st = m.sem("out_stored")
        s_fin = m.sem("out_made")
        block = ctx.enter_context(nc.Block())
        NL = len(layers)

        @block.sync
        def _(sp):
            sp.dma_start(x[:, :, :], x_in.rearrange("(k p) f -> p k f", p=P)).then_inc(s_x, 16)
            for i, (w, b) in enumerate(layers):
                sp.dma_start(W[:, i, :], w).then_inc(s_par, 16)
                sp.dma_start(bias[:, i, :], b.rearrange("(o f) -> o f", o=1).to_broadcast([P, D])).then_inc(s_par, 16)
            for j, s, freed in loads:
                if freed is not None:
                    sp.wait_ge(s_acc, freed + 1)
                sp.dma_start(ring[:, s, :, :].rearrange("p k d -> p (k d)"), W_d[j, :, :]).then_inc(s_W[s], 16)
            sp.wait_ge(s_fin, 1)
            sp.dma_start(out.rearrange("(k p) f -> p k f", p=P), x[:, :, :]).then_inc(s_st, 16)
            sp.wait_ge(s_st, 16)

        @block.gpsimd
        def _(pool):
            nc.gpsimd.iota(colno[:, :], pattern=[[1, P]], base=0, channel_multiplier=0,
                           allow_small_or_imprecise_dtypes=True).then_inc(s_c, 1)
            nc.gpsimd.iota(ident[:, :], pattern=[[0, P]], base=0, channel_multiplier=1,
                           allow_small_or_imprecise_dtypes=True).then_inc(s_c, 1)

        @block.vector
        def _(dve):
            do = Chain(dve, s_v)

            def root(n):
                def wait():
                    dve.sem_inc(s_var, 1)
                    dve.wait_ge(s_root, n)
                return wait

            dve.wait_ge(s_c, 2)
            do(nc.vector.tensor_tensor(ident[:, :], ident[:, :], colno[:, :], ALU.is_equal))
            do(nc.vector.tensor_scalar(dinv[:, :], wdeg[:, :], 1.0, None, ALU.add))
            do(nc.vector.tensor_scalar(pos[:, :], dinv[:, :], 0.0, None, ALU.is_gt))
            do(nc.vector.tensor_scalar(dinv[:, :], dinv[:, :], 1e-30, None, ALU.max))
            root(1)()
            do(nc.vector.reciprocal(dinv[:, :], dinv[:, :]))
            do(nc.vector.tensor_tensor(dinv[:, :], dinv[:, :], pos[:, :], ALU.mult))
            dve.wait_ge(s_x, 16)
            layernorm_relu(nc, do, root(2), x[:, :, :], h[:, :, :], stat, V[:, :, :])
            dve.wait_ge(s_par, 16 * 2 * NL)
            for i in range(NL):
                base = i * NT
                dve.sem_inc(s_h, 1)
                for k in range(NT):
                    dve.wait_ge(s_pr, base + k + 1)
                    nc.vector.tensor_scalar(V[:, k, :], tp[:, k % 2, P:P + D], dinv[:, k:k + 1], None,
                                            ALU.mult).then_inc(s_V, 1)
                for n, j in enumerate(orders[i]):
                    dve.wait_ge(s_acc, base + n + 1)
                    if n == 0:
                        dve.wait_ge(s_V, base + NT)
                    do(nc.vector.tensor_tensor(part[:, n % 2, :], acc[:, n % 4, 0:D], V[:, j, :], ALU.add))
                    nc.vector.scalar_tensor_tensor(h[:, j, :], part[:, n % 2, :], dinv[:, j:j + 1], bias[:, i, :],
                                                   ALU.mult, ALU.add).then_inc(s_o, 1)
                dve.wait_ge(s_o, base + NT)
                if i == 0:
                    do(nc.vector.tensor_scalar(h[:, :, :], h[:, :, :], 0.0, None, ALU.max))
            top, tot = stat[:, 0, :], stat[:, 1, :]
            do(nc.vector.tensor_reduce(top, h[:, :, :], AX.X, ALU.max))
            do(nc.vector.tensor_tensor(h[:, :, :], h[:, :, :], top.unsqueeze(2).to_broadcast([P, NT, D]), ALU.subtract))
            dve.sem_inc(s_exp, 1)
            do(nc.vector.tensor_tensor(x[:, :, :], x[:, :, :], h[:, :, :], ALU.add))
            dve.wait_ge(s_e, 1)
            do(nc.vector.tensor_reduce(tot, V[:, :, :], AX.X, ALU.add))
            dve.sem_inc(s_exp, 1)
            dve.wait_ge(s_e, 2)
            nc.vector.tensor_tensor(x[:, :, :], x[:, :, :], stat[:, 2, :].unsqueeze(2).to_broadcast([P, NT, D]),
                                    ALU.subtract).then_inc(s_fin, 1)

        @block.scalar
        def _(act):
            act.wait_ge(s_var, 1)
            nc.scalar.sqrt(dinv[:, :], dinv[:, :]).then_inc(s_root, 1)
            act.wait_ge(s_var, 2)
            nc.scalar.sqrt(stat[:, 2, :], stat[:, 1, :]).then_inc(s_root, 1)
            for i in range(NL):
                for k in range(NT):
                    act.wait_ge(s_tp, i * NT + k + 1)
                    nc.scalar.activation(hT[:, k % 2, :], tp[0:D, k % 2, 0:P], ACT.Copy).then_inc(s_hT, 1)
            act.wait_ge(s_exp, 1)
            nc.scalar.activation(V[:, :, :], h[:, :, :], ACT.Exp).then_inc(s_e, 1)
            act.wait_ge(s_exp, 2)
            nc.scalar.activation(stat[:, 2, :], stat[:, 1, :], ACT.Ln).then_inc(s_e, 1)

        @block.tensor
        def _(pe):
            pe.wait_ge(s_par, 16 * 2 * NL)
            seen = {}
            for i in range(NL):
                base = i * NT
                pe.wait_ge(s_h, i + 1)
                for k in range(NT):
                    if k >= 2:
                        pe.wait_ge(s_V, base + k - 1)
                    pe.transpose(tp[0:D, k % 2, 0:P], h[:, k, :], ident[:, :]).then_inc(s_tp, 1)
                    pe.wait_ge(s_hT, base + k + 1)
                    pe.matmul(tp[:, k % 2, P:P + D], hT[:, k % 2, :], W[:, i, :], start=True, stop=True).then_inc(s_pr, 1)
                for n in range(NT):
                    j, s, load = uses[base + n]
                    if base + n >= 4:
                        pe.wait_ge(s_o, base + n - 3)
                    if load:
                        seen[s] = seen.get(s, 0) + 16
                        pe.wait_ge(s_W[s], seen[s])
                    for k in range(NT):
                        if n == 0:
                            pe.wait_ge(s_V, base + k + 1)
                        mm = pe.matmul(acc[:, n % 4, 0:D], ring[:, s, k, :], V[:, k, :],
                                       start=(k == 0), stop=(k == NT - 1))
                    mm.then_inc(s_acc, 1)


def gnn(nc, x, src_cols, dst_cols, dst_rows, attr, w_cols, We, be, Wn, bn, W1, b1, W2, b2,
        g1w, g1b, g1a, g2w, g2b, g2a, V1, c1, V2, c2, out):
    tab_d = nc.dram_tensor("range_table", [QG * P, 2], I16, kind="Internal").ap()
    C_d = nc.dram_tensor("C_blocks", [NT, P, NP], F16, kind="Internal").ap()
    W_d = nc.dram_tensor("W_blocks", [NT, P, NP], F32, kind="Internal").ap()
    row_d = nc.dram_tensor("target_rows", [1, ET * P], I16, kind="Internal").ap()
    P_d = nc.dram_tensor("source_terms", [NP, 2 * D], F32, kind="Internal").ap()
    x1_d, x2_d, x3_d = (nc.dram_tensor(f"x_after_{i}", [NP, D], F32, kind="Internal").ap() for i in range(3))
    with ExitStack() as outer:
        o = Scope(nc, outer, "all6")
        indeg = o.sb("indeg", [P, NT * 5], F32)
        CT = o.sb("CT", [P, NT, NP], F16)
        with ExitStack() as ctx:
            m = Scope(nc, ctx, "all7")
            key = m.sb("key", [P, ETC], F32)
            smod = m.sb("smod", [P, ETC], F16)
            wpart = m.sb("wpart", [P, 3, ETC], BF16)
            edge_ranges(nc, src_cols, dst_cols, dst_rows, w_cols, tab_d, row_d, key, smod, wpart)
            build_matrices(nc, tab_d, key, smod, wpart, CT, indeg, C_d, W_d)
        propagate(nc, x, CT, indeg, x1_d)
    with ExitStack() as outer:
        o = Scope(nc, outer, "all8")
        wdeg = o.sb("wdeg", [P, NT], F32)
        gated_edges(nc, x1_d, src_cols, dst_cols, w_cols, attr, We, be, Wn, bn, tab_d, row_d, P_d, x2_d, wdeg)
        residual_gcn(nc, x2_d, C_d, ((W1, b1, g1w, g1b, g1a), (W2, b2, g2w, g2b, g2a)), x3_d)
        weighted_gcn(nc, x3_d, W_d, wdeg, ((V1, c1), (V2, c2)), out)


def kernel(x, src, dst, edge_attr_64, edge_weight, L1_gnn_W_e, L1_gnn_b_e, L1_gnn_W_n, L1_gnn_b_n,
           L2_gnn_W1, L2_gnn_b1, L2_gnn_W2, L2_gnn_b2, L2_gnn_gn1_w, L2_gnn_gn1_b, L2_gnn_gn1_a,
           L2_gnn_gn2_w, L2_gnn_gn2_b, L2_gnn_gn2_a, L3_gnn_W1, L3_gnn_b1, L3_gnn_W2, L3_gnn_b2):
    import numpy as np
    import concourse.bacc as bacc
    from concourse.bass_utils import run_bass_kernel_spmd

    def padded(a, n, value=0):
        a = np.asarray(a)
        out = np.full((n,) + a.shape[1:], value, a.dtype)
        out[:len(a)] = a
        return out

    def columns(a):
        return np.ascontiguousarray(a.reshape(ET, P)[:ETC].T)

    dst_p = padded(dst, ET * P, NO_NODE)
    arrays = {
        "x": padded(x, NP),
        "src_cols": columns(padded(src, ET * P)),
        "dst_cols": columns(dst_p),
        "dst_rows": dst_p.reshape(ET, P),
        "attr": np.ascontiguousarray(padded(edge_attr_64, ET * P).T),
        "w_cols": columns(padded(edge_weight, ET * P)),
        "We": L1_gnn_W_e, "be": L1_gnn_b_e, "Wn": L1_gnn_W_n, "bn": L1_gnn_b_n,
        "W1": L2_gnn_W1, "b1": L2_gnn_b1, "W2": L2_gnn_W2, "b2": L2_gnn_b2,
        "g1w": L2_gnn_gn1_w, "g1b": L2_gnn_gn1_b, "g1a": L2_gnn_gn1_a,
        "g2w": L2_gnn_gn2_w, "g2b": L2_gnn_gn2_b, "g2a": L2_gnn_gn2_a,
        "V1": L3_gnn_W1, "c1": L3_gnn_b1, "V2": L3_gnn_W2, "c2": L3_gnn_b2,
    }
    nc = bacc.Bacc("TRN2", target_bir_lowering=False, num_devices=1)
    args = {}
    for name, a in arrays.items():
        a = arrays[name] = np.ascontiguousarray(a)
        args[name] = nc.dram_tensor(f"in_{name}", a.shape, mybir.dt.from_np(a.dtype), kind="ExternalInput").ap()
    out = nc.dram_tensor("out", (NP, D), F32, kind="ExternalOutput").ap()
    gnn(nc, out=out, **args)
    r = run_bass_kernel_spmd(nc, [{f"in_{name}": a for name, a in arrays.items()}], core_ids=[0])
    return r.results[0]["out"][:N]
```

```python
from contextlib import ExitStack

import concourse.bass as bass
from concourse import mybir

F32, F16, BF16 = mybir.dt.float32, mybir.dt.float16, mybir.dt.bfloat16
I32, I16 = mybir.dt.int32, mybir.dt.int16
ALU = mybir.AluOpType
ACT = mybir.ActivationFunctionType
AX = mybir.AxisListType

P = 128
N, D, E, DE = 3125, 96, 103125, 64
NT = -(-N // P)
NP = NT * P
LAST = N - (NT - 1) * P
ET = 896
EG = ET // P
WIN = 8
NW = NP // WIN
WPT = P // WIN
WC = WIN * NT
CH = 4
SE = 6
NO_NODE = 4000
QG = 5
TCLAMP = -(-E // P)
ETC = TCLAMP + 16
ETB = TCLAMP + CH
K_STEPS, ALPHA, BETA = 10, 0.1, 0.9
THETA = BETA ** K_STEPS + ALPHA * sum(BETA ** i for i in range(K_STEPS))
LN_EPS = 1e-5
USCALE = 64.0
RING = 5
EVAC0 = 7
TG = ((0, 7), (7, 13), (13, 19), (19, 25))
LOSCALE = 2048.0


class Scope:

    def __init__(self, nc, ctx, stage):
        self.nc, self.ctx, self.stage = nc, ctx, stage

    def sb(self, name, shape, dt):
        return self.ctx.enter_context(self.nc.sbuf_tensor(f"{self.stage}_{name}", shape, dt))

    def ps(self, name, shape, dt=F32):
        return self.ctx.enter_context(self.nc.psum_tensor(f"{self.stage}_{name}", shape, dt))

    def sem(self, name):
        return self.ctx.enter_context(self.nc.semaphore(f"{self.stage}_{name}"))


class Chain:

    def __init__(self, eng, sem):
        self.eng, self.sem, self.n = eng, sem, 0

    def __call__(self, ins):
        self.n += 1
        ins.then_inc(self.sem, 1)
        self.eng.wait_ge(self.sem, self.n)


def edge_ranges(nc, src_cols, dst_cols, dst_rows, w_cols, tab_d, row_d, key, smod, wpart):
    with ExitStack() as ctx:
        m = Scope(nc, ctx, "ranges")
        srcI = m.sb("srcI", [P, ETB], I32)
        dstI = m.sb("dstI", [P, ETB], I32)
        rowsI = m.sb("rowsI", [P, EG, P], I32)
        rows16 = m.sb("rows16", [P, EG, P], I16)
        weight = m.sb("weight", [P, ETB], F32)
        least = m.sb("least", [P, EG], F32)
        most = m.sb("most", [P, EG], F32)
        rowno = m.sb("rowno", [P, P], F32)
        colno = m.sb("colno", [P, P], F32)
        ident = m.sb("ident", [P, P], F32)
        ones = m.sb("ones", [P, P], F32)
        spread = m.sb("spread", [P, 2, EG, P], F32)
        up = m.sb("up", [P, ET], F32)
        down = m.sb("down", [P, ET], F32)
        low = m.sb("low", [P, QG], F32)
        high = m.sb("high", [P, QG], F32)
        below = m.sb("below", [P, ET], F32)
        touch = m.sb("touch", [P, ET], F32)
        tileI = rowsI[:, :, :].rearrange("p c e -> p (c e)")[:, 0:ETB]
        left = spread[:, 0, :, :].rearrange("p c e -> p (c e)")[:, 0:ETB]
        r1 = m.sb("r1", [P, QG], F32)
        r2 = m.sb("r2", [P, QG], F32)
        bounds = m.sb("bounds", [P, QG, 2], F32)
        boundsI = m.sb("boundsI", [P, QG, 2], I16)
        bc = m.ps("bc", [P, 4, 512])
        s_in = [m.sem(f"edges_loaded{i}") for i in range(4)]
        s_iota = m.sem("iotas_made")
        s_diag = m.sem("diagonals_made")
        s_bc = m.sem("bounds_broadcast")
        s_r16 = m.sem("small_targets_made")
        s_bounds = m.sem("bounds_made")
        s_tab = m.sem("bounds_stored")
        s_v = m.sem("ranges_dve_chain")
        block = ctx.enter_context(nc.Block())

        @block.sync
        def _(sp):
            sp.dma_start(rowsI[:, :, :], dst_rows.rearrange("(c p) e -> p c e", p=P)).then_inc(s_in[0], 16)
            sp.dma_start(srcI[:, :], src_cols[:, 0:ETB]).then_inc(s_in[1], 16)
            sp.dma_start(dstI[:, :], dst_cols[:, 0:ETB]).then_inc(s_in[2], 16)
            sp.dma_start(weight[:, :], w_cols[:, 0:ETB]).then_inc(s_in[3], 16)
            sp.wait_ge(s_r16, 1)
            sp.dma_start(row_d.rearrange("o (c p e) -> p (o c) e", p=P, e=P), rows16[:, :, :]).then_inc(s_tab, 16)
            sp.wait_ge(s_bounds, 1)
            sp.dma_start(tab_d.rearrange("(q p) b -> p q b", p=P), boundsI[:, :, :]).then_inc(s_tab, 16)
            sp.wait_ge(s_tab, 32)

        @block.gpsimd
        def _(pool):
            nc.gpsimd.iota(colno[:, :], pattern=[[1, P]], base=0, channel_multiplier=0,
                           allow_small_or_imprecise_dtypes=True).then_inc(s_iota, 1)
            nc.gpsimd.iota(rowno[:, :], pattern=[[0, P]], base=0, channel_multiplier=1,
                           allow_small_or_imprecise_dtypes=True).then_inc(s_iota, 1)
            nc.gpsimd.iota(up[:, :], pattern=[[1, ET]], base=1, channel_multiplier=0,
                           allow_small_or_imprecise_dtypes=True).then_inc(s_iota, 1)
            nc.gpsimd.iota(down[:, :], pattern=[[-1, ET]], base=ET, channel_multiplier=0,
                           allow_small_or_imprecise_dtypes=True).then_inc(s_iota, 1)
            nc.gpsimd.iota(low[:, 0:QG - 1], pattern=[[WIN * P, QG - 1]], base=0, channel_multiplier=WIN,
                           allow_small_or_imprecise_dtypes=True).then_inc(s_iota, 1)
            nc.gpsimd.iota(high[:, 0:QG - 1], pattern=[[WIN * P, QG - 1]], base=WIN, channel_multiplier=WIN,
                           allow_small_or_imprecise_dtypes=True).then_inc(s_iota, 1)
            nc.gpsimd.iota(low[:, QG - 1:QG], pattern=[[0, 1]], base=0, channel_multiplier=P,
                           allow_small_or_imprecise_dtypes=True).then_inc(s_iota, 1)
            nc.gpsimd.iota(high[:, QG - 1:QG], pattern=[[0, 1]], base=P, channel_multiplier=P,
                           allow_small_or_imprecise_dtypes=True).then_inc(s_iota, 1)

        @block.tensor
        def _(pe):
            for b in range(2):
                pe.wait_ge(s_diag, b + 1)
                flat = spread[:, b, :, :].rearrange("p c e -> p (c e)")
                for h in range(2):
                    pe.matmul(bc[:, 2 * b + h, 0:ET // 2], ones[:, :], flat[:, h * ET // 2:(h + 1) * ET // 2],
                              start=True, stop=True).then_inc(s_bc, 1)

        @block.vector
        def _(dve):
            do = Chain(dve, s_v)
            dve.wait_ge(s_iota, 8)
            do(nc.vector.tensor_tensor(ident[:, :], rowno[:, :], colno[:, :], ALU.is_equal))
            do(nc.vector.memset(ones[:, :], 1.0))
            dve.wait_ge(s_in[0], 16)
            do(nc.vector.tensor_reduce(least[:, :], rowsI[:, :, :], AX.X, ALU.min))
            nc.vector.tensor_tensor(spread[:, 0, :, :], ident[:, :].unsqueeze(1).to_broadcast([P, EG, P]),
                                    least[:, :].unsqueeze(2).to_broadcast([P, EG, P]), ALU.mult).then_inc(s_diag, 1)
            do(nc.vector.tensor_reduce(most[:, :], rowsI[:, :, :], AX.X, ALU.max))
            nc.vector.tensor_tensor(spread[:, 1, :, :], ident[:, :].unsqueeze(1).to_broadcast([P, EG, P]),
                                    most[:, :].unsqueeze(2).to_broadcast([P, EG, P]), ALU.mult).then_inc(s_diag, 1)
            do(nc.vector.tensor_copy(rows16[:, :, :], rowsI[:, :, :]))
            dve.sem_inc(s_r16, 1)
            dve.wait_ge(s_bc, 4)
            for q in range(QG):
                for h in range(2):
                    cols = slice(h * ET // 2, (h + 1) * ET // 2)
                    do(nc.vector.tensor_scalar(below[:, cols], bc[:, h, 0:ET // 2], high[:, q:q + 1], None,
                                               ALU.is_lt))
                    do(nc.vector.scalar_tensor_tensor(touch[:, cols], bc[:, 2 + h, 0:ET // 2], low[:, q:q + 1],
                                                      below[:, cols], ALU.is_ge, ALU.mult))
                do(nc.vector.tensor_tensor(below[:, :], touch[:, :], down[:, :], ALU.mult))
                do(nc.vector.tensor_reduce(r1[:, q:q + 1], below[:, :], AX.X, ALU.max))
                do(nc.vector.tensor_tensor(touch[:, :], touch[:, :], up[:, :], ALU.mult))
                do(nc.vector.tensor_reduce(r2[:, q:q + 1], touch[:, :], AX.X, ALU.max))
            do(nc.vector.tensor_scalar(bounds[:, :, 0], r1[:, :], -1.0, float(ET), ALU.mult, ALU.add))
            do(nc.vector.tensor_scalar(bounds[:, :, 0], bounds[:, :, 0], float(TCLAMP), None, ALU.min))
            do(nc.vector.scalar_tensor_tensor(bounds[:, :, 1], bounds[:, :, 0], 1.0, r2[:, :], ALU.add, ALU.max))
            nc.vector.tensor_copy(boundsI[:, :, :], bounds[:, :, :]).then_inc(s_bounds, 1)
            dve.wait_ge(s_in[1], 16)
            dve.wait_ge(s_in[2], 16)
            do(nc.vector.tensor_scalar(tileI, srcI[:, :], 7, None, ALU.logical_shift_right))
            do(nc.vector.tensor_scalar(srcI[:, :], srcI[:, :], P - 1, None, ALU.bitwise_and))
            do(nc.vector.scalar_tensor_tensor(key[:, :], dstI[:, :], float(NT), tileI, ALU.mult, ALU.add))
            do(nc.vector.tensor_copy(smod[:, :], srcI[:, :]))
            dve.wait_ge(s_in[3], 16)
            do(nc.vector.tensor_copy(wpart[:, 0, :], weight[:, :]))
            do(nc.vector.tensor_tensor(left, weight[:, :], wpart[:, 0, :], ALU.subtract))
            do(nc.vector.tensor_copy(wpart[:, 1, :], left))
            do(nc.vector.tensor_tensor(left, left, wpart[:, 1, :], ALU.subtract))
            do(nc.vector.tensor_copy(wpart[:, 2, :], left))


def build_matrices(nc, tab_d, key, smod, wpart, CT, indeg, C_d, W_d):
    with ExitStack() as ctx:
        m = Scope(nc, ctx, "build")
        tab = m.sb("tab", [1, NW + 4, 2], I16)
        colsM = m.sb("colsM", [P, WC, CH], F16)
        colsS = m.sb("colsS", [P, P, CH], F16)
        wbase = m.sb("wbase", [P, NW], F32)
        ident = m.sb("ident", [P, P], F16)
        kw = m.sb("kw", [P, 3, CH], F16)
        M = m.sb("M", [P, 3, WC, CH], BF16)
        S = m.sb("S", [P, 3, 4, P, CH], BF16)
        Cblk = m.sb("Cblk", [P, NT, P], F16)
        Wblk = m.sb("Wblk", [P, NT, P], F32)
        rowh = Cblk[:, 0, :]
        win = m.ps("win", [P, 4, 512])
        tp = m.ps("tp", [P, 4, 8, P], F16)
        s_const = m.sem("constants_made")
        s_tab = m.sem("table_loaded")
        s_key = m.sem("window_keys")
        s_hot = m.sem("source_onehots")
        s_made = m.sem("operands_made")
        s_built = m.sem("window_built")
        s_evac = m.sem("window_out")
        s_xkey = m.sem("more_keys")
        s_xhot = m.sem("more_source_onehots")
        s_xmade = m.sem("more_operands_made")
        s_xused = m.sem("more_operands_used")
        s_tp = m.sem("tile_transposed")
        s_ct = m.sem("transposed_out")
        s_cst = m.sem("C_stored")
        s_wst = m.sem("W_stored")
        block = ctx.enter_context(nc.Block())

        def load_ranges(eng, regs, w0):
            eng.load(regs, tab[0:1, bass.ds(w0, 4), :])

        def window_range(eng, regs, b):
            why = "edge_ranges clamps the tables"
            return (nc.s_assert_within(eng.snap(regs[2 * b]), 0, TCLAMP, skip_runtime_bounds_check_because=why),
                    nc.s_assert_within(eng.snap(regs[2 * b + 1]), 1, TCLAMP + 1,
                                       skip_runtime_bounds_check_because=why))

        @block.gpsimd
        def _(pool):
            small = dict(allow_small_or_imprecise_dtypes=True)
            for k in range(NT):
                nc.gpsimd.iota(colsM[:, k * WIN:(k + 1) * WIN, :], pattern=[[NT, WIN], [0, CH]], base=k,
                               channel_multiplier=0, **small).then_inc(s_const, 1)
            nc.gpsimd.iota(colsS[:, :, :], pattern=[[1, P], [0, CH]], base=0, channel_multiplier=0,
                           **small).then_inc(s_const, 1)
            nc.gpsimd.iota(wbase[:, :], pattern=[[WC, NW]], base=0, channel_multiplier=0,
                           **small).then_inc(s_const, 1)
            nc.gpsimd.iota(rowh, pattern=[[0, P]], base=0, channel_multiplier=1,
                           **small).then_inc(s_const, 1)

        @block.sync
        def _(sp):
            sp.dma_start(tab[:, :, :], tab_d[0:NW + 4, :].rearrange("(o q) b -> o q b", o=1)).then_inc(s_tab, 16)
            with sp.Fori(0, NT) as j:
                sp.wait_ge(s_evac, j * (2 * WPT) + 2 * WPT + EVAC0)
                sp.dma_start(C_d[bass.ds(j, 1), :, :].rearrange("o p c -> p (o c)"),
                             Cblk[:, :, :].rearrange("p k d -> p (k d)")).then_inc(s_cst, 16)
                sp.dma_start(W_d[bass.ds(j, 1), :, :].rearrange("o p c -> p (o c)"),
                             Wblk[:, :, :].rearrange("p k d -> p (k d)")).then_inc(s_wst, 16)
            sp.wait_ge(s_cst, 16 * NT + 1)
            sp.wait_ge(s_wst, 16 * NT + 1)

        @block.vector
        def _(dve):
            dve.wait_ge(s_const, NT + 3)
            nc.vector.tensor_tensor(ident[:, :], rowh, colsS[:, :, 0], ALU.is_equal).then_inc(s_const, 1)
            dve.wait_ge(s_tab, 16)

            def operands(slot, w, t, keys, hots, made, n):
                nc.vector.tensor_scalar(kw[:, slot, :], key[:, bass.ds(t, CH)], wbase[:, bass.ds(w, 1)], 1000.0,
                                        ALU.subtract, ALU.min).then_inc(keys, 1)
                nc.vector.tensor_tensor(S[:, slot, 0, :, :], colsS[:, :, :],
                                        smod[:, bass.ds(t, CH)].unsqueeze(1).to_broadcast([P, P, CH]),
                                        ALU.is_equal).then_inc(hots, 1)
                dve.wait_ge(keys, n)
                nc.vector.tensor_tensor(M[:, slot, :, :], colsM[:, :, :],
                                        kw[:, slot, :].unsqueeze(1).to_broadcast([P, WC, CH]), ALU.is_equal)
                dve.wait_ge(hots, n)
                nc.vector.tensor_tensor(
                    S[:, slot, 1:4, :, :], S[:, slot, 0, :, :].unsqueeze(1).to_broadcast([P, 3, P, CH]),
                    wpart[:, :, bass.ds(t, CH)].unsqueeze(2).to_broadcast([P, 3, P, CH]),
                    ALU.mult).then_inc(made, 1)

            regs = [dve.alloc_register(f"dve_bound{r}") for r in range(8)]
            load_ranges(dve, regs, 0)
            more = dve.alloc_register("dve_more")
            dve.reg_mov(more, 0)
            with dve.Fori(0, NW // 4) as i:
                w0 = i * 4
                for b in range(4):
                    t, end = window_range(dve, regs, b)
                    if b == 3:
                        load_ranges(dve, regs, w0 + 4)
                    dve.wait_ge(s_built, w0 + b + 1)
                    operands(b % 2, w0 + b, t, s_key, s_hot, s_made, w0 + b + 1)
                    with dve.If(end > t + CH):
                        with dve.Fori(t + CH, end, CH) as tx:
                            dve.wait_ge(s_xused, dve.snap(more) + 1)
                            dve.reg_add(more, more, 1)
                            operands(2, w0 + b, tx, s_xkey, s_xhot, s_xmade, dve.snap(more))

        @block.tensor
        def _(pe):
            pe.sem_inc(s_built, 2)
            pe.sem_inc(s_xused, 1)
            pe.sem_inc(s_evac, EVAC0)
            pe.sem_inc(s_ct, 4)
            pe.sem_inc(s_cst, 1)
            pe.sem_inc(s_wst, 1)
            pe.wait_ge(s_tab, 16)
            pe.wait_ge(s_const, NT + 4)

            def products(slot, bank, tiles, first):
                for u in tiles:
                    for part in range(4):
                        out = win[:, bank, 0:WC] if part == 0 else win[:, bank, WC:2 * WC]
                        mm = pe.matmul(out, S[:, slot, part, :, u], M[:, slot, :, u],
                                       start=(first and u == 0 and part == 0),
                                       stop=(u == CH - 1 and part in (0, 3)), skip_group_check=True)
                return mm

            regs = [pe.alloc_register(f"pe_bound{r}") for r in range(8)]
            load_ranges(pe, regs, 0)
            more = pe.alloc_register("pe_more")
            pe.reg_mov(more, 0)
            with pe.Fori(0, NT) as j:
                with pe.Fori(0, WPT // 4) as q:
                    w0 = j * WPT + q * 4
                    for b in range(4):
                        t, end = window_range(pe, regs, b)
                        if b == 3:
                            load_ranges(pe, regs, w0 + 4)
                        pe.wait_ge(s_evac, 2 * w0 + 2 * b + 1)
                        pe.wait_ge(s_made, w0 + b + 1)
                        products(b % 2, b, range(CH - 1), True)
                        with pe.If(end > t + CH):
                            with pe.Fori(t + CH, end, CH):
                                pe.reg_add(more, more, 1)
                                pe.wait_ge(s_xmade, pe.snap(more))
                                products(2, b, range(CH), False).then_inc(s_xused, 1)
                        products(b % 2, b, range(CH - 1, CH), False).then_inc(s_built, 1)
                pe.wait_ge(s_ct, j * len(TG) + len(TG))
                pe.wait_ge(s_evac, j * (2 * WPT) + 2 * WPT + EVAC0 - 1)
                for g, (a, b) in enumerate(TG):
                    for k in range(a, b):
                        mm = pe.transpose(tp[:, g, k - a, :], Cblk[:, k, :], ident[:, :])
                    mm.then_inc(s_tp, 1)

        @block.scalar
        def _(act):
            act.preload_act_table(ACT.Copy)
            with act.Fori(0, NT) as j:
                act.wait_ge(s_cst, j * 16 + 1)
                act.wait_ge(s_wst, j * 16 + 1)
                with act.Fori(0, WPT // 4) as q:
                    w0 = j * WPT + q * 4
                    for b in range(4):
                        at = q * (4 * WIN) + b * WIN
                        act.wait_ge(s_built, w0 + b + 3)
                        nc.scalar.activation(Cblk[:, :, bass.ds(at, WIN)],
                                             win[:, b, 0:WC].rearrange("p (k d) -> p k d", d=WIN),
                                             ACT.Copy, scale=0.5).then_inc(s_evac, 1)
                        nc.scalar.activation(Wblk[:, :, bass.ds(at, WIN)],
                                             win[:, b, WC:2 * WC].rearrange("p (k d) -> p k d", d=WIN),
                                             ACT.Copy).then_inc(s_evac, 1)
                for g, (a, b) in enumerate(TG):
                    act.wait_ge(s_tp, j * len(TG) + g + 1)
                    nc.scalar.activation(CT[:, bass.ds(j, 1), a * P:b * P],
                                         tp[:, g, 0:b - a, :].rearrange("p k d -> p (k d)").unsqueeze(1), ACT.Copy,
                                         accum_out=indeg[:, bass.ds(j * len(TG) + g, 1)]).then_inc(s_ct, 1)


def layernorm_relu(nc, do, act_do, x, out, stat, scratch, eps=LN_EPS):
    mean, var, rstd = stat[:, 0, :], stat[:, 1, :], stat[:, 2, :]
    do(nc.vector.tensor_reduce(mean, x, AX.X, ALU.add))
    do(nc.vector.tensor_scalar(mean, mean, 1.0 / D, None, ALU.mult))
    do(nc.vector.tensor_tensor(out, x, mean.unsqueeze(2).to_broadcast([P, NT, D]), ALU.subtract))
    do(nc.vector.tensor_tensor(scratch, out, out, ALU.mult))
    do(nc.vector.tensor_reduce(var, scratch, AX.X, ALU.add))
    do(nc.vector.tensor_scalar(var, var, 1.0 / D, eps, ALU.mult, ALU.add))
    act_do()
    do(nc.vector.reciprocal(rstd, rstd))
    do(nc.vector.scalar_tensor_tensor(out, out, 0.0, rstd.unsqueeze(2).to_broadcast([P, NT, D]), ALU.max, ALU.mult))


def propagate(nc, x_in, CT, indeg, x_out_d):
    with ExitStack() as ctx:
        m = Scope(nc, ctx, "layer0")
        x = m.sb("x", [P, NT, D], F32)
        h = m.sb("h", [P, NT, D], F32)
        g = m.sb("g", [P, NT, D], F32)
        U = m.sb("U", [P, 2, NT, 2, D], F16)
        one = m.sb("one", [P, 1], F16)
        stat = m.sb("stat", [P, 3, NT], F32)
        dc = m.sb("dc", [P, NT], F32)
        dr = m.sb("dr", [P, NT], F32)
        gd = m.sb("gd", [P, NT], F32)
        a = m.sb("a", [P, NT], F32)
        c = m.sb("c", [P, NT], F32)
        lo, s, v, d = (h[:, i * RING:(i + 1) * RING, :] for i in range(4))
        acc = m.ps("acc", [P, RING, 512])
        deg = m.ps("deg", [P, 512])
        s_x = m.sem("x_loaded")
        s_one = m.sem("one_made")
        s_deg = m.sem("out_degrees")
        s_v = m.sem("dve_chain")
        s_var = m.sem("root_wanted")
        s_root = m.sem("root_made")
        s_u = m.sem("part_pairs_made")
        s_acc = m.sem("products_done")
        s_lo = m.sem("low_sums_out")
        s_s = m.sem("sums_made")
        s_new = m.sem("values_made")
        s_hi = m.sem("high_parts_made")
        s_d = m.sem("rests_made")
        s_fin = m.sem("x_updated")
        s_st = m.sem("x_stored")
        block = ctx.enter_context(nc.Block())

        @block.sync
        def _(sp):
            sp.dma_start(x[:, :, :], x_in.rearrange("(k p) f -> p k f", p=P)).then_inc(s_x, 16)
            sp.wait_ge(s_fin, NT)
            sp.dma_start(x_out_d.rearrange("(k p) f -> p k f", p=P), x[:, :, :]).then_inc(s_st, 16)
            sp.wait_ge(s_st, 16)

        @block.vector
        def _(dve):
            do = Chain(dve, s_v)

            def root(n):
                def wait():
                    dve.sem_inc(s_var, 1)
                    dve.wait_ge(s_root, n)
                return wait

            nc.vector.memset(one[:, :], 1.0).then_inc(s_one, 1)
            dve.wait_ge(s_x, 16)
            layernorm_relu(nc, do, root(1), x[:, :, :], h[:, :, :], stat, g[:, :, :])
            do(nc.vector.tensor_reduce(dc[:, :], indeg[:, :].rearrange("p (j g) -> p j g", g=len(TG)), AX.X, ALU.add))
            dve.wait_ge(s_deg, 1)
            do(nc.vector.tensor_scalar(dr[:, :], deg[:, 0:NT], 2.0, 1.0, ALU.mult, ALU.max))
            do(nc.vector.tensor_scalar(dc[:, :], dc[:, :], 2.0, 1.0, ALU.mult, ALU.max))
            root(3)()
            do(nc.vector.reciprocal(dc[:, :], dc[:, :]))
            do(nc.vector.reciprocal(dr[:, :], dr[:, :]))
            do(nc.vector.tensor_scalar(gd[:, :], dc[:, :], ALPHA * USCALE, None, ALU.mult))
            do(nc.vector.scalar_tensor_tensor(a[:, :], dr[:, :], 2.0 * BETA, dc[:, :], ALU.mult, ALU.mult))
            do(nc.vector.tensor_scalar(c[:, :], dr[:, :], 2.0 * BETA / USCALE / THETA, None, ALU.mult))
            do(nc.vector.tensor_tensor(g[:, :, :], h[:, :, :], gd[:, :].unsqueeze(2).to_broadcast([P, NT, D]), ALU.mult))
            do(nc.vector.scalar_tensor_tensor(x[:, :, :], h[:, :, :], ALPHA / THETA, x[:, :, :], ALU.mult, ALU.add))
            do(nc.vector.tensor_scalar(h[:, :, :], g[:, :, :], 1.0 / ALPHA, None, ALU.mult))
            do(nc.vector.tensor_copy(U[:, 0, :, 0, :], h[:, :, :]))
            do(nc.vector.tensor_tensor(h[:, :, :], h[:, :, :], U[:, 0, :, 0, :], ALU.subtract))
            do(nc.vector.tensor_scalar(U[:, 0, :, 1, :], h[:, :, :], LOSCALE, None, ALU.mult))
            dve.sem_inc(s_u, NT)

            def step(nxt, at, n):
                for k in range(NT):
                    dve.wait_ge(s_lo, n + k + 1 + RING)
                    nc.vector.tensor_tensor(s[:, k % RING, :], lo[:, k % RING, :], acc[:, k % RING, 0:D], ALU.add).then_inc(s_s, 1)
                    dve.wait_ge(s_s, n + k + 1 + RING)
                    if nxt is None:
                        nc.vector.scalar_tensor_tensor(x[:, k, :], s[:, k % RING, :], c[:, k:k + 1], x[:, k, :],
                                                       ALU.mult, ALU.add).then_inc(s_fin, 1)
                        continue
                    nc.vector.scalar_tensor_tensor(v[:, k % RING, :], s[:, k % RING, :], a[:, k:k + 1], g[:, k, :],
                                                   ALU.mult, ALU.add).then_inc(s_new, 1)
                    dve.wait_ge(s_hi, n + k + 1)
                    nc.vector.tensor_tensor(d[:, k % RING, :], v[:, k % RING, :], U[:, nxt, k, 0, :], ALU.subtract).then_inc(s_d, 1)

            with dve.Fori(0, K_STEPS - 2, 2) as i:
                for b in range(2):
                    step(1 - b, b, i * NT + b * NT)
            step(1, 0, (K_STEPS - 2) * NT)
            step(None, 1, (K_STEPS - 1) * NT)

        @block.scalar
        def _(act):
            act.wait_ge(s_var, 1)
            nc.scalar.sqrt(stat[:, 2, :], stat[:, 1, :]).then_inc(s_root, 1)
            act.wait_ge(s_var, 2)
            nc.scalar.sqrt(dc[:, :], dc[:, :]).then_inc(s_root, 1)
            nc.scalar.sqrt(dr[:, :], dr[:, :]).then_inc(s_root, 1)

            def step(nxt, n):
                for k in range(NT + 1):
                    if k < NT:
                        act.wait_ge(s_acc, n + k + 1)
                        nc.scalar.activation(lo[:, k % RING, :], acc[:, k % RING, D:2 * D], ACT.Copy,
                                             scale=1.0 / LOSCALE).then_inc(s_lo, 1)
                        if nxt is not None:
                            act.wait_ge(s_new, n + k + 1)
                            nc.scalar.activation(U[:, nxt, k, 0, :], v[:, k % RING, :], ACT.Copy).then_inc(s_hi, 1)
                    if k >= 1 and nxt is not None:
                        act.wait_ge(s_d, n + k)
                        nc.scalar.activation(U[:, nxt, k - 1, 1, :], d[:, (k - 1) % RING, :], ACT.Copy,
                                             scale=LOSCALE).then_inc(s_u, 1)

            with act.Fori(0, K_STEPS - 2, 2) as i:
                for b in range(2):
                    step(1 - b, i * NT + b * NT)
            step(1, (K_STEPS - 2) * NT)
            step(None, (K_STEPS - 1) * NT)

        @block.tensor
        def _(pe):
            pe.sem_inc(s_lo, RING)
            pe.sem_inc(s_s, RING)
            pe.wait_ge(s_one, 1)
            for k in range(NT):
                for t in range(NT):
                    mm = pe.matmul(deg[:, k:k + 1], CT[:, t, k * P:(k + 1) * P], one[:, :],
                                   start=(t == 0), stop=(t == NT - 1))
            mm.then_inc(s_deg, 1)

            def step(cur, n):
                for k in range(NT):
                    pe.wait_ge(s_lo, n + k + 1)
                    pe.wait_ge(s_s, n + k + 1)
                    for t in range(NT):
                        if k == 0:
                            pe.wait_ge(s_u, n + t + 1)
                        mm = pe.matmul(acc[:, k % RING, 0:2 * D], CT[:, t, k * P:(k + 1) * P],
                                       U[:, cur, t, :, :].rearrange("p a f -> p (a f)"),
                                       start=(t == 0), stop=(t == NT - 1))
                    mm.then_inc(s_acc, 1)

            with pe.Fori(0, K_STEPS - 2, 2) as i:
                for b in range(2):
                    step(b, i * NT + b * NT)
            step(0, (K_STEPS - 2) * NT)
            step(1, (K_STEPS - 1) * NT)


class EdgeStart:

    def __init__(self, agg, dstF, dstI, ew, tab, nodes, nodeno, Wa, hot, z, y, G):
        self.agg, self.dstF, self.dstI, self.ew, self.tab = agg, dstF, dstI, ew, tab
        self.nodes, self.nodeno, self.Wa, self.hot, self.z, self.y, self.G = nodes, nodeno, Wa, hot, z, y, G


def node_terms(nc, x_in, dst_cols, w_cols, We, be, Wn, bn, tab_d, P_d, x, Q3, start):
    D2 = 2 * D
    with ExitStack() as ctx:
        m = Scope(nc, ctx, "terms1")
        h = m.sb("h", [P, NT, D], F32)
        stat = m.sb("stat", [P, 3, NT], F32)
        rowno = m.sb("rowno", [P, P], F32)
        colno = m.sb("colno", [P, P], F32)
        ident = m.sb("ident", [P, P], F32)
        W = m.sb("W", [D, 2, D2], F32)
        bias = m.sb("bias", [P, D2], F32)
        hT = m.sb("hT", [D, 2, P], F32)
        Pn = m.sb("Pn", [P, NT, D2], F32)
        Qf = m.sb("Qf", [P, NT, D2], F32)
        tp = m.ps("tp", [P, 2, 512])
        prod = m.ps("prod", [P, 4, 512])
        s_x = m.sem("x_loaded")
        s_w = m.sem("weights_loaded")
        s_c = m.sem("iotas_made")
        s_id = m.sem("identity_made")
        s_v = m.sem("dve_chain")
        s_var = m.sem("root_wanted")
        s_root = m.sem("root_made")
        s_h = m.sem("h_made")
        s_tp = m.sem("h_turned")
        s_hT = m.sem("turned_h_out")
        s_pr = m.sem("products_done")
        s_P = m.sem("source_terms_out")
        s_Q = m.sem("target_terms_out")
        s_st = m.sem("source_terms_stored")
        s_tab = m.sem("edge_tables_loaded")
        s_dst = m.sem("targets_loaded")
        block = ctx.enter_context(nc.Block())

        @block.sync
        def _(sp):
            sp.dma_start(x[:, :, :], x_in.rearrange("(k p) f -> p k f", p=P)).then_inc(s_x, 16)
            for i, (w, b) in enumerate(((We, be), (Wn, bn))):
                sp.dma_start(W[:, 0, i * D:(i + 1) * D], w[0:D, :]).then_inc(s_w, 16)
                sp.dma_start(W[:, 1, i * D:(i + 1) * D], w[D:2 * D, :]).then_inc(s_w, 16)
                sp.dma_start(bias[:, i * D:(i + 1) * D],
                             b.rearrange("(o f) -> o f", o=1).to_broadcast([P, D])).then_inc(s_w, 16)
            sp.dma_start(start.tab[:, :, :], tab_d[(QG - 1) * P:(QG - 1) * P + NT + 1, :].rearrange("(o q) b -> o q b", o=1)).then_inc(s_tab, 16)
            sp.dma_start(start.dstI[:, :], dst_cols).then_inc(s_dst, 16)
            sp.dma_start(start.ew[:, :], w_cols).then_inc(s_tab, 16)
            sp.dma_start(start.Wa[:, 0:D], We[2 * D:, :]).then_inc(s_tab, 16)
            sp.dma_start(start.Wa[:, D:], Wn[2 * D:, :]).then_inc(s_tab, 16)
            sp.wait_ge(s_tab, 64)
            sp.wait_ge(s_P, NT)
            sp.dma_start(P_d.rearrange("(k p) f -> p k f", p=P), Pn[:, :, :]).then_inc(s_st, 16)
            sp.wait_ge(s_st, 16)

        @block.gpsimd
        def _(pool):
            nc.gpsimd.iota(colno[:, :], pattern=[[1, P]], base=0, channel_multiplier=0,
                           allow_small_or_imprecise_dtypes=True).then_inc(s_c, 1)
            nc.gpsimd.iota(rowno[:, :], pattern=[[0, P]], base=0, channel_multiplier=1,
                           allow_small_or_imprecise_dtypes=True).then_inc(s_c, 1)
            nc.gpsimd.iota(start.nodes[:, :], pattern=[[1, NP]], base=0, channel_multiplier=0,
                           allow_small_or_imprecise_dtypes=True)
            nc.gpsimd.iota(start.nodeno[:, :], pattern=[[P, NT]], base=0, channel_multiplier=1,
                           allow_small_or_imprecise_dtypes=True)
            nc.gpsimd.memset(start.agg[:, :, :], 0.0)
            nc.gpsimd.memset(start.z[:, :, :, :], 0.0)
            nc.gpsimd.memset(start.y[:, :, :, :], 0.0)
            nc.gpsimd.memset(start.hot[:, :, :, :], 0.0)
            nc.gpsimd.memset(start.G[:, :, :, 0:D + 1], 0.0)
            nc.gpsimd.memset(start.G[:, :, :, D + 1:D + 2], 1.0)
            pool.wait_ge(s_dst, 16)
            nc.gpsimd.tensor_copy(start.dstF[:, :], start.dstI[:, :])

        @block.vector
        def _(dve):
            do = Chain(dve, s_v)

            def root():
                dve.sem_inc(s_var, 1)
                dve.wait_ge(s_root, 1)

            dve.wait_ge(s_c, 2)
            nc.vector.tensor_tensor(ident[:, :], rowno[:, :], colno[:, :], ALU.is_equal).then_inc(s_id, 1)
            dve.wait_ge(s_x, 16)
            layernorm_relu(nc, do, root, x[:, :, :], h[:, :, :], stat, Qf[:, :, 0:D])
            dve.sem_inc(s_h, 1)
            do(nc.vector.tensor_tensor(x[:, :, :], x[:, :, :], h[:, :, :], ALU.add))
            dve.wait_ge(s_w, 96)
            for k in range(NT):
                dve.wait_ge(s_P, k + 1)
                nc.vector.tensor_tensor(Qf[:, k, :], prod[:, k % 4, D2:2 * D2], bias[:, :], ALU.add).then_inc(s_Q, 1)
                if k % 5 == 4:
                    dve.wait_ge(s_Q, k + 1)
                    q = slice(k - 4, k + 1)
                    do(nc.vector.tensor_copy(Q3[:, q, 0, :], Qf[:, q, :]))
                    do(nc.vector.tensor_tensor(Qf[:, q, :], Qf[:, q, :], Q3[:, q, 0, :], ALU.subtract))
                    do(nc.vector.tensor_copy(Q3[:, q, 1, :], Qf[:, q, :]))
                    do(nc.vector.tensor_tensor(Qf[:, q, :], Qf[:, q, :], Q3[:, q, 1, :], ALU.subtract))
                    do(nc.vector.tensor_copy(Q3[:, q, 2, :], Qf[:, q, :]))

        @block.scalar
        def _(act):
            act.wait_ge(s_var, 1)
            nc.scalar.sqrt(stat[:, 2, :], stat[:, 1, :]).then_inc(s_root, 1)
            for k in range(NT + 1):
                if k < NT:
                    act.wait_ge(s_tp, k + 1)
                    nc.scalar.activation(hT[:, k % 2, :], tp[0:D, k % 2, 0:P], ACT.Copy).then_inc(s_hT, 1)
                if k >= 1:
                    act.wait_ge(s_pr, k)
                    nc.scalar.activation(Pn[:, k - 1, :], prod[:, (k - 1) % 4, 0:D2], ACT.Copy).then_inc(s_P, 1)

        @block.tensor
        def _(pe):
            pe.wait_ge(s_id, 1)
            pe.wait_ge(s_w, 96)
            pe.wait_ge(s_h, 1)
            for k in range(NT + 1):
                if k < NT:
                    if k >= 2:
                        pe.wait_ge(s_hT, k - 1)
                    pe.transpose(tp[0:D, k % 2, 0:P], h[:, k, :], ident[:, :]).then_inc(s_tp, 1)
                if k >= 1:
                    pe.wait_ge(s_hT, k)
                    if k >= 5:
                        pe.wait_ge(s_Q, k - 4)
                    pe.matmul(prod[:, (k - 1) % 4, 0:2 * D2], hT[:, (k - 1) % 2, :],
                              W[:, :, :].rearrange("p s f -> p (s f)"), start=True, stop=True).then_inc(s_pr, 1)


def gated_edges(nc, x_in, src_cols, dst_cols, w_cols, attr, We, be, Wn, bn, tab_d, row_d, P_d, x, wdeg):
    D2 = 2 * D
    with ExitStack() as ctx:
        m = Scope(nc, ctx, "layer1")
        Q3 = m.sb("Q3", [P, NT, 3, D2], BF16)
        agg = m.sb("agg", [P, NT, D + 2], F32)
        dstF = m.sb("dstF", [P, ETC], F32)
        dstI = m.sb("dstI", [P, ETC], I32)
        ew = m.sb("ew", [P, ETC], F32)
        tab = m.sb("tab", [1, NT + 1, 2], I16)
        nodes = m.sb("nodes", [P, NP], F32)
        nodeno = m.sb("nodeno", [P, NT], F32)
        Wa = m.sb("Wa", [DE, D2], F32)
        count = m.sb("count", [P, NT], F32)
        srcs = m.sb("srcs", [P, 2, SE], I32)
        at = m.sb("at", [DE, 2, SE * P], F32)
        rows = m.sb("rows", [P, 2, SE * P], I16)
        R = m.sb("R", [P, 2, SE, D2], F32)
        hot = m.sb("hot", [P, 2, SE, P], F32)
        hotT = m.sb("hotT", [P, 2, SE, P], BF16)
        z = m.sb("z", [P, 2, SE, D2], F32)
        y = m.sb("y", [P, 2, SE, D2], F32)
        G = m.sb("G", [P, 2, SE, D + 2], F32)
        start = EdgeStart(agg, dstF, dstI, ew, tab, nodes, nodeno, Wa, hot, z, y, G)
        node_terms(nc, x_in, dst_cols, w_cols, We, be, Wn, bn, tab_d, P_d, x, Q3, start)
        zp = [m.ps(f"zp{h}", [P, SE // 2, 512]) for h in range(2)]
        acc = [m.ps(f"acc{h}", [P, 512]) for h in range(2)]
        s_at = [m.sem(f"attributes_loaded{h}") for h in range(2)]
        s_rows = [m.sem(f"target_rows_loaded{h}") for h in range(2)]
        s_ix = [m.sem(f"sources_loaded{h}") for h in range(2)]
        s_R = [m.sem(f"source_terms_gathered{h}") for h in range(2)]
        s_there = m.sem("gathers_arrived")
        s_taken = m.sem("waits_taken")
        s_hot = m.sem("onehots_made")
        s_hT = m.sem("turned_onehots_made")
        s_att = m.sem("attribute_products_done")
        s_z = m.sem("z_summed")
        s_add = m.sem("z_out")
        s_abs = m.sem("magnitudes_made")
        s_e = m.sem("exponentials_made")
        s_l = m.sem("logarithms_made")
        s_ms = m.sem("gate_log_and_message_made")
        s_g = m.sem("gates_made")
        s_G = m.sem("gated_messages_made")
        s_seg = m.sem("step_aggregated")
        s_acc = m.sem("sums_accumulated")
        s_v = m.sem("dve_chain")
        block = ctx.enter_context(nc.Block())

        def first_range(eng):
            regs = [eng.alloc_register(f"layer1_bound{r}_{eng.engine.name}") for r in range(2)]
            eng.load(regs, tab[0:1, 0:1, :])
            return regs

        def ranges(eng, regs, j):
            why = "edge_ranges clamps the tables"
            t0 = nc.s_assert_within(eng.snap(regs[0]), 0, TCLAMP, skip_runtime_bounds_check_because=why)
            end = nc.s_assert_within(eng.snap(regs[1]), 1, TCLAMP + 1, skip_runtime_bounds_check_because=why)
            eng.load(regs, tab[0:1, bass.ds(j + 1, 1), :])
            return t0, end


        @block.sync
        def _(sp):
            n = sp.alloc_register("sp_steps")
            sp.reg_mov(n, 0)
            bounds = first_range(sp)
            with sp.Fori(0, NT) as j:
                t0, end = ranges(sp, bounds, j)
                with sp.Fori(t0, end, 2 * SE) as t:
                    p = sp.snap(n)
                    for h in range(2):
                        first = t + h * SE
                        sp.wait_ge(s_hT, p + h + 1)
                        sp.sem_inc(s_taken, 1)
                        sp.dma_start(rows[:, h, :], row_d[:, bass.ds(first * P, SE * P)].to_broadcast([P, SE * P])).then_inc(s_rows[h], 16)
                        sp.wait_ge(s_att, p + h + 1)
                        sp.sem_inc(s_taken, 1)
                        sp.dma_start(at[:, h, :], attr[:, bass.ds(first * P, SE * P)]).then_inc(s_at[h], 16)
                        sp.wait_ge(s_there, p + h + 1)
                        sp.sem_inc(s_taken, 1)
                        sp.dma_start(srcs[:, h, :], src_cols[:, bass.ds(first, SE)]).then_inc(s_ix[h], 16)
                    sp.reg_add(n, n, 2)

        @block.gpsimd
        def _(pool):
            n = pool.alloc_register("pool_steps")
            pool.reg_mov(n, 0)
            loads = pool.alloc_register("pool_loads")
            pool.reg_mov(loads, 0)
            bounds = first_range(pool)
            with pool.Fori(0, NT) as j:
                t0, end = ranges(pool, bounds, j)
                with pool.Fori(t0, end, 2 * SE):
                    p = pool.snap(n)
                    pool.reg_add(n, n, 2)
                    pool.reg_add(loads, loads, 16)
                    loaded = pool.snap(loads)
                    for h in range(2):
                        pool.wait_ge(s_ix[h], loaded)
                        pool.sem_inc(s_taken, 1)
                        pool.wait_ge(s_add, p + h + 1)
                        pool.sem_inc(s_taken, 1)
                        for u in range(SE):
                            nc.gpsimd.indirect_dma_start(
                                R[:, h, u, :], None, P_d,
                                bass.IndirectOffsetOnAxis(ap=srcs[:, h, u:u + 1], axis=0)).then_inc(s_R[h], 16)

        @block.vector
        def _(dve):
            do = Chain(dve, s_v)
            n = dve.alloc_register("dve_steps")
            dve.reg_mov(n, 0)
            loads = dve.alloc_register("dve_loads")
            dve.reg_mov(loads, 0)
            gathered = dve.alloc_register("dve_gathered")
            dve.reg_mov(gathered, 0)
            last = dve.alloc_register("dve_last_node_tile")
            dve.reg_mov(last, 0)

            def turned(h, j, loaded):
                dve.wait_ge(s_rows[h], loaded)
                nc.vector.tensor_scalar(hotT[:, h, :, :].rearrange("p u e -> p (u e)"), rows[:, h, :],
                                        nodeno[:, bass.ds(j, 1)], None, ALU.is_equal).then_inc(s_hT, 1)

            def onehots(h, t, j):
                nc.vector.tensor_copy(G[:, h, :, D:D + 1], ew[:, bass.ds(t + h * SE, SE)].unsqueeze(2))
                nc.vector.tensor_tensor(hot[:, h, :, :],
                                        nodes[:, bass.ds(j * P, P)].unsqueeze(1).to_broadcast([P, SE, P]),
                                        dstF[:, bass.ds(t + h * SE, SE)].unsqueeze(2).to_broadcast([P, SE, P]),
                                        ALU.is_equal).then_inc(s_hot, 1)

            def add(h, p, arrived):
                dve.wait_ge(s_R[h], arrived)
                dve.sem_inc(s_there, 1)
                dve.wait_ge(s_z, p + 1)
                dve.wait_ge(s_G, p + 1)
                nc.vector.tensor_tensor(z[:, h, :, :].rearrange("p (b u) f -> p b (u f)", b=SE // 2),
                                        zp[h][:, :, 0:2 * D2],
                                        R[:, h, :, :].rearrange("p (b u) f -> p b (u f)", b=SE // 2),
                                        ALU.add).then_inc(s_add, 1)

            def logs(h, p):
                dve.wait_ge(s_l, p + 2)
                nc.vector.scalar_tensor_tensor(z[:, h, :, D:], z[:, h, :, D:], 0.0, y[:, h, :, D:],
                                               ALU.max, ALU.add)
                nc.vector.scalar_tensor_tensor(z[:, h, :, 0:D], z[:, h, :, 0:D], 0.0, y[:, h, :, 0:D],
                                               ALU.min, ALU.subtract).then_inc(s_ms, 1)

            def gated(h, p):
                dve.wait_ge(s_g, p + 3)
                nc.vector.tensor_tensor(G[:, h, :, 0:D], y[:, h, :, 0:D], z[:, h, :, D:],
                                        ALU.mult).then_inc(s_G, 1)

            def accumulate(h, p, j):
                dve.wait_ge(s_seg, p + 3)
                into = agg[:, bass.ds(j, 1), :]
                nc.vector.tensor_tensor(into, into, acc[h][:, 0:D + 2].unsqueeze(1), ALU.add).then_inc(s_acc, 1)

            bounds = first_range(dve)
            with dve.Fori(0, NT) as j:
                t0, end = ranges(dve, bounds, j)
                with dve.Fori(t0, end, 2 * SE) as t:
                    p = dve.snap(n)
                    before = nc.s_assert_within(dve.snap(last), 0, NT - 1,
                                                skip_runtime_bounds_check_because="zero or a past j of the loop")
                    dve.reg_add(loads, loads, 16)
                    loaded = dve.snap(loads)
                    dve.reg_add(gathered, gathered, 16 * SE)
                    arrived = dve.snap(gathered)
                    for h in range(2):
                        turned(h, j, loaded)
                    gated(0, p - 2)
                    for h in range(2):
                        add(h, p + h, arrived)
                        logs(1 - h, p + (h - 1))
                        accumulate(h, p + (h - 2), before)
                        onehots(h, t, j)
                        if h == 0:
                            gated(1, p - 1)
                    dve.reg_mov(last, j)
                    dve.reg_add(n, n, 2)
            end = dve.snap(n)
            gated(0, end - 2)
            logs(1, end - 1)
            accumulate(0, end - 2, NT - 1)
            gated(1, end - 1)
            dve.wait_ge(s_acc, end + 3)
            accumulate(1, end - 1, NT - 1)
            dve.wait_ge(s_acc, end + 4)
            cnt = count[:, :]
            do(nc.vector.tensor_copy(wdeg[:, :], agg[:, :, D]))
            do(nc.vector.tensor_scalar(cnt, agg[:, :, D + 1], 1.0, None, ALU.max))
            do(nc.vector.reciprocal(cnt, cnt))
            do(nc.vector.tensor_tensor(agg[:, :, 0:D], agg[:, :, 0:D], cnt.unsqueeze(2).to_broadcast([P, NT, D]), ALU.mult))
            do(nc.vector.tensor_tensor(x[:, :, :], x[:, :, :], agg[:, :, 0:D], ALU.add))

        @block.scalar
        def _(act):
            act.preload_act_table_set("natural_log_exp_and_others")
            act.sem_inc(s_l, 1)
            act.sem_inc(s_g, 1)
            n = act.alloc_register("act_steps")
            act.reg_mov(n, 0)

            def gates(h, p):
                act.wait_ge(s_ms, p + 2)
                nc.scalar.activation(y[:, h, :, 0:D], z[:, h, :, 0:D], ACT.Exp).then_inc(s_g, 1)

            def magnitude(h, p):
                act.wait_ge(s_add, p + 3)
                nc.scalar.activation(y[:, h, :, :], z[:, h, :, :], ACT.Abs).then_inc(s_abs, 1)

            def softplus(h, p):
                act.wait_ge(s_abs, p + 1)
                nc.scalar.activation(y[:, h, :, :], y[:, h, :, :], ACT.Exp, scale=-1.0).then_inc(s_e, 1)
                act.wait_ge(s_e, p + 1)
                nc.scalar.activation(y[:, h, :, :], y[:, h, :, :], ACT.Ln, bias=1.0).then_inc(s_l, 1)

            bounds = first_range(act)
            with act.Fori(0, NT) as j:
                t0, end = ranges(act, bounds, j)
                with act.Fori(t0, end, 2 * SE):
                    p = act.snap(n)
                    for h in range(2):
                        magnitude(h, p + h)
                        gates(1 - h, p + (h - 1))
                        softplus(h, p + h)
                    act.reg_add(n, n, 2)
            gates(1, act.snap(n) - 1)

        @block.tensor
        def _(pe):
            pe.sem_inc(s_add, 2)
            pe.sem_inc(s_there, 2)
            pe.sem_inc(s_att, 2)
            pe.sem_inc(s_hT, 2)
            pe.sem_inc(s_acc, 2)
            pe.sem_inc(s_hot, 2)
            n = pe.alloc_register("pe_steps")
            pe.reg_mov(n, 0)
            loads = pe.alloc_register("pe_loads")
            pe.reg_mov(loads, 0)

            def sums(h, p, loaded, j):
                pe.wait_ge(s_add, p + 1)
                pe.wait_ge(s_at[h], loaded)
                for u in range(SE):
                    mm = pe.matmul(zp[h][:, u // 2, u % 2 * D2:(u % 2 + 1) * D2], at[:, h, u * P:(u + 1) * P],
                                   Wa[:, :], start=(u % 2 == 0), stop=False, skip_group_check=True)
                mm.then_inc(s_att, 1)
                pe.wait_ge(s_hT, p + 3)
                for u in range(SE):
                    for part in range(3):
                        mm = pe.matmul(zp[h][:, u // 2, u % 2 * D2:(u % 2 + 1) * D2], hotT[:, h, u, :],
                                       Q3[:, bass.ds(j, 1), part, :].rearrange("p o f -> p (o f)"),
                                       start=False, stop=(part == 2), skip_group_check=True)
                mm.then_inc(s_z, 1)

            def aggregate(h, p):
                pe.wait_ge(s_hot, p + 3)
                pe.wait_ge(s_acc, p + 3)
                pe.wait_ge(s_G, p + 3)
                for u in range(SE):
                    mm = pe.matmul(acc[h][:, 0:D + 2], hot[:, h, u, :], G[:, h, u, :],
                                   start=(u == 0), stop=(u == SE - 1))
                mm.then_inc(s_seg, 1)

            bounds = first_range(pe)
            with pe.Fori(0, NT) as j:
                t0, end = ranges(pe, bounds, j)
                with pe.Fori(t0, end, 2 * SE):
                    p = pe.snap(n)
                    pe.reg_add(loads, loads, 16)
                    loaded = pe.snap(loads)
                    for h in range(2):
                        sums(h, p + h, loaded, j)
                        aggregate(h, p + (h - 2))
                    pe.reg_add(n, n, 2)
            for h in range(2):
                aggregate(h, pe.snap(n) + (h - 2))


def residual_gcn(nc, x, C_d, layers):
    with ExitStack() as ctx:
        m = Scope(nc, ctx, "layer2")
        C = m.sb("C", [P, NT, NT, P], F16)
        h = m.sb("h", [P, NT, D], F32)
        cv = m.sb("cv", [P, NT, D], F32)
        U = m.sb("U", [P, NT, 3, D], BF16)
        ident = m.sb("ident", [P, P], F32)
        mask = m.sb("mask", [P, 2, P], F32)
        W = m.sb("W", [D, 2, D], F32)
        vec = m.sb("vec", [P, 2, 4, D], F32)
        stat = m.sb("stat", [P, 3, NT], F32)
        hT = m.sb("hT", [D, 2, P], F32)
        rest = m.sb("rest", [P, 2, D], F32)
        part = m.sb("part", [P, 2, D], F32)
        sq = U[:, :, :, :].rearrange("p k a f -> p (k a f)").bitcast(F32)[:, 0:NT * D].rearrange("p (k f) -> p k f", f=D)
        mu = m.sb("mu", [P, D], F32)
        sd = m.sb("sd", [P, D], F32)
        tp = m.ps("tp", [P, 4, 512])
        acc = m.ps("acc", [P, 4, 512])
        tot = tp[:, 2:4, :]
        s_par = m.sem("parameters_loaded")
        s_C = [m.sem(f"C_loaded{q}") for q in range(5)]
        s_c = m.sem("iotas_made")
        s_id = m.sem("identity_made")
        s_v = m.sem("dve_chain")
        s_a = m.sem("act_chain")
        s_var = m.sem("root_wanted")
        s_root = m.sem("root_made")
        s_h = m.sem("h_made")
        s_tp = m.sem("h_turned")
        s_hT = m.sem("turned_h_out")
        s_pr = m.sem("hW_done")
        s_u0 = m.sem("first_parts_made")
        s_r = m.sem("rests_made")
        s_u1 = m.sem("second_parts_made")
        s_u2 = m.sem("third_parts_made")
        s_acc = m.sem("aggregates_done")
        s_p2 = m.sem("third_sums_out")
        s_cv = m.sem("conv_tiles_made")
        s_sum = m.sem("column_sums_done")
        s_xc = m.sem("centred")
        s_sq = m.sem("squares_made")
        s_sqs = m.sem("squares_summed")
        block = ctx.enter_context(nc.Block())
        NL = len(layers)

        @block.sync
        def _(sp):
            for i, (w, b, gw, gb, ga) in enumerate(layers):
                sp.dma_start(W[:, i, :], w).then_inc(s_par, 16)
                for q, vct in enumerate((b, gw, gb, ga)):
                    sp.dma_start(vec[:, i, q, :], vct.rearrange("(o f) -> o f", o=1).to_broadcast([P, D])).then_inc(s_par, 16)
            for j in range(NT):
                sp.dma_start(C[:, j, :, :].rearrange("p k d -> p (k d)"), C_d[j, :, :]).then_inc(s_C[j // 5], 16)

        @block.gpsimd
        def _(pool):
            nc.gpsimd.iota(mask[:, 0, :], pattern=[[1, P]], base=0, channel_multiplier=0,
                           allow_small_or_imprecise_dtypes=True).then_inc(s_c, 1)
            nc.gpsimd.iota(mask[:, 1, :], pattern=[[0, P]], base=0, channel_multiplier=1,
                           allow_small_or_imprecise_dtypes=True).then_inc(s_c, 1)

        @block.vector
        def _(dve):
            do = Chain(dve, s_v)

            def root(n):
                def wait():
                    dve.sem_inc(s_var, 1)
                    dve.wait_ge(s_root, n)
                return wait

            dve.wait_ge(s_c, 2)
            do(nc.vector.tensor_tensor(ident[:, :], mask[:, 0, :], mask[:, 1, :], ALU.is_equal))
            do(nc.vector.memset(mask[:, 0, :], 1.0))
            nc.vector.tensor_scalar(mask[:, 1, :], mask[:, 1, :], float(LAST), None, ALU.is_lt).then_inc(s_id, 1)
            layernorm_relu(nc, do, root(1), x[:, :, :], h[:, :, :], stat, cv[:, :, :])
            dve.wait_ge(s_par, 16 * 5 * NL)
            for i in range(NL):
                base = i * NT
                dve.sem_inc(s_h, 1)
                for k in range(NT + 1):
                    if k < NT:
                        if k >= 2:
                            dve.wait_ge(s_u2, base + k - 1)
                        dve.wait_ge(s_u0, base + k + 1)
                        nc.vector.tensor_tensor(rest[:, k % 2, :], tp[:, k % 4, P:P + D], U[:, k, 0, :],
                                                ALU.subtract).then_inc(s_r, 1)
                    if k >= 1:
                        dve.wait_ge(s_u1, base + k)
                        nc.vector.tensor_tensor(U[:, k - 1, 2, :], rest[:, (k - 1) % 2, :], U[:, k - 1, 1, :],
                                                ALU.subtract).then_inc(s_u2, 1)
                for j in range(NT):
                    dve.wait_ge(s_p2, base + j + 1)
                    do(nc.vector.scalar_tensor_tensor(part[:, j % 2, :], acc[:, j % 4, D:2 * D], 2.0,
                                                      part[:, j % 2, :], ALU.mult, ALU.add))
                    do(nc.vector.scalar_tensor_tensor(part[:, j % 2, :], acc[:, j % 4, 0:D], 2.0,
                                                      part[:, j % 2, :], ALU.mult, ALU.add))
                    nc.vector.tensor_tensor(cv[:, j, :], part[:, j % 2, :], vec[:, i, 0, :], ALU.add).then_inc(s_cv, 1)
                dve.wait_ge(s_sum, i + 1)
                do(nc.vector.scalar_tensor_tensor(mu[:, :], tot[:, 0, 0:D], 1.0 / N, vec[:, i, 3, :], ALU.mult, ALU.mult))
                do(nc.vector.tensor_tensor(cv[:, :, :], cv[:, :, :], mu[:, :].unsqueeze(1).to_broadcast([P, NT, D]), ALU.subtract))
                dve.sem_inc(s_xc, 1)
                dve.wait_ge(s_sqs, (i + 1) * 5)
                do(nc.vector.tensor_scalar(mu[:, :], tot[:, 1, 0:D], 1.0 / N, LN_EPS, ALU.mult, ALU.add))
                root(2 + i)()
                do(nc.vector.reciprocal(sd[:, :], sd[:, :]))
                do(nc.vector.tensor_tensor(sd[:, :], sd[:, :], vec[:, i, 1, :], ALU.mult))
                do(nc.vector.tensor_tensor(cv[:, :, :], cv[:, :, :], sd[:, :].unsqueeze(1).to_broadcast([P, NT, D]), ALU.mult))
                do(nc.vector.tensor_tensor(cv[:, :, :], cv[:, :, :], vec[:, i, 2, :].unsqueeze(1).to_broadcast([P, NT, D]), ALU.add))
                do(nc.vector.scalar_tensor_tensor(h[:, :, :], cv[:, :, :], 0.0, h[:, :, :], ALU.max, ALU.add))
            do(nc.vector.tensor_tensor(x[:, :, :], x[:, :, :], h[:, :, :], ALU.add))

        @block.scalar
        def _(act):
            act.wait_ge(s_var, 1)
            nc.scalar.sqrt(stat[:, 2, :], stat[:, 1, :]).then_inc(s_root, 1)
            for i in range(NL):
                base = i * NT
                for k in range(NT + 2):
                    if k < NT:
                        act.wait_ge(s_tp, base + k + 1)
                        nc.scalar.activation(hT[:, k % 2, :], tp[0:D, k % 4, 0:P], ACT.Copy).then_inc(s_hT, 1)
                    if k >= 2:
                        act.wait_ge(s_r, base + k - 1)
                        nc.scalar.activation(U[:, k - 2, 1, :], rest[:, k % 2, :], ACT.Copy).then_inc(s_u1, 1)
                    if 1 <= k <= NT:
                        act.wait_ge(s_pr, base + k)
                        nc.scalar.activation(U[:, k - 1, 0, :], tp[:, (k - 1) % 4, P:P + D], ACT.Copy).then_inc(s_u0, 1)
                for j in range(NT):
                    act.wait_ge(s_acc, base + j + 1)
                    if base + j >= 2:
                        act.wait_ge(s_cv, base + j - 1)
                    nc.scalar.activation(part[:, j % 2, :], acc[:, j % 4, 2 * D:3 * D], ACT.Copy,
                                         scale=2.0).then_inc(s_p2, 1)
                act.wait_ge(s_xc, i + 1)
                for q in range(5):
                    nc.scalar.activation(sq[:, 5 * q:5 * q + 5, :], cv[:, 5 * q:5 * q + 5, :], ACT.Square).then_inc(s_sq, 1)
                act.wait_ge(s_var, 2 + i)
                nc.scalar.sqrt(sd[:, :], mu[:, :]).then_inc(s_root, 1)

        @block.tensor
        def _(pe):
            pe.wait_ge(s_id, 1)
            pe.wait_ge(s_par, 16 * 5 * NL)
            for i in range(NL):
                base = i * NT
                pe.wait_ge(s_h, i + 1)
                for k in range(NT + 1):
                    if k < NT:
                        if k >= 4:
                            pe.wait_ge(s_r, base + k - 3)
                        pe.transpose(tp[0:D, k % 4, 0:P], h[:, k, :], ident[:, :]).then_inc(s_tp, 1)
                    if k >= 1:
                        pe.wait_ge(s_hT, base + k)
                        pe.matmul(tp[:, (k - 1) % 4, P:P + D], hT[:, (k - 1) % 2, :], W[:, i, :],
                                  start=True, stop=True).then_inc(s_pr, 1)
                for j in range(NT + 2):
                    if j < NT:
                        if base + j >= 4:
                            pe.wait_ge(s_cv, base + j - 3)
                        if i == 0 and j % 5 == 0:
                            pe.wait_ge(s_C[j // 5], 5 * 16)
                        for k in range(NT):
                            if j == 0:
                                pe.wait_ge(s_u2, base + k + 1)
                            mm = pe.matmul(acc[:, j % 4, 0:3 * D], C[:, j, k, :],
                                           U[:, k, :, :].rearrange("p a f -> p (a f)"),
                                           start=(k == 0), stop=(k == NT - 1))
                        mm.then_inc(s_acc, 1)
                    if j >= 2:
                        t = j - 2
                        pe.wait_ge(s_cv, base + t + 1)
                        mm = pe.matmul(tot[:, 0, 0:D], mask[:, int(t == NT - 1), :], cv[:, t, :],
                                       start=(t == 0), stop=(t == NT - 1))
                mm.then_inc(s_sum, 1)
                for q in range(5):
                    pe.wait_ge(s_sq, i * 5 + q + 1)
                    for u in range(5):
                        t = 5 * q + u
                        mm = pe.matmul(tot[:, 1, 0:D], mask[:, int(t == NT - 1), :], sq[:, t, :],
                                       start=(t == 0), stop=(t == NT - 1))
                    mm.then_inc(s_sqs, 1)


def stream_plan(orders, slots):
    holder, last, uses, loads = [None] * slots, [None] * slots, [], []
    for u, j in enumerate(j for order in orders for j in order):
        hit = j in holder
        if not hit:
            s = holder.index(None) if None in holder else min(range(slots), key=lambda q: last[q])
            loads.append((j, s, last[s]))
            holder[s] = j
        s = holder.index(j)
        last[s] = u
        uses.append((j, s, not hit))
    return uses, loads


def weighted_gcn(nc, x, W_d, wdeg, layers, out):
    RW = 12
    orders = (list(range(NT)), list(range(NT))[::-1])
    uses, loads = stream_plan(orders, RW)
    with ExitStack() as ctx:
        m = Scope(nc, ctx, "layer3")
        ring = m.sb("ring", [P, RW, NT, P], F32)
        h = m.sb("h", [P, NT, D], F32)
        V = m.sb("V", [P, NT, D], F32)
        ident = m.sb("ident", [P, P], F32)
        colno = m.sb("colno", [P, P], F32)
        W = m.sb("W", [D, 2, D], F32)
        bias = m.sb("bias", [P, 2, D], F32)
        stat = m.sb("stat", [P, 3, NT], F32)
        dinv = m.sb("dinv", [P, NT], F32)
        pos = m.sb("pos", [P, NT], F32)
        hT = m.sb("hT", [D, 2, P], F32)
        part = m.sb("part", [P, 2, D], F32)
        ex = m.sb("ex", [P, 5, D], F32)
        tp = m.ps("tp", [P, 4, 512])
        acc = m.ps("acc", [P, 4, 512])
        s_par = m.sem("parameters_loaded")
        s_W = [m.sem(f"W_slot{s}_loaded") for s in range(RW)]
        s_c = m.sem("iotas_made")
        s_v = m.sem("dve_chain")
        s_var = m.sem("root_wanted")
        s_root = m.sem("root_made")
        s_h = m.sem("h_made")
        s_tp = m.sem("h_turned")
        s_hT = m.sem("turned_h_out")
        s_pr = m.sem("hV_done")
        s_V = m.sem("scaled_made")
        s_acc = m.sem("aggregates_done")
        s_o = m.sem("conv_tiles_made")
        s_exp = m.sem("exponentials_wanted")
        s_e = m.sem("exponentials_made")
        s_st = m.sem("out_stored")
        s_fin = m.sem("out_made")
        block = ctx.enter_context(nc.Block())
        NL = len(layers)
        GROUPS = NT // 5

        def group(g):
            return slice(NT - 5 * (g + 1), NT - 5 * g)

        @block.sync
        def _(sp):
            for i, (w, b) in enumerate(layers):
                sp.dma_start(W[:, i, :], w).then_inc(s_par, 16)
                sp.dma_start(bias[:, i, :], b.rearrange("(o f) -> o f", o=1).to_broadcast([P, D])).then_inc(s_par, 16)
            for j, s, freed in loads:
                if freed is not None:
                    sp.wait_ge(s_acc, freed + 1)
                sp.dma_start(ring[:, s, :, :].rearrange("p k d -> p (k d)"), W_d[j, :, :]).then_inc(s_W[s], 16)
            for g in range(GROUPS):
                sp.wait_ge(s_fin, g + 1)
                sp.dma_start(out.rearrange("(k p) f -> p k f", p=P)[:, group(g), :],
                             x[:, group(g), :]).then_inc(s_st, 16)
            sp.wait_ge(s_st, 16 * GROUPS)

        @block.gpsimd
        def _(pool):
            nc.gpsimd.iota(colno[:, :], pattern=[[1, P]], base=0, channel_multiplier=0,
                           allow_small_or_imprecise_dtypes=True).then_inc(s_c, 1)
            nc.gpsimd.iota(ident[:, :], pattern=[[0, P]], base=0, channel_multiplier=1,
                           allow_small_or_imprecise_dtypes=True).then_inc(s_c, 1)

        @block.vector
        def _(dve):
            do = Chain(dve, s_v)

            def root(n):
                def wait():
                    dve.sem_inc(s_var, 1)
                    dve.wait_ge(s_root, n)
                return wait

            def log_softmax(g):
                t = group(g)
                top, tot = stat[:, 0, t], stat[:, 1, t]
                do(nc.vector.tensor_reduce(top, h[:, t, :], AX.X, ALU.max))
                do(nc.vector.tensor_tensor(h[:, t, :], h[:, t, :], top.unsqueeze(2).to_broadcast([P, 5, D]), ALU.subtract))
                dve.sem_inc(s_exp, 1)
                do(nc.vector.tensor_tensor(x[:, t, :], x[:, t, :], h[:, t, :], ALU.add))
                dve.wait_ge(s_e, 2 * g + 1)
                do(nc.vector.tensor_reduce(tot, ex[:, :, :], AX.X, ALU.add))
                dve.sem_inc(s_exp, 1)
                dve.wait_ge(s_e, 2 * g + 2)
                nc.vector.tensor_tensor(x[:, t, :], x[:, t, :], stat[:, 2, t].unsqueeze(2).to_broadcast([P, 5, D]),
                                        ALU.subtract).then_inc(s_fin, 1)

            dve.wait_ge(s_c, 2)
            do(nc.vector.tensor_tensor(ident[:, :], ident[:, :], colno[:, :], ALU.is_equal))
            do(nc.vector.tensor_scalar(dinv[:, :], wdeg[:, :], 1.0, None, ALU.add))
            do(nc.vector.tensor_scalar(pos[:, :], dinv[:, :], 0.0, None, ALU.is_gt))
            do(nc.vector.tensor_scalar(dinv[:, :], dinv[:, :], 1e-30, None, ALU.max))
            root(1)()
            do(nc.vector.reciprocal(dinv[:, :], dinv[:, :]))
            do(nc.vector.tensor_tensor(dinv[:, :], dinv[:, :], pos[:, :], ALU.mult))
            layernorm_relu(nc, do, root(2), x[:, :, :], h[:, :, :], stat, V[:, :, :])
            dve.wait_ge(s_par, 16 * 2 * NL)
            for i in range(NL):
                base = i * NT
                dve.sem_inc(s_h, 1)
                for k in range(NT):
                    dve.wait_ge(s_pr, base + k + 1)
                    nc.vector.tensor_scalar(V[:, k, :], tp[:, k % 4, P:P + D], dinv[:, k:k + 1], None,
                                            ALU.mult).then_inc(s_V, 1)
                for n, j in enumerate(orders[i]):
                    dve.wait_ge(s_acc, base + n + 1)
                    if n == 0:
                        dve.wait_ge(s_V, base + NT)
                    do(nc.vector.tensor_tensor(part[:, n % 2, :], acc[:, n % 4, 0:D], V[:, j, :], ALU.add))
                    nc.vector.scalar_tensor_tensor(h[:, j, :], part[:, n % 2, :], dinv[:, j:j + 1], bias[:, i, :],
                                                   ALU.mult, ALU.add).then_inc(s_o, 1)
                    if i == 1 and n % 5 == 4:
                        dve.wait_ge(s_o, base + n + 1)
                        log_softmax(n // 5)
                if i == 0:
                    dve.wait_ge(s_o, NT)
                    do(nc.vector.tensor_scalar(h[:, :, :], h[:, :, :], 0.0, None, ALU.max))

        @block.scalar
        def _(act):
            act.wait_ge(s_var, 1)
            nc.scalar.sqrt(dinv[:, :], dinv[:, :]).then_inc(s_root, 1)
            act.wait_ge(s_var, 2)
            nc.scalar.sqrt(stat[:, 2, :], stat[:, 1, :]).then_inc(s_root, 1)
            for i in range(NL):
                for k in range(NT):
                    act.wait_ge(s_tp, i * NT + k + 1)
                    nc.scalar.activation(hT[:, k % 2, :], tp[0:D, k % 4, 0:P], ACT.Copy).then_inc(s_hT, 1)
            for g in range(GROUPS):
                act.wait_ge(s_exp, 2 * g + 1)
                nc.scalar.activation(ex[:, :, :], h[:, group(g), :], ACT.Exp).then_inc(s_e, 1)
                act.wait_ge(s_exp, 2 * g + 2)
                nc.scalar.activation(stat[:, 2, group(g)], stat[:, 1, group(g)], ACT.Ln).then_inc(s_e, 1)

        @block.tensor
        def _(pe):
            pe.wait_ge(s_par, 16 * 2 * NL)
            seen = {}
            for i in range(NL):
                base = i * NT
                pe.wait_ge(s_h, i + 1)
                for k in range(NT + 1):
                    if k < NT:
                        if k >= 4:
                            pe.wait_ge(s_V, base + k - 3)
                        pe.transpose(tp[0:D, k % 4, 0:P], h[:, k, :], ident[:, :]).then_inc(s_tp, 1)
                    if k >= 1:
                        pe.wait_ge(s_hT, base + k)
                        pe.matmul(tp[:, (k - 1) % 4, P:P + D], hT[:, (k - 1) % 2, :], W[:, i, :],
                                  start=True, stop=True).then_inc(s_pr, 1)
                for n in range(NT):
                    j, s, load = uses[base + n]
                    if base + n >= 4:
                        pe.wait_ge(s_o, base + n - 3)
                    if load:
                        seen[s] = seen.get(s, 0) + 16
                        pe.wait_ge(s_W[s], seen[s])
                    for k in range(NT):
                        if n == 0:
                            pe.wait_ge(s_V, base + k + 1)
                        mm = pe.matmul(acc[:, n % 4, 0:D], ring[:, s, k, :], V[:, k, :],
                                       start=(k == 0), stop=(k == NT - 1))
                    mm.then_inc(s_acc, 1)


def gnn(nc, x, src_cols, dst_cols, dst_rows, attr, w_cols, We, be, Wn, bn, W1, b1, W2, b2,
        g1w, g1b, g1a, g2w, g2b, g2a, V1, c1, V2, c2, out):
    tab_d = nc.dram_tensor("range_table", [QG * P, 2], I16, kind="Internal").ap()
    C_d = nc.dram_tensor("C_blocks", [NT, P, NP], F16, kind="Internal").ap()
    W_d = nc.dram_tensor("W_blocks", [NT, P, NP], F32, kind="Internal").ap()
    row_d = nc.dram_tensor("target_rows", [1, ET * P], I16, kind="Internal").ap()
    P_d = nc.dram_tensor("source_terms", [NP, 2 * D], F32, kind="Internal").ap()
    x1_d = nc.dram_tensor("x_after_layer0", [NP, D], F32, kind="Internal").ap()
    with ExitStack() as outer:
        o = Scope(nc, outer, "graph")
        indeg = o.sb("indeg", [P, NT * len(TG)], F32)
        CT = o.sb("CT", [P, NT, NP], F16)
        with ExitStack() as ctx:
            m = Scope(nc, ctx, "edges")
            key = m.sb("key", [P, ETB], F32)
            smod = m.sb("smod", [P, ETB], F16)
            wpart = m.sb("wpart", [P, 3, ETB], BF16)
            edge_ranges(nc, src_cols, dst_cols, dst_rows, w_cols, tab_d, row_d, key, smod, wpart)
            build_matrices(nc, tab_d, key, smod, wpart, CT, indeg, C_d, W_d)
        propagate(nc, x, CT, indeg, x1_d)
    with ExitStack() as outer:
        o = Scope(nc, outer, "nodes")
        wdeg = o.sb("wdeg", [P, NT], F32)
        xs = o.sb("x", [P, NT, D], F32)
        gated_edges(nc, x1_d, src_cols, dst_cols, w_cols, attr, We, be, Wn, bn, tab_d, row_d, P_d, xs, wdeg)
        residual_gcn(nc, xs, C_d, ((W1, b1, g1w, g1b, g1a), (W2, b2, g2w, g2b, g2a)))
        weighted_gcn(nc, xs, W_d, wdeg, ((V1, c1), (V2, c2)), out)


def kernel(x, src, dst, edge_attr_64, edge_weight, L1_gnn_W_e, L1_gnn_b_e, L1_gnn_W_n, L1_gnn_b_n,
           L2_gnn_W1, L2_gnn_b1, L2_gnn_W2, L2_gnn_b2, L2_gnn_gn1_w, L2_gnn_gn1_b, L2_gnn_gn1_a,
           L2_gnn_gn2_w, L2_gnn_gn2_b, L2_gnn_gn2_a, L3_gnn_W1, L3_gnn_b1, L3_gnn_W2, L3_gnn_b2):
    import numpy as np
    import concourse.bacc as bacc
    from concourse.bass_utils import run_bass_kernel_spmd

    def padded(a, n, value=0):
        a = np.asarray(a)
        out = np.full((n,) + a.shape[1:], value, a.dtype)
        out[:len(a)] = a
        return out

    def columns(a):
        return np.ascontiguousarray(a.reshape(ET, P)[:ETC].T)

    dst_p = padded(dst, ET * P, NO_NODE)
    arrays = {
        "x": padded(x, NP),
        "src_cols": columns(padded(src, ET * P)),
        "dst_cols": columns(dst_p),
        "dst_rows": dst_p.reshape(ET, P),
        "attr": np.ascontiguousarray(padded(edge_attr_64, ET * P).T),
        "w_cols": columns(padded(edge_weight, ET * P)),
        "We": L1_gnn_W_e, "be": L1_gnn_b_e, "Wn": L1_gnn_W_n, "bn": L1_gnn_b_n,
        "W1": L2_gnn_W1, "b1": L2_gnn_b1, "W2": L2_gnn_W2, "b2": L2_gnn_b2,
        "g1w": L2_gnn_gn1_w, "g1b": L2_gnn_gn1_b, "g1a": L2_gnn_gn1_a,
        "g2w": L2_gnn_gn2_w, "g2b": L2_gnn_gn2_b, "g2a": L2_gnn_gn2_a,
        "V1": L3_gnn_W1, "c1": L3_gnn_b1, "V2": L3_gnn_W2, "c2": L3_gnn_b2,
    }
    nc = bacc.Bacc("TRN2", target_bir_lowering=False, num_devices=1)
    args = {}
    for name, a in arrays.items():
        a = arrays[name] = np.ascontiguousarray(a)
        args[name] = nc.dram_tensor(f"in_{name}", a.shape, mybir.dt.from_np(a.dtype), kind="ExternalInput").ap()
    out = nc.dram_tensor("out", (NP, D), F32, kind="ExternalOutput").ap()
    gnn(nc, out=out, **args)
    r = run_bass_kernel_spmd(nc, [{f"in_{name}": a for name, a in arrays.items()}], core_ids=[0])
    return r.results[0]["out"][:N]
```
